# Optimizing a Trainium2 kernel written in Bass

```python
import numpy as np
import jax
import jax.numpy as jnp

def _softmax(x, axis=-1):
    return jax.nn.softmax(x, axis=axis)

def _gelu(x):
    return jax.nn.gelu(x, approximate=True)

def _silu(x):
    return jax.nn.silu(x)

def _sigmoid(x):
    return jax.nn.sigmoid(x)

def _layernorm(x, axis=-1, eps=1e-05):
    m = jnp.mean(x, axis=axis, keepdims=True)
    v = jnp.var(x, axis=axis, keepdims=True)
    return (x - m) / jnp.sqrt(v + eps)

def _scatter_add(tgt, idx, src, axis=0):
    return tgt.at[idx].add(src)

def _segment_sum(src, seg, n):
    return jax.ops.segment_sum(src, seg, n)
kernel_name = 'mk_gnn_preln_d4_gnn_r8_f81a47'

def setup_inputs(seed: int=0):
    np.random.seed(seed)
    _w = jnp.asarray

    def _rec_inputs():
        import jax
        import jax.numpy as jnp
        _gk = jax.random.key(seed)
        x = -0.000202 + 1 * jax.random.normal(jax.random.fold_in(_gk, 1), (12500, 64), jnp.float32)
        src = jax.random.randint(jax.random.fold_in(_gk, 2), (400000,), 0, 12500, jnp.int32)
        dst = jax.random.randint(jax.random.fold_in(_gk, 3), (400000,), 0, 12500, jnp.int32)
        _o = jnp.argsort(dst, stable=True)
        src = src[_o]
        dst = dst[_o]
        edge_attr_10 = 0.000262864 + 0.999894 * jax.random.normal(jax.random.fold_in(_gk, 12), (400000, 10), jnp.float32)
        edge_attr_64 = -8.16379e-05 + 0.999858 * jax.random.normal(jax.random.fold_in(_gk, 13), (400000, 64), jnp.float32)
        return (x, src, dst, edge_attr_10, edge_attr_64)
    x, src, dst, edge_attr_10, edge_attr_64 = _rec_inputs()

    def _L0_gnn_setup():
        import jax, jax.numpy as jnp
        import numpy as np
        N_NODES = 12500
        N_EDGES = 156250
        IN_DIM = 64
        HID_DIM = 64
        EDGE_DIM = 10
        BN_EPS = 1e-05
        key = jax.random.key(seed)
        ks = jax.random.split(key, 10)
        x = jax.random.normal(ks[0], (N_NODES, IN_DIM), dtype=jnp.float32)
        edge_index = jax.random.randint(ks[1], (2, N_EDGES), 0, N_NODES, dtype=jnp.int64)
        edge_attr = jax.random.normal(ks[2], (N_EDGES, EDGE_DIM), dtype=jnp.float32)
        W_edge = jax.random.normal(ks[3], (EDGE_DIM, IN_DIM), dtype=jnp.float32) * (1.0 / np.sqrt(EDGE_DIM))
        b_edge = jnp.zeros((IN_DIM,), dtype=jnp.float32)
        W1 = jax.random.normal(ks[4], (IN_DIM, HID_DIM), dtype=jnp.float32) * (1.0 / np.sqrt(IN_DIM))
        b1 = jnp.zeros((HID_DIM,), dtype=jnp.float32)
        W2 = jax.random.normal(ks[5], (HID_DIM, HID_DIM), dtype=jnp.float32) * (1.0 / np.sqrt(HID_DIM))
        b2 = jnp.zeros((HID_DIM,), dtype=jnp.float32)
        bn_gamma = jnp.ones((HID_DIM,), dtype=jnp.float32)
        bn_beta = jnp.zeros((HID_DIM,), dtype=jnp.float32)
        return {'x': x, 'edge_index': edge_index, 'edge_attr': edge_attr, 'W_edge': W_edge, 'b_edge': b_edge, 'W1': W1, 'b1': b1, 'W2': W2, 'b2': b2, 'bn_gamma': bn_gamma, 'bn_beta': bn_beta}
    _L0_gnn_all = _L0_gnn_setup()
    _L0_gnn_in = {k: v for k, v in _L0_gnn_all.items() if k in ('W_edge', 'b_edge', 'W1', 'b1', 'W2', 'b2', 'bn_gamma', 'bn_beta')}
    del _L0_gnn_all

    def _L1_gnn_setup():
        import jax, jax.numpy as jnp
        import numpy as np
        N_NODES = 12500
        N_EDGES = 200000
        IN_CH = 64
        OUT_CH = 64
        key = jax.random.key(seed)
        ks = jax.random.split(key, 6)
        x = jax.random.normal(ks[0], (N_NODES, IN_CH), dtype=jnp.float32)
        edge_index = jax.random.randint(ks[1], (2, N_EDGES), 0, N_NODES, dtype=jnp.int64)
        W1 = jax.random.normal(ks[2], (2 * IN_CH, OUT_CH), dtype=jnp.float32) * (1.0 / np.sqrt(2 * IN_CH))
        b1 = jnp.zeros((OUT_CH,), dtype=jnp.float32)
        W2 = jax.random.normal(ks[3], (OUT_CH, OUT_CH), dtype=jnp.float32) * (1.0 / np.sqrt(OUT_CH))
        b2 = jnp.zeros((OUT_CH,), dtype=jnp.float32)
        return {'x': x, 'edge_index': edge_index, 'W1': W1, 'b1': b1, 'W2': W2, 'b2': b2}
    _L1_gnn_all = _L1_gnn_setup()
    _L1_gnn_in = {k: v for k, v in _L1_gnn_all.items() if k in ('W1', 'b1', 'W2', 'b2')}
    del _L1_gnn_all

    def _L2_gnn_setup():
        import jax, jax.numpy as jnp
        import numpy as np
        N_NODES = 6250
        N_EDGES = 100000
        D_IN = 64
        D_OUT = 64
        key = jax.random.key(seed)
        k1, k2, k3, k4 = jax.random.split(key, 4)
        feat = jax.random.normal(k1, (N_NODES, D_IN), dtype=jnp.float32)
        W = jax.random.normal(k2, (D_OUT, D_IN), dtype=jnp.float32) * (1.0 / np.sqrt(D_IN))
        b = jnp.zeros((D_OUT,), dtype=jnp.float32)
        src = jax.random.randint(k3, (N_EDGES,), 0, N_NODES, dtype=jnp.int64)
        dst = jax.random.randint(k4, (N_EDGES,), 0, N_NODES, dtype=jnp.int64)
        return {'feat': feat, 'W': W, 'b': b, 'src': src, 'dst': dst}
    _L2_gnn_all = _L2_gnn_setup()
    _L2_gnn_in = {k: v for k, v in _L2_gnn_all.items() if k in ('W', 'b')}
    del _L2_gnn_all

    def _L3_gnn_setup():
        import jax, jax.numpy as jnp
        import numpy as np
        N = 12500
        E = 200000
        D = 64
        H = 128
        OUT = 64
        EPS = 1e-07
        BN_EPS = 1e-05
        NORM_EPS = 1e-12
        key = jax.random.key(seed)
        ks = jax.random.split(key, 10)
        feats = jax.random.normal(ks[0], (N, D), dtype=jnp.float32)
        edge_h = jax.random.normal(ks[1], (E, D), dtype=jnp.float32)
        src = jax.random.randint(ks[2], (E,), 0, N, dtype=jnp.int32)
        dst = jax.random.randint(ks[3], (E,), 0, N, dtype=jnp.int32)
        W1 = jax.random.normal(ks[4], (D, H), dtype=jnp.float32) * 0.05
        b1 = jnp.zeros((H,), dtype=jnp.float32)
        gamma = jnp.ones((H,), dtype=jnp.float32)
        bn_beta = jnp.zeros((H,), dtype=jnp.float32)
        W2 = jax.random.normal(ks[5], (H, OUT), dtype=jnp.float32) * 0.05
        b2 = jnp.zeros((OUT,), dtype=jnp.float32)
        scale = jnp.ones((1,), dtype=jnp.float32)
        return {'feats': feats, 'edge_h': edge_h, 'src': src, 'dst': dst, 'W1': W1, 'b1': b1, 'gamma': gamma, 'bn_beta': bn_beta, 'W2': W2, 'b2': b2, 'scale': scale}
    _L3_gnn_all = _L3_gnn_setup()
    _L3_gnn_in = {k: v for k, v in _L3_gnn_all.items() if k in ('W1', 'b1', 'gamma', 'bn_beta', 'W2', 'b2', 'scale')}
    del _L3_gnn_all
    return {'x': x, 'src': src, 'dst': dst, 'edge_attr_10': edge_attr_10, 'edge_attr_64': edge_attr_64, 'L0_gnn_W_edge': _L0_gnn_in['W_edge'], 'L0_gnn_b_edge': _L0_gnn_in['b_edge'], 'L0_gnn_W1': _L0_gnn_in['W1'], 'L0_gnn_b1': _L0_gnn_in['b1'], 'L0_gnn_W2': _L0_gnn_in['W2'], 'L0_gnn_b2': _L0_gnn_in['b2'], 'L0_gnn_bn_gamma': _L0_gnn_in['bn_gamma'], 'L0_gnn_bn_beta': _L0_gnn_in['bn_beta'], 'L1_gnn_W1': _L1_gnn_in['W1'], 'L1_gnn_b1': _L1_gnn_in['b1'], 'L1_gnn_W2': _L1_gnn_in['W2'], 'L1_gnn_b2': _L1_gnn_in['b2'], 'L2_gnn_W': _L2_gnn_in['W'], 'L2_gnn_b': _L2_gnn_in['b'], 'L3_gnn_W1': _L3_gnn_in['W1'], 'L3_gnn_b1': _L3_gnn_in['b1'], 'L3_gnn_gamma': _L3_gnn_in['gamma'], 'L3_gnn_bn_beta': _L3_gnn_in['bn_beta'], 'L3_gnn_W2': _L3_gnn_in['W2'], 'L3_gnn_b2': _L3_gnn_in['b2'], 'L3_gnn_scale': _L3_gnn_in['scale']}

def reference(x, src, dst, edge_attr_10, edge_attr_64, L0_gnn_W_edge, L0_gnn_b_edge, L0_gnn_W1, L0_gnn_b1, L0_gnn_W2, L0_gnn_b2, L0_gnn_bn_gamma, L0_gnn_bn_beta, L1_gnn_W1, L1_gnn_b1, L1_gnn_W2, L1_gnn_b2, L2_gnn_W, L2_gnn_b, L3_gnn_W1, L3_gnn_b1, L3_gnn_gamma, L3_gnn_bn_beta, L3_gnn_W2, L3_gnn_b2, L3_gnn_scale):
    import jax
    import jax.numpy as jnp

    def _L0_gnn_ref(x, edge_index, edge_attr, W_edge, b_edge, W1, b1, W2, b2, bn_gamma, bn_beta):
        import jax, jax.numpy as jnp
        import numpy as np
        N_NODES = 12500
        N_EDGES = 156250
        IN_DIM = 64
        HID_DIM = 64
        EDGE_DIM = 10
        BN_EPS = 1e-05
        src, dst = (edge_index[0], edge_index[1])
        msg = jax.nn.relu(x[src] + edge_attr @ W_edge + b_edge)
        aggr = jax.ops.segment_sum(msg, dst, num_segments=N_NODES)
        h = x + aggr
        h = jax.nn.relu(h @ W1 + b1) @ W2 + b2
        h = jax.nn.relu(h)
        mean = jnp.mean(h, axis=0)
        var = jnp.var(h, axis=0)
        out = (h - mean) * jax.lax.rsqrt(var + BN_EPS) * bn_gamma + bn_beta
        return out

    def _L1_gnn_ref(x, edge_index, W1, b1, W2, b2):
        import jax, jax.numpy as jnp
        import numpy as np
        N_NODES = 12500
        N_EDGES = 200000
        IN_CH = 64
        OUT_CH = 64
        src = edge_index[0]
        dst = edge_index[1]
        x_i = x[dst]
        x_j = x[src]
        edge_features = jnp.concatenate([x_i, x_j - x_i], axis=-1)
        h = jax.nn.relu(edge_features @ W1 + b1)
        edge_messages = h @ W2 + b2
        out = jax.ops.segment_max(edge_messages, dst, num_segments=x.shape[0])
        return jnp.where(jnp.isfinite(out), out, jnp.zeros_like(out))

    def _L2_gnn_ref(feat, W, b, src, dst):
        import jax, jax.numpy as jnp
        import numpy as np
        N_NODES = 6250
        N_EDGES = 100000
        D_IN = 64
        D_OUT = 64
        N = feat.shape[0]
        ones = jnp.ones(src.shape[0], dtype=feat.dtype)
        out_deg = jnp.clip(jax.ops.segment_sum(ones, src, num_segments=N), 1.0)
        in_deg = jnp.clip(jax.ops.segment_sum(ones, dst, num_segments=N), 1.0)
        h = feat @ W.T + b
        h = h * (out_deg ** (-0.5))[:, None]
        rst = jax.ops.segment_sum(h[src], dst, num_segments=N)
        rst = rst * (in_deg ** (-0.5))[:, None]
        return rst

    def _L3_gnn_ref(feats, edge_h, W1, b1, gamma, bn_beta, W2, b2, scale, src, dst):
        import jax, jax.numpy as jnp
        import numpy as np
        N = 12500
        E = 200000
        D = 64
        H = 128
        OUT = 64
        EPS = 1e-07
        BN_EPS = 1e-05
        NORM_EPS = 1e-12
        beta = 1.0
        m = jax.nn.relu(feats[src] + edge_h) + EPS
        logits = m * beta
        gmax = jax.ops.segment_max(logits, dst, num_segments=N)
        ex = jnp.exp(logits - gmax[dst])
        den = jax.ops.segment_sum(ex, dst, num_segments=N)
        a = ex / den[dst]
        h = jax.ops.segment_sum(m * a, dst, num_segments=N)
        feat_norm = jnp.linalg.norm(feats, axis=-1, keepdims=True)
        msg_norm = jnp.linalg.norm(h, axis=-1, keepdims=True)
        msg = h / jnp.maximum(msg_norm, NORM_EPS)
        x = feats + msg * feat_norm * scale
        x = x @ W1 + b1
        mean = jnp.mean(x, axis=0)
        var = jnp.mean(jnp.square(x - mean), axis=0)
        x = (x - mean) * jax.lax.rsqrt(var + BN_EPS) * gamma + bn_beta
        x = jax.nn.relu(x)
        return x @ W2 + b2
    edge_index = jnp.stack([src, dst])
    h = jnp.maximum(_layernorm(x, axis=-1), 0.0)
    x = x + _L0_gnn_ref(h, edge_index, edge_attr_10, L0_gnn_W_edge, L0_gnn_b_edge, L0_gnn_W1, L0_gnn_b1, L0_gnn_W2, L0_gnn_b2, L0_gnn_bn_gamma, L0_gnn_bn_beta)
    h = jnp.maximum(_layernorm(x, axis=-1), 0.0)
    x = x + _L1_gnn_ref(h, edge_index, L1_gnn_W1, L1_gnn_b1, L1_gnn_W2, L1_gnn_b2)
    h = jnp.maximum(_layernorm(x, axis=-1), 0.0)
    x = x + _L2_gnn_ref(h, L2_gnn_W, L2_gnn_b, src, dst)
    h = jnp.maximum(_layernorm(x, axis=-1), 0.0)
    x = x + _L3_gnn_ref(h, edge_attr_64, L3_gnn_W1, L3_gnn_b1, L3_gnn_gamma, L3_gnn_bn_beta, L3_gnn_W2, L3_gnn_b2, L3_gnn_scale, src, dst)
    return x

_drawn_inputs = setup_inputs


def setup_inputs(seed=0):
    import zlib

    import numpy as np

    out = dict(_drawn_inputs(seed))
    spreads = {'L0_gnn_b_edge': (0.0, 0.1),
     'L0_gnn_b1': (0.0, 0.8),
     'L0_gnn_b2': (0.0, 0.45),
     'L0_gnn_bn_gamma': (1.0, 0.2),
     'L0_gnn_bn_beta': (0.0, 0.1),
     'L1_gnn_b1': (0.0, 0.1),
     'L1_gnn_b2': (0.0, 0.1),
     'L2_gnn_b': (0.0, 0.1),
     'L3_gnn_b1': (0.0, 0.8),
     'L3_gnn_gamma': (1.0, 0.2),
     'L3_gnn_bn_beta': (0.0, 0.327),
     'L3_gnn_b2': (0.0, 0.1)}
    factors = {}
    for name, (base, spread) in spreads.items():
        noise = np.random.default_rng([zlib.crc32(name.encode()), seed]).standard_normal(out[name].shape)
        drawn = base * np.exp(spread * noise) if base else spread * noise
        out[name] = jnp.asarray(drawn.astype(out[name].dtype))
    for name, factor in factors.items():
        out[name] = (out[name] * factor).astype(out[name].dtype)
    return out
```

```python
from contextlib import ExitStack

import concourse.bass as bass
from concourse import mybir

ALU = mybir.AluOpType
ACT = mybir.ActivationFunctionType
F32 = mybir.dt.float32
BF16 = mybir.dt.bfloat16
I32 = mybir.dt.int32
AX = mybir.AxisListType.X

F = 64
P = 128
NP = 125
CH = 10
NPR = CH // 2
T = 8
BK = P * T
Q = T // 4
D10 = 10
BIG = 1e30
LN_EPS = 1e-5
BN_EPS = 1e-5
SM_EPS = 1e-7
NORM_EPS = 1e-12
IND = bass.IndirectOffsetOnAxis


def wait_reuse(eng, sem, value):
    if not (isinstance(value, int) and value == 0):
        eng.wait_ge(sem, value)


def steps(*names):
    return {n: i + 1 for i, n in enumerate(names)}


def at(seq, name, rnd):
    return rnd * len(seq) + seq[name]


def gnn_kernel(nc, x, src, dst, ea10, ea64, w, out):
    N = x.shape[0]
    E = src.shape[0]
    NT = N // NP
    NC = NT // CH
    NB = -(-E // (2 * BK))
    NB += NB % 2
    NIT = NB // 2
    H = NB * BK
    BASE = E - H
    OVER = 2 * H - E
    HB = -(-N // P)
    assert N % (NP * CH) == 0 and E % P == 0 and HB <= P and 0 < BASE < E and OVER > 0 and OVER % P == 0
    OT = OVER // P

    def dram(name, shape, dt):
        return nc.dram_tensor(name, shape, dt, kind="Internal").ap()

    same_d = dram("same_d", (E,), BF16)
    reset_d = dram("reset_d", (E,), BF16)
    table0 = dram("table0", (N, F), F32)
    table1 = dram("table1", (N, F), F32)
    table2 = dram("table2", (N, F), F32)
    table3 = dram("table3", (N, F), F32)
    own_d = dram("own_d", (N, F), F32)
    own_at_start = dram("own_at_start", (2 * H, F), F32)
    stream = dram("stream", (2 * H, F), F32)
    stream3 = dram("stream3", (2 * H, 2 * F), F32)
    maxes = dram("maxes", (P, H), F32)
    count_d = dram("count_d", (2, HB * P), F32)

    def node_view(t):
        return t.rearrange("(p t) f -> p t f", p=NP)

    def edges_of(half, b):
        return b * BK + (BASE if half else 0)

    root = ExitStack()
    with root:
        class Stage(ExitStack):

            def __init__(self):
                super().__init__()
                self.sems = []

            def sem(self, name):
                self.sems.append(self.enter_context(nc.semaphore(name)))
                return self.sems[-1]

            def pair(self, name):
                return [self.sem(f"{name}{i}") for i in range(2)]

            def clear(self):
                with nc.Block() as block:
                    @block.gpsimd
                    def _(pool):
                        for s in self.sems:
                            pool.sem_clear(s)

        def sb(name, shape, dt=F32, ctx=root):
            return ctx.enter_context(nc.sbuf_tensor(name, shape, dt))

        def ps(name, shape, ctx):
            return ctx.enter_context(nc.psum_tensor(name, shape, F32))

        def dma_pair(name):
            return [root.enter_context(nc.semaphore(f"{name}{i}")) for i in range(2)]

        X = sb("X", [NP, NT, F])
        HN = sb("HN", [NP, NT, F])
        ident = sb("ident", [P, P])
        halves = sb("halves", [P, P])
        before = sb("before", [P, P])
        iota = sb("iota", [P, P])
        row_at = sb("row_at", [NP, NT + CH], I32)
        first_at = sb("first_at", [NP, NT + CH], I32)
        has = sb("has", [NP, NT])
        cut = sb("cut", [NP, NT])
        cut_last = sb("cut_last", [1, 1], I32)
        in_scale = sb("in_scale", [NP, NT])
        out_scale = sb("out_scale", [NP, NT])
        eps = sb("eps", [P, 1])

        with Stage() as ctx:
            W = E // P
            d_cur = sb("d_cur", [P, W + 1], I32, ctx)
            m_same = sb("m_same", [P, W], BF16, ctx)
            m_reset = sb("m_reset", [P, W], BF16, ctx)
            mean = sb("mean", [NP, NT], F32, ctx)
            var = sb("var", [NP, NT], F32, ctx)
            rstd = sb("rstd", [NP, NT], F32, ctx)
            sq = sb("sq", [NP, NT, F], F32, ctx)
            s_x, s_dst, s_first, s_dve, s_std, s_out, s_const = (
                ctx.sem(n) for n in ("setup_x", "setup_dst", "setup_first", "setup_dve", "setup_std", "setup_out", "setup_const"))
            SD = steps("eps", "same", "reset", "mean", "mean_s", "centred", "square", "var", "var_s", "rstd", "h")
            with nc.Block() as block:
                @block.sync
                def _(sp):
                    sp.dma_start(X[:], node_view(x)).then_inc(s_x, 16)
                    dv = dst.rearrange("(p i) -> p i", p=P)
                    sp.dma_start(d_cur[:, 1:W + 1], dv).then_inc(s_dst, 16)
                    sp.dma_start(d_cur[1:P, 0:1], dv[0:P - 1, W - 1:W], allow_slow_non_contiguous=True).then_inc(s_dst, 16)
                    sp.wait_ge(s_dve, SD["same"])
                    sp.dma_start(same_d.rearrange("(p i) -> p i", p=P), m_same[:]).then_inc(s_out, 16)
                    sp.wait_ge(s_dve, SD["reset"])
                    sp.dma_start(reset_d.rearrange("(p i) -> p i", p=P), m_reset[:]).then_inc(s_out, 16)
                    sp.wait_ge(s_dve, SD["h"])
                    sp.dma_start(node_view(table0), HN[:]).then_inc(s_out, 16)
                    sp.wait_ge(s_out, 48)

                @block.gpsimd
                def _(pool):
                    nc.gpsimd.memset(d_cur[0:1, 0:1], -1).then_inc(s_first, 1)
                    nc.gpsimd.memset(ident[:], 0.0).then_inc(s_const, 1)
                    nc.gpsimd.memset(halves[:], 0.0).then_inc(s_const, 1)
                    nc.gpsimd.memset(before[:], 1.0).then_inc(s_const, 1)
                    nc.gpsimd.iota(iota[:], pattern=[[1, P]], base=0, channel_multiplier=0,
                                   allow_small_or_imprecise_dtypes=True).then_inc(s_const, 1)
                    pool.wait_ge(s_const, 4)
                    nc.gpsimd.affine_select(out=ident[:], in_=ident[:], compare_op=ALU.not_equal, fill=1.0, base=0,
                                            pattern=[[-1, P]], channel_multiplier=1).then_inc(s_const, 1)
                    nc.gpsimd.affine_select(out=before[:], in_=before[:], compare_op=ALU.is_gt, fill=0.0, base=0,
                                            pattern=[[1, P]], channel_multiplier=-1).then_inc(s_const, 1)
                    for n, off in enumerate((0, F, -F)):
                        nc.gpsimd.affine_select(out=halves[:], in_=halves[:], compare_op=ALU.not_equal, fill=1.0,
                                                base=off, pattern=[[-1, P]], channel_multiplier=1).then_inc(s_const, 1)
                        pool.wait_ge(s_const, 7 + n)

                @block.vector
                def _(dve):
                    nc.vector.memset(eps[:], LN_EPS).then_inc(s_dve, 1)
                    dve.wait_ge(s_dst, 32)
                    dve.wait_ge(s_first, 1)
                    nc.vector.tensor_tensor(m_same[:], d_cur[:, 1:W + 1], d_cur[:, 0:W], ALU.is_equal).then_inc(s_dve, 1)
                    dve.wait_ge(s_dve, SD["same"])
                    nc.vector.tensor_scalar(m_reset[:], m_same[:], -1.0, BIG, ALU.add, ALU.mult).then_inc(s_dve, 1)
                    dve.wait_ge(s_x, 16)
                    nc.vector.tensor_reduce(mean[:], X[:], AX, ALU.add).then_inc(s_dve, 1)
                    dve.wait_ge(s_dve, SD["mean"])
                    nc.vector.tensor_scalar(mean[:], mean[:], 1.0 / F, None, ALU.mult).then_inc(s_dve, 1)
                    dve.wait_ge(s_dve, SD["mean_s"])
                    nc.vector.tensor_tensor(HN[:], X[:], mean[:].unsqueeze(2).to_broadcast([NP, NT, F]),
                                            ALU.subtract).then_inc(s_dve, 1)
                    dve.wait_ge(s_dve, SD["centred"])
                    nc.vector.tensor_tensor(sq[:], HN[:], HN[:], ALU.mult).then_inc(s_dve, 1)
                    dve.wait_ge(s_dve, SD["square"])
                    nc.vector.tensor_reduce(var[:], sq[:], AX, ALU.add).then_inc(s_dve, 1)
                    dve.wait_ge(s_dve, SD["var"])
                    nc.vector.tensor_scalar(var[:], var[:], 1.0 / F, None, ALU.mult).then_inc(s_dve, 1)
                    dve.wait_ge(s_std, 1)
                    nc.vector.reciprocal(rstd[:], rstd[:]).then_inc(s_dve, 1)
                    dve.wait_ge(s_dve, SD["rstd"])
                    nc.vector.scalar_tensor_tensor(out=HN[:], in0=HN[:], scalar=0.0,
                                                   in1=rstd[:].unsqueeze(2).to_broadcast([NP, NT, F]),
                                                   op0=ALU.max, op1=ALU.mult).then_inc(s_dve, 1)

                @block.scalar
                def _(act):
                    act.wait_ge(s_dve, SD["var_s"])
                    nc.scalar.activation(rstd[:], var[:], ACT.Sqrt, bias=eps[0:NP, :]).then_inc(s_std, 1)
            ctx.clear()

        def rounds(eng, body):
            body(0, 0)
            body(0, 1)
            with eng.Fori(1, NIT) as it:
                body(it, 0)
                body(it, 1)

        def staggered(eng, early, late):
            def one(it):
                early(it, 1)
                late(it, 0)
                early(it + 1, 0)
                late(it, 1)
            early(0, 0)
            one(0)
            if NIT > 2:
                with eng.Fori(1, NIT - 1) as it:
                    one(it)
            early(NIT - 1, 1)
            late(NIT - 1, 0)
            late(NIT - 1, 1)

        def turned(t, q):
            return t.rearrange("f (p j) -> f j p", j=T)[:, 4 * q:4 * q + 4, :]

        def block_rows(eng, b):
            return [eng.snap(edges_of(half, b)) if not isinstance(b, int) else edges_of(half, b) for half in range(2)]

        def load_rows(sp, buf, array, b, s, cols):
            for half in range(2):
                rows = array[bass.ds(b[half], BK)] if cols == 1 else array[bass.ds(b[half], BK), :]
                view = rows.rearrange("(p j) -> p j", p=P) if cols == 1 else rows.rearrange("(p j) f -> p (j f)", p=P)
                sp.dma_start(buf[:, half * T * cols:(half + 1) * T * cols], view).then_inc(s, 16)

        def load_mask(sp, buf, mask, b, s):
            for half in range(2):
                row = mask[bass.ds(b[half], BK)]
                sp.dma_start(buf[half * F:(half + 1) * F, :], row.partition_broadcast(F)).then_inc(s, 16)

        def gather(g, table, idx, s, top):
            for j in range(T):
                for half in range(2):
                    nc.gpsimd.indirect_dma_start(
                        g[:, j * P + half * F:j * P + (half + 1) * F], None, table,
                        IND(ap=idx[:, half * T + j:half * T + j + 1], axis=0),
                        bounds_check=top, oob_is_err=False).then_inc(s, 16)

        GOT = 2 * T * 16

        def store_rows(act, buf, to, b, s, cols):
            for half in range(2):
                rows = to[bass.ds(b * BK + half * H, BK), :].rearrange("(p j) f -> p (j f)", p=P)
                act.dma_start(rows, buf[:, half, :, :].rearrange("p j f -> p (j f)")).then_inc(s, 16)

        def edge0():
            with Stage() as ctx:
                sd = [sb(f"e0_sd{i}", [P, 4 * T], I32, ctx) for i in range(2)]
                same = [sb(f"e0_same{i}", [P, BK], BF16, ctx) for i in range(2)]
                ea = [sb(f"e0_ea{i}", [P, 2 * T * D10], F32, ctx) for i in range(2)]
                eaT = [sb(f"e0_eaT{i}", [T * D10, 2 * P], F32, ctx) for i in range(2)]
                g = [sb(f"e0_g{i}", [P, T * P], F32, ctx) for i in range(2)]
                msg = [sb(f"e0_msg{i}", [P, BK], F32, ctx) for i in range(2)]
                R = [sb(f"e0_R{i}", [P, BK], F32, ctx) for i in range(2)]
                o = [sb(f"e0_o{i}", [P, 2, T, F], F32, ctx) for i in range(2)]
                wpad = sb("e0_wpad", [T * D10, 2 * T, P], F32, ctx)
                bias = sb("e0_bias", [P, 1], F32, ctx)
                zero = sb("e0_zero", [P, 2 * BK * F // P], F32, ctx)
                low = sb("e0_low", [P, 4 * T], I32, ctx)
                high = sb("e0_high", [P, 4 * T], I32, ctx)
                hot_low = [sb(f"e0_hot_low{i}", [P, T, P], BF16, ctx) for i in range(2)]
                hot_high = [sb(f"e0_hot_high{i}", [P, T, HB], BF16, ctx) for i in range(2)]
                over = sb("e0_over", [P, 2 * OT], I32, ctx)
                over_low = sb("e0_over_low", [P, 2 * OT], I32, ctx)
                over_high = sb("e0_over_high", [P, 2 * OT], I32, ctx)
                o_low = sb("e0_o_low", [P, 2 * OT, P], BF16, ctx)
                o_high = sb("e0_o_high", [P, 2 * OT, HB], BF16, ctx)
                counts = sb("e0_counts", [HB, 2, P], F32, ctx)
                zT = [ps(f"e0_zT{i}", [P, 4, P], ctx) for i in range(Q)]
                oT = [ps(f"e0_oT{i}", [P, 4, 2, F], ctx) for i in range(Q)]
                eT = ps("e0_eT", [T * D10, 2 * P], ctx)
                cnt = [ps(f"e0_cnt{i}", [HB, P], ctx) for i in range(2)]
                s_w, s_wz, s_over, s_ov, s_ovm, s_zero, s_zf, s_init, s_cnt, s_cnto = (ctx.sem(f"e0_{n}") for n in (
                    "weights", "weights_zeroed", "over_loaded", "over_hot", "over_counted", "zero_set", "own_zeroed", "initial",
                    "counts_read", "counts_stored"))
                gathered = dma_pair("e0_gathered")
                idx_in, same_in, ea_in, ea_turned, ea_copied, scanned, stored = (ctx.pair(f"e0_{n}") for n in (
                    "idx_in", "same_in", "ea_in", "ea_turned", "ea_copied", "scanned", "stored"))
                z_ready, msg_ready, o_turned, o_copied = ([ctx.pair(f"e0_{n}{q}_") for q in range(Q)] for n in (
                    "z_ready", "msg_ready", "o_turned", "o_copied"))
                low_made, high_made = ctx.pair("e0_low_made"), ctx.pair("e0_high_made")
                hot = [ctx.sem(f"e0_hot{s}") for s in range(4)]
                begun, loading = ctx.sem("e0_gathers_begun"), ctx.sem("e0_loads_begun")
                s_cntp = ctx.sem("e0_counts_read0")
                counted = [ctx.sem(f"e0_counted{s}") for s in range(4)]
                with nc.Block() as block:
                    @block.sync
                    def _(sp):
                        sp.wait_ge(s_wz, 1)
                        for j in range(T):
                            for half in range(2):
                                sp.dma_start(wpad[j * D10:(j + 1) * D10, half * T + j, half * F:(half + 1) * F],
                                             w["L0_gnn_W_edge"]).then_inc(s_w, 16)
                        for half in range(2):
                            sp.dma_start(bias[half * F:(half + 1) * F, :],
                                         w["L0_gnn_b_edge"].rearrange("(f o) -> f o", o=1)).then_inc(s_w, 16)
                        sp.dma_start(over[:, 0:OT], src[BASE:H].rearrange("(p j) -> p j", p=P)).then_inc(s_over, 16)
                        sp.dma_start(over[:, OT:2 * OT], dst[BASE:H].rearrange("(p j) -> p j", p=P)).then_inc(s_over, 16)
                        sp.wait_ge(s_zero, 1)

                        def load(it, par):
                            b = 2 * it + par
                            rows = block_rows(sp, b)
                            zeros_at = b * 2 * BK if isinstance(b, int) else sp.snap(b * 2 * BK)
                            wait_reuse(sp, gathered[par], it * GOT)
                            wait_reuse(sp, high_made[par], it)
                            sp.sem_inc(loading, 1)
                            load_rows(sp, sd[par][:, 0:2 * T], src, rows, idx_in[par], 1)
                            load_rows(sp, sd[par][:, 2 * T:4 * T], dst, rows, idx_in[par], 1)
                            wait_reuse(sp, ea_turned[par], it)
                            sp.sem_inc(loading, 1)
                            load_rows(sp, ea[par], ea10, rows, ea_in[par], D10)
                            wait_reuse(sp, scanned[par], it)
                            sp.sem_inc(loading, 1)
                            load_mask(sp, same[par], same_d, rows, same_in[par])
                            sp.dma_start(own_at_start[bass.ds(zeros_at, 2 * BK), :].rearrange("(p j) f -> p (j f)", p=P),
                                         zero[:]).then_inc(s_zf, 16)
                        rounds(sp, load)
                        sp.wait_ge(s_zf, 16 * NB)
                        sp.wait_ge(s_cnt, 1)
                        sp.dma_start(count_d.rearrange("a (h l) -> h a l", l=P), counts[:]).then_inc(s_cnto, 16)
                        sp.wait_ge(s_cnto, 16)

                    @block.gpsimd
                    def _(pool):
                        def g_block(it, par):
                            pool.wait_ge(idx_in[par], 64 * (it + 1))
                            wait_reuse(pool, z_ready[Q - 1][par], it)
                            pool.sem_inc(begun, 1)
                            gather(g[par], table0, sd[par], gathered[par], top)
                        top = pool.to_reg(N - 1)
                        rounds(pool, g_block)

                    @block.tensor
                    def _(pe):
                        pe.wait_ge(s_w, 16 * (2 * T + 2))
                        pe.wait_ge(s_ov, 5)
                        for a in range(2):
                            for j in range(OT):
                                mm = nc.tensor.matmul(cnt[a][:], o_high[:, a * OT + j, :], o_low[:, a * OT + j, :],
                                                      start=(j == 0), stop=False, skip_group_check=True)
                            mm.then_inc(s_ovm, 1)

                        def turn_in(it, par):
                            b = 2 * it + par
                            for s in range(4):
                                pe.wait_ge(hot[s], b + 1)
                                for j in range(T):
                                    mm = nc.tensor.matmul(cnt[s // 2][:], hot_high[s % 2][:, j, :], hot_low[s % 2][:, j, :],
                                                          start=False, stop=False, skip_group_check=True)
                                mm.then_inc(counted[s], 1)
                            pe.wait_ge(ea_in[par], 32 * (it + 1))
                            wait_reuse(pe, ea_copied[1 - par], it + par)
                            for half in range(2):
                                mm = nc.tensor.transpose(eT[:, half * P:(half + 1) * P],
                                                         ea[par][:, half * T * D10:(half + 1) * T * D10], ident[:])
                            mm.then_inc(ea_turned[par], 1)
                            pe.wait_ge(ea_copied[par], it + 1)
                            pe.wait_ge(gathered[par], GOT * (it + 1))
                            for q in range(Q):
                                wait_reuse(pe, msg_ready[q][1 - par], it + par)
                                for jj in range(4):
                                    j = 4 * q + jj
                                    nc.tensor.matmul(zT[q][:, jj, :], g[par][:, j * P:(j + 1) * P], ident[:],
                                                     start=True, stop=False)
                                    for half in range(2):
                                        mm = nc.tensor.matmul(zT[q][:, jj, :], wpad[:, half * T + j, :],
                                                              eaT[par][:, half * P:(half + 1) * P],
                                                              start=False, stop=(half == 1))
                                mm.then_inc(z_ready[q][par], 1)

                        def turn_out(it, par):
                            pe.wait_ge(scanned[par], it + 1)
                            v = R[par][:, :].rearrange("f (p j) -> f j p", j=T)
                            for q in range(Q):
                                wait_reuse(pe, o_copied[q][1 - par], it + par)
                                for jj in range(4):
                                    mm = nc.tensor.transpose(oT[q][:, jj, :, :].rearrange("p h f -> p (h f)"),
                                                             v[:, 4 * q + jj, :], ident[:])
                                mm.then_inc(o_turned[q][par], 1)
                        staggered(pe, turn_in, turn_out)

                    @block.scalar
                    def _(act):
                        act.wait_ge(s_w, 16 * (2 * T + 2))

                        def relu(it, par):
                            act.wait_ge(ea_turned[par], it + 1)
                            wait_reuse(act, z_ready[Q - 1][par], it)
                            nc.scalar.copy(eaT[par][:], eT[:]).then_inc(ea_copied[par], 1)
                            wait_reuse(act, scanned[par], it)
                            for q in range(Q):
                                act.wait_ge(z_ready[q][par], it + 1)
                                nc.scalar.activation(turned(msg[par][:, :], q), zT[q][:], ACT.Relu,
                                                     bias=bias[:]).then_inc(msg_ready[q][par], 1)

                        def give(it, par):
                            wait_reuse(act, stored[par], 32 * it)
                            for q in range(Q):
                                act.wait_ge(o_turned[q][par], it + 1)
                                nc.scalar.copy(o[par][:, :, 4 * q:4 * q + 4, :], oT[q][:].rearrange("p j h f -> p h j f")
                                               ).then_inc(o_copied[q][par], 1)
                            act.wait_ge(o_copied[0][par], it + 1)
                            act.wait_ge(o_copied[Q - 1][par], it + 1)
                            store_rows(act, o[par], stream, 2 * it + par, stored[par], F)
                        staggered(act, relu, give)
                        act.wait_ge(stored[0], 32 * NIT)
                        act.wait_ge(stored[1], 32 * NIT)

                    @block.vector
                    def _(dve):
                        nc.vector.memset(wpad[:], 0.0).then_inc(s_wz, 1)
                        nc.vector.memset(zero[:], 0.0).then_inc(s_zero, 1)
                        nc.vector.memset(R[1][:, BK - 1:BK], 0.0).then_inc(s_init, 1)
                        dve.wait_ge(s_over, 32)
                        nc.vector.tensor_scalar(over_low[:], over[:], P - 1, None, ALU.bitwise_and).then_inc(s_ov, 1)
                        nc.vector.tensor_scalar(over_high[:], over[:], 7, None, ALU.logical_shift_right).then_inc(s_ov, 1)
                        dve.wait_ge(s_ov, 2)
                        nc.vector.tensor_tensor(o_low[:], iota[:, 0:P].unsqueeze(1).to_broadcast([P, 2 * OT, P]),
                                                over_low[:].unsqueeze(2).to_broadcast([P, 2 * OT, P]),
                                                ALU.is_equal).then_inc(s_ov, 1)
                        nc.vector.tensor_tensor(o_high[:], iota[:, 0:HB].unsqueeze(1).to_broadcast([P, 2 * OT, HB]),
                                                over_high[:].unsqueeze(2).to_broadcast([P, 2 * OT, HB]),
                                                ALU.is_equal).then_inc(s_ov, 1)
                        dve.wait_ge(s_ov, 4)
                        nc.vector.tensor_scalar(o_high[:], o_high[:], -1.0, None, ALU.mult).then_inc(s_ov, 1)
                        dve.wait_ge(s_init, 1)

                        def histogram(it, par):
                            b = 2 * it + par
                            dve.wait_ge(idx_in[par], 64 * (it + 1))
                            wait_reuse(dve, hot[3], b)
                            nc.vector.tensor_scalar(low[:], sd[par][:], P - 1, None, ALU.bitwise_and
                                                    ).then_inc(low_made[par], 1)
                            nc.vector.tensor_scalar(high[:], sd[par][:], 7, None, ALU.logical_shift_right
                                                    ).then_inc(high_made[par], 1)
                            dve.wait_ge(low_made[par], it + 1)
                            dve.wait_ge(high_made[par], it + 1)
                            for s in range(4):
                                if s < 2:
                                    wait_reuse(dve, counted[s + 2], b)
                                else:
                                    dve.wait_ge(counted[s - 2], b + 1)
                                lv = low[:, s * T:(s + 1) * T].unsqueeze(2)
                                hv = high[:, s * T:(s + 1) * T].unsqueeze(2)
                                nc.vector.tensor_tensor(hot_low[s % 2][:], iota[:, 0:P].unsqueeze(1).to_broadcast([P, T, P]),
                                                        lv.to_broadcast([P, T, P]), ALU.is_equal)
                                nc.vector.tensor_tensor(hot_high[s % 2][:], iota[:, 0:HB].unsqueeze(1).to_broadcast([P, T, HB]),
                                                        hv.to_broadcast([P, T, HB]), ALU.is_equal).then_inc(hot[s], 1)

                        def scan(it, par):
                            dve.wait_ge(same_in[par], 32 * (it + 1))
                            for q in range(Q):
                                dve.wait_ge(msg_ready[q][par], it + 1)
                            wait_reuse(dve, o_turned[Q - 1][par], it)
                            wait_reuse(dve, scanned[1 - par], it + par)
                            nc.vector.tensor_tensor_scan(R[par][:, :], same[par][:, :], msg[par][:, :],
                                                         R[1 - par][:, BK - 1:BK], ALU.mult, ALU.add
                                                         ).then_inc(scanned[par], 1)
                        staggered(dve, histogram, scan)
                        for s in range(4):
                            dve.wait_ge(counted[s], NB)
                        nc.vector.tensor_copy(counts[:, 0, :], cnt[0][:]).then_inc(s_cntp, 1)
                        dve.wait_ge(s_cntp, 1)
                        nc.vector.tensor_copy(counts[:, 1, :], cnt[1][:]).then_inc(s_cnt, 1)
                ctx.clear()

                        
        def edge1():
            with Stage() as ctx:
                idx = [sb(f"e1_idx{i}", [P, 2 * T], I32, ctx) for i in range(2)]
                same = [sb(f"e1_same{i}", [P, BK], BF16, ctx) for i in range(2)]
                reset = [sb(f"e1_reset{i}", [P, BK], BF16, ctx) for i in range(2)]
                g = [sb(f"e1_g{i}", [P, T * P], F32, ctx) for i in range(2)]
                own = [sb(f"e1_own{i}", [P, T, 2, F], F32, ctx) for i in range(2)]
                ownT = [sb(f"e1_ownT{i}", [P, BK], F32, ctx) for i in range(2)]
                filled = [sb(f"e1_filled{i}", [P, BK], F32, ctx) for i in range(2)]
                z = [sb(f"e1_z{i}", [P, BK], F32, ctx) for i in range(2)]
                R = [sb(f"e1_R{i}", [P, BK], F32, ctx) for i in range(2)]
                o = [sb(f"e1_o{i}", [P, 2, T, F], F32, ctx) for i in range(2)]
                w2 = sb("e1_w2", [P, P], F32, ctx)
                base_dst = sb("e1_base_dst", [1, 1], I32, ctx)
                owT = [ps(f"e1_owT{i}", [P, 4, P], ctx) for i in range(Q)]
                gT = [ps(f"e1_gT{i}", [P, 4, P], ctx) for i in range(Q)]
                zW = [ps(f"e1_zW{i}", [P, 4 * P], ctx) for i in range(Q)]
                oT = [ps(f"e1_oT{i}", [P, 4, 2, F], ctx) for i in range(Q)]
                s_w, s_wz, s_b, s_init, s_first, begun, loading = (ctx.sem(f"e1_{n}") for n in (
                    "weights", "weights_zeroed", "base_dst", "initial", "first_own", "gathers_begun", "loads_begun"))
                gathered = dma_pair("e1_gathered")
                idx_in, same_in, reset_in, own_in, fill_done, relued, scanned, stored = (ctx.pair(f"e1_{n}") for n in (
                    "idx_in", "same_in", "reset_in", "own_in", "fill_done", "relued", "scanned", "stored"))
                own_turned, own_copied, g_turned, z_made, w_ready, o_turned, o_copied = (
                    [ctx.pair(f"e1_{n}{q}_") for q in range(Q)] for n in (
                        "own_turned", "own_copied", "g_turned", "z_made", "w_ready", "o_turned", "o_copied"))
                with nc.Block() as block:
                    @block.sync
                    def _(sp):
                        sp.dma_start(base_dst[:], dst[BASE:BASE + 1].rearrange("(o f) -> o f", o=1)).then_inc(s_b, 16)
                        sp.wait_ge(s_wz, 1)
                        for half in range(2):
                            sp.dma_start(w2[half * F:(half + 1) * F, half * F:(half + 1) * F], w["L1_gnn_W2"]).then_inc(s_w, 16)
                        sp.wait_ge(s_b, 16)
                        node = sp.value_load(base_dst[0:1, 0:1], min_val=0, max_val=N - 1)
                        sp.wait_ge(s_init, 2)
                        sp.dma_start(filled[1][F:P, BK - 1:BK], own_d[bass.ds(node, 1), :].rearrange("o f -> f o")
                                     ).then_inc(s_first, 16)

                        def load(it, par):
                            rows = block_rows(sp, 2 * it + par)
                            wait_reuse(sp, gathered[par], it * GOT)
                            sp.sem_inc(loading, 1)
                            load_rows(sp, idx[par], src, rows, idx_in[par], 1)
                            wait_reuse(sp, own_turned[Q - 1][par], it)
                            sp.sem_inc(loading, 1)
                            load_pairs(sp, own[par], own_at_start, rows, own_in[par])
                            wait_reuse(sp, fill_done[par], it)
                            sp.sem_inc(loading, 1)
                            load_mask(sp, same[par], same_d, rows, same_in[par])
                            wait_reuse(sp, scanned[par], it)
                            sp.sem_inc(loading, 1)
                            load_mask(sp, reset[par], reset_d, rows, reset_in[par])
                        rounds(sp, load)

                    @block.gpsimd
                    def _(pool):
                        top = pool.to_reg(N - 1)

                        def g_block(it, par):
                            pool.wait_ge(idx_in[par], 32 * (it + 1))
                            wait_reuse(pool, g_turned[Q - 1][par], it)
                            pool.sem_inc(begun, 1)
                            gather(g[par], table1, idx[par], gathered[par], top)
                        rounds(pool, g_block)

                    @block.tensor
                    def _(pe):
                        pe.wait_ge(s_w, 32)

                        def turn_in(it, par):
                            pe.wait_ge(own_in[par], 32 * (it + 1))
                            for q in range(Q):
                                wait_reuse(pe, own_copied[q][1 - par], it + par)
                                for jj in range(4):
                                    mm = nc.tensor.transpose(owT[q][:, jj, :],
                                                             own[par][:, 4 * q + jj, :, :].rearrange("p h f -> p (h f)"), ident[:])
                                mm.then_inc(own_turned[q][par], 1)
                            pe.wait_ge(gathered[par], GOT * (it + 1))
                            for q in range(Q):
                                wait_reuse(pe, z_made[q][1 - par], it + par)
                                for jj in range(4):
                                    j = 4 * q + jj
                                    mm = nc.tensor.transpose(gT[q][:, jj, :], g[par][:, j * P:(j + 1) * P], ident[:])
                                mm.then_inc(g_turned[q][par], 1)

                        def turn_out(it, par):
                            pe.wait_ge(relued[par], it + 1)
                            wait_reuse(pe, scanned[1 - par], it + par)
                            for q in range(Q):
                                nc.tensor.matmul(zW[q][:], w2[:], z[par][:, q * 4 * P:(q + 1) * 4 * P], start=True, stop=True
                                                 ).then_inc(w_ready[q][par], 1)
                            turn_back(pe, it, par, R[par], scanned, oT, o_copied, o_turned)
                        staggered(pe, turn_in, turn_out)

                    @block.scalar
                    def _(act):
                        def copy_own(it, par):
                            wait_reuse(act, fill_done[par], it)
                            for q in range(Q):
                                act.wait_ge(own_turned[q][par], it + 1)
                                nc.scalar.copy(turned(ownT[par][:, :], q), owT[q][:]).then_inc(own_copied[q][par], 1)

                        def give(it, par):
                            for q in range(Q):
                                act.wait_ge(z_made[q][par], it + 1)
                            nc.scalar.activation(z[par][:], z[par][:], ACT.Relu).then_inc(relued[par], 1)
                            give_back(act, it, par, o[par], stream, oT, o_turned, o_copied, stored)
                        staggered(act, copy_own, give)
                        act.wait_ge(stored[0], 32 * NIT)
                        act.wait_ge(stored[1], 32 * NIT)

                    @block.vector
                    def _(dve):
                        nc.vector.memset(w2[:], 0.0).then_inc(s_wz, 1)
                        nc.vector.memset(filled[1][:, BK - 1:BK], 0.0).then_inc(s_init, 1)
                        nc.vector.memset(R[1][:, BK - 1:BK], -BIG).then_inc(s_init, 1)
                        dve.wait_ge(s_first, 16)

                        def fill(it, par):
                            dve.wait_ge(same_in[par], 32 * (it + 1))
                            for q in range(Q):
                                dve.wait_ge(own_copied[q][par], it + 1)
                            wait_reuse(dve, fill_done[1 - par], it + par)
                            nc.vector.tensor_tensor_scan(filled[par][:], same[par][:], ownT[par][:],
                                                         filled[1 - par][:, BK - 1:BK], ALU.mult, ALU.add
                                                         ).then_inc(fill_done[par], 1)
                            dve.wait_ge(fill_done[par], it + 1)
                            wait_reuse(dve, w_ready[Q - 1][par], it)
                            for q in range(Q):
                                dve.wait_ge(g_turned[q][par], it + 1)
                                nc.vector.tensor_tensor(turned(z[par][:, :], q), gT[q][:], turned(filled[par][:, :], q),
                                                        ALU.add).then_inc(z_made[q][par], 1)

                        def scan(it, par):
                            dve.wait_ge(reset_in[par], 32 * (it + 1))
                            wait_reuse(dve, o_turned[Q - 1][par], it)
                            wait_reuse(dve, scanned[1 - par], it + par)
                            for q in range(Q):
                                dve.wait_ge(w_ready[q][par], it + 1)
                                before_ = R[1 - par][:, BK - 1:BK] if q == 0 else R[par][:, q * 512 - 1:q * 512]
                                if q:
                                    dve.wait_ge(half_scanned[par], it * (Q - 1) + q)
                                sc = nc.vector.tensor_tensor_scan(
                                    R[par][:, q * 512:(q + 1) * 512], reset[par][:, q * 512:(q + 1) * 512], zW[q][:],
                                    before_, ALU.add, ALU.max)
                                sc.then_inc(scanned[par] if q == Q - 1 else half_scanned[par], 1)
                        half_scanned = ctx.pair("e1_half_scanned")

                        def both(it, par):
                            fill(it, par)
                            scan(it, par)
                        rounds(dve, both)
                ctx.clear()

        def edge2():
            with Stage() as ctx:
                idx = [sb(f"e2_idx{i}", [P, 2 * T], I32, ctx) for i in range(2)]
                same = [sb(f"e2_same{i}", [P, BK], BF16, ctx) for i in range(2)]
                g = [sb(f"e2_g{i}", [P, T * P], F32, ctx) for i in range(2)]
                msg = [sb(f"e2_msg{i}", [P, BK], F32, ctx) for i in range(2)]
                R = [sb(f"e2_R{i}", [P, BK], F32, ctx) for i in range(2)]
                o = [sb(f"e2_o{i}", [P, 2, T, F], F32, ctx) for i in range(2)]
                gT = [ps(f"e2_gT{i}", [P, 4, P], ctx) for i in range(Q)]
                oT = [ps(f"e2_oT{i}", [P, 4, 2, F], ctx) for i in range(Q)]
                s_init, begun, loading = (ctx.sem(f"e2_{n}") for n in ("initial", "gathers_begun", "loads_begun"))
                gathered = dma_pair("e2_gathered")
                idx_in, same_in, scanned, stored = (ctx.pair(f"e2_{n}") for n in (
                    "idx_in", "same_in", "scanned", "stored"))
                g_turned, msg_ready, o_turned, o_copied = ([ctx.pair(f"e2_{n}{q}_") for q in range(Q)] for n in (
                    "g_turned", "msg_ready", "o_turned", "o_copied"))
                with nc.Block() as block:
                    @block.sync
                    def _(sp):
                        def load(it, par):
                            rows = block_rows(sp, 2 * it + par)
                            wait_reuse(sp, gathered[par], it * GOT)
                            sp.sem_inc(loading, 1)
                            load_rows(sp, idx[par], src, rows, idx_in[par], 1)
                            wait_reuse(sp, scanned[par], it)
                            sp.sem_inc(loading, 1)
                            load_mask(sp, same[par], same_d, rows, same_in[par])
                        rounds(sp, load)

                    @block.gpsimd
                    def _(pool):
                        top = pool.to_reg(N - 1)

                        def g_block(it, par):
                            pool.wait_ge(idx_in[par], 32 * (it + 1))
                            wait_reuse(pool, g_turned[Q - 1][par], it)
                            pool.sem_inc(begun, 1)
                            gather(g[par], table2, idx[par], gathered[par], top)
                        rounds(pool, g_block)

                    @block.tensor
                    def _(pe):
                        def turn_in(it, par):
                            pe.wait_ge(gathered[par], GOT * (it + 1))
                            for q in range(Q):
                                wait_reuse(pe, msg_ready[q][1 - par], it + par)
                                for jj in range(4):
                                    j = 4 * q + jj
                                    mm = nc.tensor.transpose(gT[q][:, jj, :], g[par][:, j * P:(j + 1) * P], ident[:])
                                mm.then_inc(g_turned[q][par], 1)

                        def turn_out(it, par):
                            turn_back(pe, it, par, R[par], scanned, oT, o_copied, o_turned)
                        staggered(pe, turn_in, turn_out)

                    @block.scalar
                    def _(act):
                        def copy_in(it, par):
                            wait_reuse(act, scanned[par], it)
                            for q in range(Q):
                                act.wait_ge(g_turned[q][par], it + 1)
                                nc.scalar.copy(turned(msg[par][:, :], q), gT[q][:]).then_inc(msg_ready[q][par], 1)

                        def give(it, par):
                            give_back(act, it, par, o[par], stream, oT, o_turned, o_copied, stored)
                        staggered(act, copy_in, give)
                        act.wait_ge(stored[0], 32 * NIT)
                        act.wait_ge(stored[1], 32 * NIT)

                    @block.vector
                    def _(dve):
                        nc.vector.memset(R[1][:, BK - 1:BK], 0.0).then_inc(s_init, 1)
                        dve.wait_ge(s_init, 1)

                        def scan(it, par):
                            dve.wait_ge(same_in[par], 32 * (it + 1))
                            for q in range(Q):
                                dve.wait_ge(msg_ready[q][par], it + 1)
                            wait_reuse(dve, o_turned[Q - 1][par], it)
                            wait_reuse(dve, scanned[1 - par], it + par)
                            nc.vector.tensor_tensor_scan(R[par][:, :], same[par][:, :], msg[par][:, :],
                                                         R[1 - par][:, BK - 1:BK], ALU.mult, ALU.add
                                                         ).then_inc(scanned[par], 1)
                        rounds(dve, scan)
                ctx.clear()

        def edge3():
            with Stage() as ctx:
                C = 4 * P
                idx = [sb(f"e3_idx{i}", [P, 2 * T], I32, ctx) for i in range(2)]
                same = [sb(f"e3_same{i}", [P, BK], BF16, ctx) for i in range(2)]
                g = [sb(f"e3_g{i}", [P, T * P], F32, ctx) for i in range(2)]
                eh = [sb(f"e3_eh{i}", [P, T, 2, F], F32, ctx) for i in range(2)]
                m = [sb(f"e3_m{i}", [P, BK], F32, ctx) for i in range(2)]
                top_ = [sb(f"e3_max{i}", [P, BK + 1], F32, ctx) for i in range(2)]
                lift = [sb(f"e3_lift{q}", [P, 2, C], F32, ctx) for q in range(Q)]
                part = [sb(f"e3_part{q}", [P, 2, C], F32, ctx) for q in range(Q)]
                den = [sb(f"e3_den{i}", [P, BK], F32, ctx) for i in range(2)]
                num = [sb(f"e3_num{i}", [P, BK], F32, ctx) for i in range(2)]
                o = [sb(f"e3_o{i}", [P, 2, T, 2 * F], F32, ctx) for i in range(2)]
                zT = [ps(f"e3_zT{i}", [P, 4, P], ctx) for i in range(Q)]
                oT = [[ps(f"e3_oT{k}_{i}", [P, 4, 2, F], ctx) for i in range(Q)] for k in range(2)]
                s_init, begun, loading = (ctx.sem(f"e3_{n}") for n in ("initial", "gathers_begun", "loads_begun"))
                gathered = dma_pair("e3_gathered")
                idx_in, same_in, eh_in, stored, carried = (ctx.pair(f"e3_{n}") for n in (
                    "idx_in", "same_in", "eh_in", "stored", "carried"))
                z_ready, m_ready, maxed, lifted, under, expd, decay, parted, den_done, num_done = (
                    [ctx.pair(f"e3_{n}{q}_") for q in range(Q)] for n in (
                        "z_ready", "m_ready", "maxed", "lifted", "under", "expd", "decay", "parted", "den_done", "num_done"))
                o_turned = [ctx.pair(f"e3_o_turned{q}_") for q in range(Q)]
                o_copied = [ctx.pair(f"e3_o_copied{q}_") for q in range(Q)]
                with nc.Block() as block:
                    @block.sync
                    def _(sp):
                        def load(it, par):
                            rows = block_rows(sp, 2 * it + par)
                            wait_reuse(sp, gathered[par], it * GOT)
                            sp.sem_inc(loading, 1)
                            load_rows(sp, idx[par], src, rows, idx_in[par], 1)
                            wait_reuse(sp, z_ready[Q - 1][par], it)
                            sp.sem_inc(loading, 1)
                            load_pairs(sp, eh[par], ea64, rows, eh_in[par])
                            wait_reuse(sp, num_done[Q - 1][par], it)
                            sp.sem_inc(loading, 1)
                            load_mask(sp, same[par], same_d, rows, same_in[par])
                        rounds(sp, load)

                    @block.gpsimd
                    def _(pool):
                        top = pool.to_reg(N - 1)

                        def g_block(it, par):
                            pool.wait_ge(idx_in[par], 32 * (it + 1))
                            wait_reuse(pool, z_ready[Q - 1][par], it)
                            pool.sem_inc(begun, 1)
                            gather(g[par], table3, idx[par], gathered[par], top)
                        rounds(pool, g_block)

                    @block.tensor
                    def _(pe):
                        def turn_in(it, par):
                            pe.wait_ge(eh_in[par], 32 * (it + 1))
                            pe.wait_ge(gathered[par], GOT * (it + 1))
                            for q in range(Q):
                                wait_reuse(pe, m_ready[q][1 - par], it + par)
                                for jj in range(4):
                                    j = 4 * q + jj
                                    nc.tensor.matmul(zT[q][:, jj, :], g[par][:, j * P:(j + 1) * P], ident[:],
                                                     start=True, stop=False)
                                    mm = nc.tensor.matmul(zT[q][:, jj, :], eh[par][:, j, :, :].rearrange("p h f -> p (h f)"),
                                                          ident[:], start=False, stop=True)
                                mm.then_inc(z_ready[q][par], 1)

                        def turn_out(it, par):
                            for q in range(Q):
                                pe.wait_ge(num_done[q][par], it + 1)
                            pe.wait_ge(den_done[Q - 1][par], it + 1)
                            for q in range(Q):
                                wait_reuse(pe, o_copied[q][1 - par], it + par)
                                for k, t in enumerate((num[par][:, :], den[par][:, :])):
                                    v = t.rearrange("f (p j) -> f j p", j=T)
                                    for jj in range(4):
                                        mm = nc.tensor.transpose(oT[k][q][:, jj, :, :].rearrange("p h f -> p (h f)"),
                                                                 v[:, 4 * q + jj, :], ident[:])
                                mm.then_inc(o_turned[q][par], 1)
                        staggered(pe, turn_in, turn_out)

                    @block.scalar
                    def _(act):
                        def exps(it, par):
                            for q in range(Q):
                                act.wait_ge(lifted[q][par], it + 1)
                                act.wait_ge(under[q][par], it + 1)
                                nc.scalar.activation(lift[q][:], lift[q][:], ACT.Exp).then_inc(expd[q][par], 1)

                        def relu(it, par):
                            wait_reuse(act, num_done[Q - 1][par], it)
                            for q in range(Q):
                                act.wait_ge(z_ready[q][par], it + 1)
                                nc.scalar.activation(turned(m[par][:, :], q), zT[q][:], ACT.Relu).then_inc(m_ready[q][par], 1)
                            exps(it, par)

                        def give(it, par):
                            wait_reuse(act, stored[par], 48 * it)
                            for q in range(Q):
                                act.wait_ge(o_turned[q][par], it + 1)
                                for k in range(2):
                                    cp = nc.scalar.copy(o[par][:, :, 4 * q:4 * q + 4, k * F:(k + 1) * F],
                                                        oT[k][q][:].rearrange("p j h f -> p h j f"))
                                cp.then_inc(o_copied[q][par], 1)
                            for q in range(Q):
                                act.wait_ge(o_copied[q][par], it + 1)
                            store_rows(act, o[par], stream3, 2 * it + par, stored[par], 2 * F)
                            act.dma_start(maxes[:, bass.ds((2 * it + par) * BK, BK)], top_[par][:, 1:BK + 1]
                                          ).then_inc(stored[par], 16)
                        staggered(act, relu, give)
                        act.wait_ge(stored[0], 48 * NIT)
                        act.wait_ge(stored[1], 48 * NIT)

                    @block.vector
                    def _(dve):
                        nc.vector.memset(top_[1][:, BK:BK + 1], 0.0).then_inc(s_init, 1)
                        nc.vector.memset(den[1][:, BK - 1:BK], 0.0).then_inc(s_init, 1)
                        nc.vector.memset(num[1][:, BK - 1:BK], 0.0).then_inc(s_init, 1)
                        dve.wait_ge(s_init, 3)

                        def logits(it, par, q):
                            c = slice(q * C, (q + 1) * C)
                            dve.wait_ge(maxed[q - 1][par] if q else carried[par], it + 1)
                            nc.vector.tensor_tensor_scan(top_[par][:, q * C + 1:(q + 1) * C + 1], same[par][:, c], m[par][:, c],
                                                         top_[par][:, q * C:q * C + 1], ALU.mult, ALU.max
                                                         ).then_inc(maxed[q][par], 1)
                            dve.wait_ge(maxed[q][par], it + 1)
                            wait_reuse(dve, den_done[q][1 - par], it + par)
                            nc.vector.tensor_tensor(lift[q][:, 0, :], top_[par][:, c], top_[par][:, q * C + 1:(q + 1) * C + 1],
                                                    ALU.subtract).then_inc(lifted[q][par], 1)
                            nc.vector.tensor_tensor(lift[q][:, 1, :], m[par][:, c], top_[par][:, q * C + 1:(q + 1) * C + 1],
                                                    ALU.subtract).then_inc(under[q][par], 1)

                        def sums(it, par, q):
                            c = slice(q * C, (q + 1) * C)
                            last = slice(BK - 1, BK) if q == 0 else slice(q * C - 1, q * C)
                            of = 1 - par if q == 0 else par
                            dve.wait_ge(expd[q][par], it + 1)
                            nc.vector.tensor_tensor(part[q][:, 0, :], lift[q][:, 0, :], same[par][:, c], ALU.mult
                                                    ).then_inc(decay[q][par], 1)
                            nc.vector.tensor_tensor(part[q][:, 1, :], lift[q][:, 1, :], m[par][:, c], ALU.mult
                                                    ).then_inc(parted[q][par], 1)
                            dve.wait_ge(decay[q][par], it + 1)
                            dve.wait_ge(parted[q][par], it + 1)
                            n_before = it + par if q == 0 else it + 1
                            wait_reuse(dve, den_done[(q - 1) % Q][of], n_before)
                            wait_reuse(dve, num_done[(q - 1) % Q][of], n_before)
                            nc.vector.tensor_tensor_scan(den[par][:, c], part[q][:, 0, :], lift[q][:, 1, :], den[of][:, last],
                                                         ALU.mult, ALU.add).then_inc(den_done[q][par], 1)
                            nc.vector.tensor_tensor_scan(num[par][:, c], part[q][:, 0, :], part[q][:, 1, :], num[of][:, last],
                                                         ALU.mult, ALU.add).then_inc(num_done[q][par], 1)

                        def both(it, par):
                            dve.wait_ge(same_in[par], 32 * (it + 1))
                            wait_reuse(dve, o_turned[Q - 1][par], it)
                            wait_reuse(dve, stored[par], 48 * it)
                            for q in range(Q):
                                dve.wait_ge(m_ready[q][par], it + 1)
                            wait_reuse(dve, maxed[Q - 1][1 - par], it + par)
                            nc.vector.tensor_copy(top_[par][:, 0:1], top_[1 - par][:, BK:BK + 1]).then_inc(carried[par], 1)
                            for q in range(Q):
                                logits(it, par, q)
                            for q in range(Q):
                                sums(it, par, q)
                        rounds(dve, both)
                ctx.clear()

        def load_pairs(sp, buf, array, b, s):
            for half in range(2):
                sp.dma_start(buf[:, :, half, :], array[bass.ds(b[half], BK), :].rearrange("(p j) f -> p j f", p=P)
                             ).then_inc(s, 16)

        def turn_back(pe, it, par, R, scanned, oT, o_copied, o_turned):
            pe.wait_ge(scanned[par], it + 1)
            v = R[:, :].rearrange("f (p j) -> f j p", j=T)
            for q in range(Q):
                wait_reuse(pe, o_copied[q][1 - par], it + par)
                for jj in range(4):
                    mm = nc.tensor.transpose(oT[q][:, jj, :, :].rearrange("p h f -> p (h f)"), v[:, 4 * q + jj, :], ident[:])
                mm.then_inc(o_turned[q][par], 1)

        def give_back(act, it, par, o, to, oT, o_turned, o_copied, stored):
            wait_reuse(act, stored[par], 32 * it)
            for q in range(Q):
                act.wait_ge(o_turned[q][par], it + 1)
                nc.scalar.copy(o[:, :, 4 * q:4 * q + 4, :], oT[q][:].rearrange("p j h f -> p h j f")
                               ).then_inc(o_copied[q][par], 1)
            for q in range(Q):
                act.wait_ge(o_copied[q][par], it + 1)
            store_rows(act, o, to, 2 * it + par, stored[par], F)

        def chunk(t, c):
            return t[:, bass.ds(c * CH, CH)]

        def same_values(to, of):
            return nc.vector.tensor_scalar(to, of, 1.0, None, ALU.mult)

        def over_f(v):
            return v.unsqueeze(2).to_broadcast([NP, CH, F])

        def over_n(row):
            return row.unsqueeze(1).to_broadcast([NP, CH, F])

        def chunks(eng, body):
            body(0, 0, 0)
            body(1, 0, 1)
            if NC > 2:
                with eng.Fori(1, NC // 2) as it:
                    body(2 * it, it, 0)
                    body(2 * it + 1, it, 1)

        def fetch(pool, ag, ix, table, got, ix_ready, used, begun, top):
            def one(c, it, par):
                pool.wait_ge(ix_ready[par], it + 1)
                wait_reuse(pool, used[par], it)
                pool.sem_inc(begun, 1)
                for t in range(CH):
                    nc.gpsimd.indirect_dma_start(ag[par][:, t, :], None, table, IND(ap=ix[par][:, t:t + 1], axis=0),
                                                 bounds_check=top, oob_is_err=False).then_inc(got[par], 16)
            chunks(pool, one)

        def next_index(dve, c, it, par, ix, got, ix_ready):
            wait_reuse(dve, got[1 - par], 16 * CH * (it + par))
            same_values(ix[1 - par][:], row_at[:, bass.ds(c * CH + CH, CH)]).then_inc(ix_ready[1 - par], 1)

        class Normed:
            names = ("mean", "mean_s", "centred", "square", "var", "var_s", "rstd", "h")

            def __init__(self, ctx, tag):
                self.small = [sb(f"{tag}_{n}", [NP, CH], F32, ctx) for n in ("lmean", "lvar", "lrstd")]
                self.sq = sb(f"{tag}_lsq", [NP, CH, F], F32, ctx)

            def vector(self, dve, xs, hn, s, seq, std, c, ready):
                mean, var, rstd = self.small
                nc.vector.tensor_reduce(mean[:], xs, AX, ALU.add).then_inc(s, 1)
                wait_reuse(dve, s, at(seq, "mean", c))
                nc.vector.tensor_scalar(mean[:], mean[:], 1.0 / F, None, ALU.mult).then_inc(s, 1)
                wait_reuse(dve, s, at(seq, "mean_s", c))
                ready()
                nc.vector.tensor_tensor(hn, xs, over_f(mean[:]), ALU.subtract).then_inc(s, 1)
                wait_reuse(dve, s, at(seq, "centred", c))
                nc.vector.tensor_tensor(self.sq[:], hn, hn, ALU.mult).then_inc(s, 1)
                wait_reuse(dve, s, at(seq, "square", c))
                nc.vector.tensor_reduce(var[:], self.sq[:], AX, ALU.add).then_inc(s, 1)
                wait_reuse(dve, s, at(seq, "var", c))
                nc.vector.tensor_scalar(var[:], var[:], 1.0 / F, None, ALU.mult).then_inc(s, 1)
                dve.wait_ge(std, c + 1)
                nc.vector.reciprocal(rstd[:], rstd[:]).then_inc(s, 1)
                wait_reuse(dve, s, at(seq, "rstd", c))
                nc.vector.scalar_tensor_tensor(out=hn, in0=hn, scalar=0.0, in1=over_f(rstd[:]), op0=ALU.max,
                                               op1=ALU.mult).then_inc(s, 1)

            def scalar(self, act, s, seq, std, c):
                mean, var, rstd = self.small
                wait_reuse(act, s, at(seq, "var_s", c))
                nc.scalar.activation(rstd[:], var[:], ACT.Sqrt, bias=eps[0:NP, :]).then_inc(std, 1)

        def turn_nodes(pT, rows):
            for i in range(NPR):
                mm = nc.tensor.transpose(pT[:, i, 0:NP], rows[:, 2 * i:2 * i + 2, :].rearrange("p a f -> p (a f)"),
                                         ident[0:NP, 0:NP])
            return mm

        def blocks_of(sp, big, small, s):
            for half in range(2):
                sp.dma_start(big[half * F:(half + 1) * F, half * F:(half + 1) * F], small).then_inc(s, 16)

        def column(sp, col, vec, s):
            for half in range(2):
                sp.dma_start(col[half * F:(half + 1) * F, :], vec.rearrange("(f o) -> f o", o=1)).then_inc(s, 16)

        def runs():
            with Stage() as ctx:
                c2 = sb("r_counts", [NP, 2, NT], F32, ctx)
                ones = sb("r_ones", [NP, NT], F32, ctx)
                cum = sb("r_cum", [NP, NT], F32, ctx)
                off = sb("r_off", [NP, 1], F32, ctx)
                first = sb("r_first", [NP, NT], F32, ctx)
                lastf = sb("r_last", [NP, NT], F32, ctx)
                late = sb("r_late", [NP, NT], F32, ctx)
                tmp = sb("r_tmp", [NP, NT], F32, ctx)
                none = sb("r_none", [NP, NT], F32, ctx)
                p = ps("r_p", [P, 512], ctx)
                at_cut = sb("r_at_cut", [NP, 1], F32, ctx)
                s_c, s_d, s_p, s_a = (ctx.sem(f"r_{n}") for n in ("counts_in", "dve", "rows_before", "roots"))
                with nc.Block() as block:
                    @block.sync
                    def _(sp):
                        for a in range(2):
                            sp.dma_start(c2[:, a, :], count_d[a, 0:N].rearrange("(p t) -> p t", p=NP)).then_inc(s_c, 16)

                    @block.tensor
                    def _(pe):
                        pe.wait_ge(s_d, 2)
                        nc.tensor.matmul(p[0:NP, 0:1], before[0:NP, 0:NP], cum[:, NT - 1:NT], start=True, stop=True
                                         ).then_inc(s_p, 1)

                        pe.wait_ge(s_d, 18)
                        nc.tensor.matmul(p[0:1, 0:1], at_cut[:], ones[:, 0:1], start=True, stop=True).then_inc(s_p, 1)

                    @block.scalar
                    def _(act):
                        act.wait_ge(s_d, 4)
                        nc.scalar.activation(in_scale[:], in_scale[:], ACT.Sqrt).then_inc(s_a, 1)
                        nc.scalar.activation(out_scale[:], out_scale[:], ACT.Sqrt).then_inc(s_a, 1)

                    @block.vector
                    def _(dve):
                        done = [0]

                        def then(i):
                            i.then_inc(s_d, 1)
                            done[0] += 1
                            dve.wait_ge(s_d, done[0])
                        then(nc.vector.memset(ones[:], 1.0))
                        dve.wait_ge(s_c, 32)
                        then(nc.vector.tensor_tensor_scan(cum[:], ones[:], c2[:, 1, :], 0.0, ALU.mult, ALU.add))
                        then(nc.vector.tensor_scalar(out_scale[:], c2[:, 0, :], 1.0, None, ALU.max))
                        then(nc.vector.tensor_scalar(in_scale[:], c2[:, 1, :], 1.0, None, ALU.max))
                        then(nc.vector.tensor_scalar(has[:], c2[:, 1, :], 1.0, None, ALU.is_ge))
                        dve.wait_ge(s_p, 1)
                        then(nc.vector.tensor_copy(off[:], p[0:NP, 0:1]))
                        then(nc.vector.tensor_scalar(cum[:], cum[:], off[:], None, ALU.add))
                        then(nc.vector.tensor_tensor(first[:], cum[:], c2[:, 1, :], ALU.subtract))
                        then(nc.vector.tensor_scalar(lastf[:], cum[:], -1.0, 0.0, ALU.add, ALU.max))
                        then(nc.vector.tensor_scalar(late[:], lastf[:], float(H), None, ALU.is_ge))
                        then(nc.vector.scalar_tensor_tensor(out=lastf[:], in0=late[:], scalar=float(H - BASE), in1=lastf[:],
                                                            op0=ALU.mult, op1=ALU.add))
                        then(nc.vector.memset(row_at[:], 0))
                        then(nc.vector.memset(first_at[:], 0))
                        then(nc.vector.tensor_copy(row_at[:, 0:NT], lastf[:]))
                        then(nc.vector.tensor_scalar(tmp[:], first[:], float(BASE), None, ALU.is_lt))
                        then(nc.vector.tensor_tensor(cut[:], tmp[:], late[:], ALU.mult))
                        then(nc.vector.scalar_tensor_tensor(out=tmp[:], in0=lastf[:], scalar=-float(H), in1=cut[:],
                                                            op0=ALU.add, op1=ALU.mult))
                        then(nc.vector.tensor_reduce(at_cut[:], tmp[:], AX, ALU.add))
                        dve.wait_ge(s_p, 2)
                        then(nc.vector.tensor_copy(cut_last[:], p[0:1, 0:1]))
                        then(nc.vector.tensor_scalar(none[:], has[:], -1.0, -float(1 << 22), ALU.add, ALU.mult))
                        then(nc.vector.tensor_tensor(none[:], none[:], first[:], ALU.add))
                        then(nc.vector.tensor_copy(first_at[:, 0:NT], none[:]))
                        dve.wait_ge(s_a, 2)
                        then(nc.vector.reciprocal(out_scale[:], out_scale[:]))
                        then(nc.vector.reciprocal(in_scale[:], in_scale[:]))
                        then(nc.vector.tensor_tensor(in_scale[:], in_scale[:], has[:], ALU.mult))
                ctx.clear()

        def node0():
            with Stage() as ctx:
                G = sb("n0_G", [P, NC * NPR * NP], F32, ctx)
                dev = sb("n0_dev", [P, NC * NPR * NP], F32, ctx)
                ag = [sb(f"n0_ag{i}", [NP, CH, F], F32, ctx) for i in range(2)]
                ix = [sb(f"n0_ix{i}", [NP, CH], I32, ctx) for i in range(2)]
                carry = sb("n0_carry", [NP, F], F32, ctx)
                hs = sb("n0_hs", [NP, CH, F], F32, ctx)
                cr = sb("n0_cr", [NP, CH, F], F32, ctx)
                hT = sb("n0_hT", [P, NPR, NP], F32, ctx)
                a1 = sb("n0_a1", [P, NPR, NP], F32, ctx)
                w1, w2 = (sb(f"n0_w{i}", [P, P], F32, ctx) for i in (1, 2))
                b1, b2, gamma, beta = (sb(f"n0_{n}", [P, 1], F32, ctx) for n in ("b1", "b2", "gamma", "beta"))
                total, nmean, ssq, var, rstd, scale, shift, beps = (sb(f"n0_{n}", [P, 1], F32, ctx) for n in (
                    "total", "nmean", "ssq", "var", "rstd", "scale", "shift", "beps"))
                pA, pB = (ps(f"n0_p{n}", [P, 8, P], ctx) for n in "AB")
                s_w, s_wz, s_d, s_p, s_a, begun, s_ix0, s_bn = (ctx.sem(f"n0_{n}") for n in (
                    "weights", "weights_zeroed", "dve", "pe", "act", "gathers_begun", "index0", "bn"))
                got = dma_pair("n0_got")
                ix_ready, used = (ctx.pair(f"n0_{n}") for n in ("ix_ready", "used"))
                D = steps("masked", "plus_h", "carry", "sum")
                PEQ = steps("turned", "lin1", "lin2")
                A = steps("hT", "a1", "g")
                with nc.Block() as block:
                    @block.sync
                    def _(sp):
                        sp.wait_ge(s_wz, 2)
                        blocks_of(sp, w1, w["L0_gnn_W1"], s_w)
                        blocks_of(sp, w2, w["L0_gnn_W2"], s_w)
                        column(sp, b1, w["L0_gnn_b1"], s_w)
                        column(sp, b2, w["L0_gnn_b2"], s_w)
                        column(sp, gamma, w["L0_gnn_bn_gamma"], s_w)
                        column(sp, beta, w["L0_gnn_bn_beta"], s_w)
                        sp.dma_start(carry[:], stream[BASE - 1, :].partition_broadcast(NP)).then_inc(s_w, 16)

                    @block.gpsimd
                    def _(pool):
                        fetch(pool, ag, ix, stream, got, ix_ready, used, begun, pool.to_reg(2 * H - 1))

                    @block.vector
                    def _(dve):
                        nc.vector.memset(w1[:], 0.0).then_inc(s_wz, 1)
                        nc.vector.memset(w2[:], 0.0).then_inc(s_wz, 1)
                        nc.vector.memset(beps[:], BN_EPS).then_inc(s_ix0, 1)
                        nc.vector.tensor_copy(ix[0][:], row_at[:, 0:CH]).then_inc(ix_ready[0], 1)
                        dve.wait_ge(s_w, 208)

                        def one(c, it, par):
                            next_index(dve, c, it, par, ix, got, ix_ready)
                            dve.wait_ge(got[par], 16 * CH * (it + 1))
                            wait_reuse(dve, s_p, c * len(PEQ))
                            nc.vector.tensor_tensor(hs[:], ag[par][:], over_f(chunk(has, c)), ALU.mult).then_inc(s_d, 1)
                            wait_reuse(dve, s_d, at(D, "masked", c))
                            nc.vector.tensor_tensor(hs[:], hs[:], HN[:, bass.ds(c * CH, CH), :], ALU.add).then_inc(s_d, 1)
                            nc.vector.tensor_tensor(cr[:], over_n(carry[:]), over_f(chunk(cut, c)), ALU.mult).then_inc(s_d, 1)
                            wait_reuse(dve, s_d, at(D, "carry", c))
                            nc.vector.tensor_tensor(hs[:], hs[:], cr[:], ALU.add).then_inc(s_d, 1)
                            wait_reuse(dve, s_d, at(D, "sum", c))
                            dve.sem_inc(used[par], 1)
                        chunks(dve, one)

                        dve.wait_ge(s_a, NC * len(A))
                        nc.vector.tensor_reduce(total[:], G[:], AX, ALU.add).then_inc(s_bn, 1)
                        dve.wait_ge(s_bn, 2)
                        nc.vector.tensor_scalar(nmean[:], pA[:, 0, 0:1], -1.0 / N, None, ALU.mult).then_inc(s_bn, 1)
                        dve.wait_ge(s_bn, 5)
                        nc.vector.tensor_scalar(var[:], pA[:, 4, 0:1], 1.0 / N, None, ALU.mult).then_inc(s_bn, 1)
                        dve.wait_ge(s_bn, 7)
                        nc.vector.reciprocal(rstd[:], rstd[:]).then_inc(s_bn, 1)
                        dve.wait_ge(s_bn, 8)
                        nc.vector.tensor_tensor(scale[:], rstd[:], gamma[:], ALU.mult).then_inc(s_bn, 1)
                        dve.wait_ge(s_bn, 9)
                        nc.vector.scalar_tensor_tensor(out=shift[:], in0=nmean[:], scalar=scale[:], in1=beta[:],
                                                       op0=ALU.mult, op1=ALU.add).then_inc(s_bn, 1)
                        dve.wait_ge(s_bn, 10)
                        nc.vector.tensor_scalar(G[:], G[:], scale[:], shift[:], ALU.mult, ALU.add).then_inc(s_bn, 1)

                    @block.tensor
                    def _(pe):
                        pe.wait_ge(s_w, 208)

                        def one(c, it, par):
                            wait_reuse(pe, s_d, at(D, "sum", c))
                            wait_reuse(pe, s_a, c * len(A))
                            turn_nodes(pA, hs).then_inc(s_p, 1)
                            wait_reuse(pe, s_a, at(A, "hT", c))
                            for i in range(NPR):
                                mm = nc.tensor.matmul(pB[:, i, 0:NP], w1[:], hT[:, i, :], start=True, stop=True)
                            mm.then_inc(s_p, 1)
                            wait_reuse(pe, s_a, at(A, "a1", c))
                            for i in range(NPR):
                                mm = nc.tensor.matmul(pA[:, i, 0:NP], w2[:], a1[:, i, :], start=True, stop=True)
                            mm.then_inc(s_p, 1)
                        chunks(pe, one)
                        pe.wait_ge(s_a, NC * len(A))
                        pe.wait_ge(s_bn, 1)
                        nc.tensor.matmul(pA[:, 0, 0:1], halves[:], total[:], start=True, stop=True).then_inc(s_bn, 1)
                        pe.wait_ge(s_bn, 4)
                        nc.tensor.matmul(pA[:, 4, 0:1], halves[:], ssq[:], start=True, stop=True).then_inc(s_bn, 1)

                    @block.scalar
                    def _(act):
                        act.wait_ge(s_w, 208)
                        act.wait_ge(s_ix0, 1)

                        def one(c, it, par):
                            wait_reuse(act, s_p, at(PEQ, "turned", c))
                            nc.scalar.copy(hT[:], pA[:, 0:NPR, 0:NP]).then_inc(s_a, 1)
                            wait_reuse(act, s_p, at(PEQ, "lin1", c))
                            nc.scalar.activation(a1[:], pB[:, 0:NPR, 0:NP], ACT.Relu, bias=b1[:]).then_inc(s_a, 1)
                            wait_reuse(act, s_p, at(PEQ, "lin2", c))
                            nc.scalar.activation(G[:, bass.ds(c * NPR * NP, NPR * NP)].rearrange("p (i n) -> p i n", i=NPR),
                                                 pA[:, 0:NPR, 0:NP], ACT.Relu, bias=b2[:]).then_inc(s_a, 1)
                        chunks(act, one)
                        act.wait_ge(s_bn, 3)
                        nc.scalar.activation(dev[:], G[:], ACT.Square, bias=nmean[:], accum_out=ssq[:]).then_inc(s_bn, 1)
                        act.wait_ge(s_bn, 6)
                        nc.scalar.activation(rstd[:], var[:], ACT.Sqrt, bias=beps[:]).then_inc(s_bn, 1)

                xs = sb("n0_xs", [NP, CH, F], F32, ctx)
                wa, wb = (sb(f"n0_w{i}", [P, P], F32, ctx) for i in "ab")
                ownb = sb("n0_ownb", [NP, F], F32, ctx)
                ln = Normed(ctx, "n0")
                own = [sb(f"n0_own{i}", [NP, CH, F], F32, ctx) for i in range(2)]
                tab = [sb(f"n0_tab{i}", [NP, CH, F], F32, ctx) for i in range(2)]
                fx = [sb(f"n0_fx{i}", [NP, CH], I32, ctx) for i in range(2)]
                s_w, s_wz, s_d, s_p, s_a, begun, std = (ctx.sem(f"n0b_{n}") for n in (
                    "weights", "weights_zeroed", "dve", "pe", "act", "scatters_begun", "roots"))
                stored, scattered = ctx.pair("n0b_stored"), dma_pair("n0b_scattered")
                storing = ctx.sem("n0b_stores_begun")
                DB = steps("g", "xs", "x", *Normed.names, "index", "own")
                PB = steps("back", "turned", "lin")
                AB = steps("hT", "tab")
                with nc.Block() as block:
                    @block.sync
                    def _(sp):
                        sp.wait_ge(s_wz, 2)
                        blocks_of(sp, wa, w["L1_gnn_W1"][0:F, :], s_w)
                        blocks_of(sp, wb, w["L1_gnn_W1"][F:2 * F, :], s_w)
                        sp.dma_start(ownb[:], w["L1_gnn_b1"].partition_broadcast(NP)).then_inc(s_w, 16)

                        def one(c, it, par):
                            t_at = c * CH if isinstance(c, int) else sp.snap(c * CH)
                            wait_reuse(sp, s_d, at(DB, "own", c))
                            wait_reuse(sp, s_a, at(AB, "tab", c))
                            sp.sem_inc(storing, 1)
                            sp.dma_start(node_view(own_d)[:, bass.ds(t_at, CH), :], own[par][:]).then_inc(stored[par], 16)
                            sp.dma_start(node_view(table1)[:, bass.ds(t_at, CH), :], tab[par][:]).then_inc(stored[par], 16)
                        chunks(sp, one)
                        sp.wait_ge(stored[0], 32 * (NC // 2))
                        sp.wait_ge(stored[1], 32 * (NC // 2))

                    @block.gpsimd
                    def _(pool):
                        top = pool.to_reg(E - 1)

                        def one(c, it, par):
                            wait_reuse(pool, s_d, at(DB, "own", c))
                            pool.sem_inc(begun, 1)
                            for t in range(CH):
                                nc.gpsimd.indirect_dma_start(own_at_start, IND(ap=fx[par][:, t:t + 1], axis=0), own[par][:, t, :],
                                                             None, bounds_check=top, oob_is_err=False
                                                             ).then_inc(scattered[par], 16)
                        chunks(pool, one)
                        pool.wait_ge(scattered[0], 16 * CH * (NC // 2))
                        pool.wait_ge(scattered[1], 16 * CH * (NC // 2))

                    @block.vector
                    def _(dve):
                        nc.vector.memset(wa[:], 0.0).then_inc(s_wz, 1)
                        nc.vector.memset(wb[:], 0.0).then_inc(s_wz, 1)
                        dve.wait_ge(s_w, 80)
                        nc.vector.tensor_tensor(wa[:], wa[:], wb[:], ALU.subtract).then_inc(s_wz, 1)

                        def one(c, it, par):
                            wait_reuse(dve, s_p, c * len(PB))
                            same_values(hT[:], G[:, bass.ds(c * NPR * NP, NPR * NP)].rearrange("p (i n) -> p i n", i=NPR)
                                                  ).then_inc(s_d, 1)
                            wait_reuse(dve, s_p, at(PB, "back", c))
                            nc.vector.tensor_tensor(xs[:], X[:, bass.ds(c * CH, CH), :],
                                                    pA[0:NP, 0:NPR, :].rearrange("p i (a f) -> p (i a) f", a=2), ALU.add
                                                    ).then_inc(s_d, 1)
                            wait_reuse(dve, s_d, at(DB, "xs", c))
                            same_values(X[:, bass.ds(c * CH, CH), :], xs[:]).then_inc(s_d, 1)
                            ln.vector(dve, xs[:], hs[:], s_d, DB, std, c, lambda: None)
                            wait_reuse(dve, scattered[par], 16 * CH * it)
                            wait_reuse(dve, stored[par], 32 * it)
                            same_values(fx[par][:], chunk(first_at, c)).then_inc(s_d, 1)
                            wait_reuse(dve, s_p, at(PB, "lin", c))
                            nc.vector.tensor_tensor(own[par][:], pA[0:NP, 0:NPR, :].rearrange("p i (a f) -> p (i a) f", a=2),
                                                    over_n(ownb[:]), ALU.add).then_inc(s_d, 1)
                        chunks(dve, one)

                    @block.tensor
                    def _(pe):
                        pe.wait_ge(s_wz, 3)

                        def one(c, it, par):
                            wait_reuse(pe, s_d, at(DB, "g", c))
                            wait_reuse(pe, s_a, c * len(AB))
                            for i in range(NPR):
                                mm = nc.tensor.transpose(pA[0:NP, i, :], hT[:, i, :], ident[:])
                            mm.then_inc(s_p, 1)
                            wait_reuse(pe, s_d, at(DB, "h", c))
                            turn_nodes(pB, hs).then_inc(s_p, 1)
                            wait_reuse(pe, s_a, at(AB, "hT", c))
                            for i in range(NPR):
                                nc.tensor.matmul(pA[0:NP, i, :], a1[:, i, :], wa[:], start=True, stop=True)
                            for i in range(NPR):
                                mm = nc.tensor.matmul(pB[0:NP, i, :], a1[:, i, :], wb[:], start=True, stop=True)
                            mm.then_inc(s_p, 1)
                        chunks(pe, one)

                    @block.scalar
                    def _(act):
                        def one(c, it, par):
                            ln.scalar(act, s_d, DB, std, c)
                            wait_reuse(act, s_p, at(PB, "turned", c))
                            nc.scalar.copy(a1[:], pB[:, 0:NPR, 0:NP]).then_inc(s_a, 1)
                            wait_reuse(act, s_p, at(PB, "lin", c))
                            wait_reuse(act, stored[par], 32 * it)
                            nc.scalar.copy(tab[par][:], pB[0:NP, 0:NPR, :].rearrange("p i (a f) -> p (i a) f", a=2)
                                           ).then_inc(s_a, 1)
                        chunks(act, one)
                ctx.clear()

        def node12(layer):
            tag = f"n{layer}"
            with Stage() as ctx:
                ag = [sb(f"{tag}_ag{i}", [NP, CH, F], F32, ctx) for i in range(2)]
                ix = [sb(f"{tag}_ix{i}", [NP, CH], I32, ctx) for i in range(2)]
                carry = sb(f"{tag}_carry", [NP, F], F32, ctx)
                cr = sb(f"{tag}_cr", [NP, CH, F], F32, ctx)
                pen = sb(f"{tag}_pen", [NP, NT], F32, ctx)
                xs = sb(f"{tag}_xs", [NP, CH, F], F32, ctx)
                hs = sb(f"{tag}_hs", [NP, CH, F], F32, ctx)
                hT = sb(f"{tag}_hT", [P, NPR, NP], F32, ctx)
                tab = [sb(f"{tag}_tab{i}", [NP, CH, F], F32, ctx) for i in range(2)]
                wt = sb(f"{tag}_wt", [P, P], F32, ctx)
                br, b2r = (sb(f"{tag}_{n}", [NP, F], F32, ctx) for n in ("br", "b2r"))
                ln = Normed(ctx, tag)
                pA, pB = (ps(f"{tag}_p{n}", [P, 8, P], ctx) for n in "AB")
                s_w, s_wz, s_pen, s_d, s_p, s_a, begun, std, storing = (ctx.sem(f"{tag}_{n}") for n in (
                    "weights", "weights_zeroed", "penalty", "dve", "pe", "act", "gathers_begun", "roots", "stores_begun"))
                got = dma_pair(f"{tag}_got")
                ix_ready, used, stored = (ctx.pair(f"{tag}_{n}") for n in ("ix_ready", "used", "stored"))
                if layer == 1:
                    D = steps("carry", "less", "max", "bias", "masked", "xs", "x", *Normed.names, "lin_b", "tab")
                else:
                    D = steps("carry", "sum", "scaled", "xs", "x", *Normed.names, "tab")
                PEQ = steps("turned", "lin")
                A = steps("hT")
                with nc.Block() as block:
                    @block.sync
                    def _(sp):
                        sp.dma_start(carry[:], stream[BASE - 1, :].partition_broadcast(NP)).then_inc(s_w, 16)
                        sp.dma_start(br[:], w["L2_gnn_b"].partition_broadcast(NP)).then_inc(s_w, 16)
                        sp.dma_start(b2r[:], w["L1_gnn_b2"].partition_broadcast(NP)).then_inc(s_w, 16)
                        sp.wait_ge(s_wz, 1)
                        blocks_of(sp, wt, w["L2_gnn_W"], s_w)

                        def one(c, it, par):
                            t_at = c * CH if isinstance(c, int) else sp.snap(c * CH)
                            wait_reuse(sp, s_d, at(D, "tab", c))
                            sp.sem_inc(storing, 1)
                            sp.dma_start(node_view(table2 if layer == 1 else table3)[:, bass.ds(t_at, CH), :], tab[par][:]
                                         ).then_inc(stored[par], 16)
                        chunks(sp, one)
                        sp.wait_ge(stored[0], 16 * (NC // 2))
                        sp.wait_ge(stored[1], 16 * (NC // 2))

                    @block.gpsimd
                    def _(pool):
                        fetch(pool, ag, ix, stream, got, ix_ready, used, begun, pool.to_reg(2 * H - 1))

                    @block.vector
                    def _(dve):
                        nc.vector.memset(wt[:], 0.0).then_inc(s_wz, 1)
                        nc.vector.tensor_scalar(pen[:], cut[:], -1.0, BIG, ALU.add, ALU.mult).then_inc(s_pen, 1)
                        nc.vector.tensor_copy(ix[0][:], row_at[:, 0:CH]).then_inc(ix_ready[0], 1)
                        dve.wait_ge(s_w, 80)
                        dve.wait_ge(s_pen, 1)

                        def one(c, it, par):
                            next_index(dve, c, it, par, ix, got, ix_ready)
                            dve.wait_ge(got[par], 16 * CH * (it + 1))

                            def step(name, i):
                                i.then_inc(s_d, 1)
                                wait_reuse(dve, s_d, at(D, name, c))
                            step("carry", nc.vector.tensor_tensor(cr[:], over_n(carry[:]), over_f(chunk(cut, c)), ALU.mult))
                            if layer == 1:
                                step("less", nc.vector.tensor_tensor(cr[:], cr[:], over_f(chunk(pen, c)), ALU.add))
                                step("max", nc.vector.tensor_tensor(cr[:], cr[:], ag[par][:], ALU.max))
                                step("bias", nc.vector.tensor_tensor(cr[:], cr[:], over_n(b2r[:]), ALU.add))
                                step("masked", nc.vector.tensor_tensor(cr[:], cr[:], over_f(chunk(has, c)), ALU.mult))
                            else:
                                step("sum", nc.vector.tensor_tensor(cr[:], cr[:], ag[par][:], ALU.add))
                                step("scaled", nc.vector.tensor_tensor(cr[:], cr[:], over_f(chunk(in_scale, c)), ALU.mult))
                            step("xs", nc.vector.tensor_tensor(xs[:], X[:, bass.ds(c * CH, CH), :], cr[:], ALU.add))
                            dve.sem_inc(used[par], 1)
                            same_values(X[:, bass.ds(c * CH, CH), :], xs[:]).then_inc(s_d, 1)
                            if layer == 1:
                                ln.vector(dve, xs[:], hs[:], s_d, D, std, c, lambda: None)
                                wait_reuse(dve, stored[par], 16 * it)
                                wait_reuse(dve, s_p, at(PEQ, "lin", c))
                                step("lin_b", nc.vector.tensor_tensor(
                                    tab[par][:], pB[0:NP, 0:NPR, :].rearrange("p i (a f) -> p (i a) f", a=2), over_n(br[:]), ALU.add))
                                nc.vector.tensor_tensor(tab[par][:], tab[par][:], over_f(chunk(out_scale, c)), ALU.mult
                                                        ).then_inc(s_d, 1)
                            else:
                                ln.vector(dve, xs[:], hs[:], s_d, D, std, c, lambda: None)
                                wait_reuse(dve, s_d, at(D, "h", c))
                                wait_reuse(dve, stored[par], 16 * it)
                                same_values(HN[:, bass.ds(c * CH, CH), :], hs[:])
                                nc.vector.tensor_copy(tab[par][:], hs[:]).then_inc(s_d, 1)
                        chunks(dve, one)

                    @block.scalar
                    def _(act):
                        def one(c, it, par):
                            ln.scalar(act, s_d, D, std, c)
                            if layer == 1:
                                wait_reuse(act, s_p, at(PEQ, "turned", c))
                                nc.scalar.copy(hT[:], pA[:, 0:NPR, 0:NP]).then_inc(s_a, 1)
                        chunks(act, one)

                    if layer == 1:
                        @block.tensor
                        def _(pe):
                            pe.wait_ge(s_w, 80)

                            def one(c, it, par):
                                wait_reuse(pe, s_d, at(D, "h", c))
                                wait_reuse(pe, s_a, c * len(A))
                                turn_nodes(pA, hs).then_inc(s_p, 1)
                                wait_reuse(pe, s_a, at(A, "hT", c))
                                for i in range(NPR):
                                    mm = nc.tensor.matmul(pB[0:NP, i, :], hT[:, i, :], wt[:], start=True, stop=True)
                                mm.then_inc(s_p, 1)
                            chunks(pe, one)
                ctx.clear()

        def node3():
            with Stage() as ctx:
                G = sb("n3_G", [P, NC * CH * NP], F32, ctx)
                ag = [sb(f"n3_ag{i}", [NP, CH, 2 * F], F32, ctx) for i in range(2)]
                ix = [sb(f"n3_ix{i}", [NP, CH], I32, ctx) for i in range(2)]
                carry = sb("n3_carry", [NP, 2 * F], F32, ctx)
                top0, top1, top01, w0, w1_ = (sb(f"n3_{n}", [NP, F], F32, ctx) for n in ("top0", "top1", "top01", "wt0", "wt1"))
                whole = sb("n3_whole", [NP, NT], F32, ctx)
                mc, mx, wc, wo, t1 = (sb(f"n3_{n}", [NP, CH, F], F32, ctx) for n in ("mc", "mx", "wc", "wo", "t1"))
                hT = sb("n3_hT", [P, NPR, NP], F32, ctx)
                w1 = sb("n3_w1", [P, 2, P], F32, ctx)
                w2 = sb("n3_w2", [P, F], F32, ctx)
                b1, gamma, beta, total, nmean, ssq, ssq2, var, rstd, scale, shift, beps = (sb(f"n3_{n}", [P, 1], F32, ctx) for n in (
                    "b1", "gamma", "beta", "total", "nmean", "ssq", "ssq2", "var", "rstd", "scale", "shift", "beps"))
                b2r = sb("n3_b2r", [NP, F], F32, ctx)
                lscale = sb("n3_lscale", [NP, 1], F32, ctx)
                hsq, fsq = (sb(f"n3_{n}", [NP, CH], F32, ctx) for n in ("hsq", "fsq"))
                dev = sb("n3_dev", [P, CH * NP], F32, ctx)
                act2 = sb("n3_act2", [P, CH, NP], F32, ctx)
                ot = [sb(f"n3_ot{i}", [NP, CH, F], F32, ctx) for i in range(2)]
                pA = ps("n3_pA", [P, 8, P], ctx)
                pB = ps("n3_pB", [P, 12, P], ctx)
                pO = ps("n3_pO", [P, 16, F], ctx)
                s_w, s_wz, s_set, s_d, s_p, s_a, begun, s_bn, s_d2, s_p2, s_a2, storing = (ctx.sem(f"n3_{n}") for n in (
                    "weights", "weights_zeroed", "set", "dve", "pe", "act", "gathers_begun", "bn", "dve2", "pe2", "act2",
                    "stores_begun"))
                got = dma_pair(f"n3_got")
                ix_ready, used, stored = (ctx.pair(f"n3_{n}") for n in ("ix_ready", "used", "stored"))
                D = steps("w_cut", "w", "den_c", "den_o", "den", "num_c", "num_o", "num",
                          "rden", "h", "h_eps", "h_masked", "hh", "hsq", "ff", "fsq", "hmax", "hrec", "coef", "coef_s", "scaled", "y")
                PEQ = steps("turned", "lin1")
                A = steps("hroot", "froot", "hT", "g")
                with nc.Block() as block:
                    @block.sync
                    def _(sp):
                        sp.wait_ge(s_wz, 1)
                        for k in range(2):
                            sp.dma_start(w1[k * F:(k + 1) * F, k, :], w["L3_gnn_W1"]).then_inc(s_w, 16)
                        sp.dma_start(w2[:], w["L3_gnn_W2"]).then_inc(s_w, 16)
                        for col, v in ((b1, "L3_gnn_b1"), (gamma, "L3_gnn_gamma"), (beta, "L3_gnn_bn_beta")):
                            sp.dma_start(col[:], w[v].rearrange("(f o) -> f o", o=1)).then_inc(s_w, 16)
                        sp.dma_start(b2r[:], w["L3_gnn_b2"].partition_broadcast(NP)).then_inc(s_w, 16)
                        sp.dma_start(lscale[:], w["L3_gnn_scale"].partition_broadcast(NP)).then_inc(s_w, 16)
                        sp.dma_start(carry[:], stream3[BASE - 1, :].partition_broadcast(NP)).then_inc(s_w, 16)
                        sp.dma_start(top0[:], maxes[0:F, BASE - 1].partition_broadcast(NP), allow_slow_non_contiguous=True
                                     ).then_inc(s_w, 16)
                        edge = sp.value_load(cut_last[0:1, 0:1], min_val=0, max_val=H - 1)
                        sp.dma_start(top1[:], maxes[F:P, bass.ds(edge, 1)].rearrange("f o -> (f o)").partition_broadcast(NP),
                                     allow_slow_non_contiguous=True).then_inc(s_w, 16)

                        def one(c, it, par):
                            t_at = c * CH if isinstance(c, int) else sp.snap(c * CH)
                            sp.wait_ge(s_d2, 2 * (c + 1))
                            sp.sem_inc(storing, 1)
                            sp.dma_start(node_view(out)[:, bass.ds(t_at, CH), :], ot[par][:]).then_inc(stored[par], 16)
                        chunks(sp, one)
                        sp.wait_ge(stored[0], 16 * (NC // 2))
                        sp.wait_ge(stored[1], 16 * (NC // 2))

                    @block.gpsimd
                    def _(pool):
                        fetch(pool, ag, ix, stream3, got, ix_ready, used, begun, pool.to_reg(2 * H - 1))

                    @block.vector
                    def _(dve):
                        nc.vector.memset(w1[:], 0.0).then_inc(s_wz, 1)
                        nc.vector.memset(beps[:], BN_EPS).then_inc(s_set, 1)
                        nc.vector.tensor_scalar(whole[:], cut[:], -1.0, 1.0, ALU.mult, ALU.add).then_inc(s_set, 1)
                        nc.vector.tensor_copy(ix[0][:], row_at[:, 0:CH]).then_inc(ix_ready[0], 1)
                        dve.wait_ge(s_w, 176)
                        nc.vector.tensor_tensor(top01[:], top0[:], top1[:], ALU.max).then_inc(s_set, 1)
                        dve.wait_ge(s_set, 3)
                        nc.vector.tensor_tensor(w0[:], top0[:], top01[:], ALU.subtract).then_inc(s_set, 1)
                        nc.vector.tensor_tensor(w1_[:], top1[:], top01[:], ALU.subtract).then_inc(s_set, 1)
                        dve.wait_ge(s_set, 7)
                        nc.vector.tensor_tensor(carry[:, 0:F], carry[:, 0:F], w0[:], ALU.mult).then_inc(s_set, 1)
                        nc.vector.tensor_tensor(carry[:, F:2 * F], carry[:, F:2 * F], w0[:], ALU.mult).then_inc(s_set, 1)
                        dve.wait_ge(s_set, 9)

                        def one(c, it, par):
                            next_index(dve, c, it, par, ix, got, ix_ready)
                            dve.wait_ge(got[par], 16 * CH * (it + 1))
                            num, den = (ag[par][:, :, k * F:(k + 1) * F] for k in range(2))
                            cnum, cden = (over_n(carry[:, k * F:(k + 1) * F]) for k in range(2))
                            hn = HN[:, bass.ds(c * CH, CH), :]
                            tt = nc.vector.tensor_tensor

                            def step(name, i):
                                i.then_inc(s_d, 1)
                                wait_reuse(dve, s_d, at(D, name, c))
                            step("w_cut", tt(wo[:], over_n(w1_[:]), over_f(chunk(cut, c)), ALU.mult))
                            step("w", tt(wo[:], wo[:], over_f(chunk(whole, c)), ALU.add))
                            step("den_c", tt(mc[:], cden, over_f(chunk(cut, c)), ALU.mult))
                            step("den_o", tt(mx[:], den, wo[:], ALU.mult))
                            step("den", tt(mx[:], mx[:], mc[:], ALU.add))
                            step("num_c", tt(wc[:], cnum, over_f(chunk(cut, c)), ALU.mult))
                            step("num_o", tt(wo[:], num, wo[:], ALU.mult))
                            step("num", tt(wo[:], wo[:], wc[:], ALU.add))
                            dve.sem_inc(used[par], 1)
                            step("rden", nc.vector.reciprocal(mx[:], mx[:]))
                            step("h", tt(wo[:], wo[:], mx[:], ALU.mult))
                            step("h_eps", nc.vector.tensor_scalar(wo[:], wo[:], SM_EPS, None, ALU.add))
                            step("h_masked", tt(wo[:], wo[:], over_f(chunk(has, c)), ALU.mult))
                            step("hh", tt(wc[:], wo[:], wo[:], ALU.mult))
                            step("hsq", nc.vector.tensor_reduce(hsq[:], wc[:], AX, ALU.add))
                            step("ff", tt(wc[:], hn, hn, ALU.mult))
                            step("fsq", nc.vector.tensor_reduce(fsq[:], wc[:], AX, ALU.add))
                            wait_reuse(dve, s_a, at(A, "froot", c))
                            step("hmax", nc.vector.tensor_scalar(hsq[:], hsq[:], NORM_EPS, None, ALU.max))
                            step("hrec", nc.vector.reciprocal(hsq[:], hsq[:]))
                            step("coef", tt(hsq[:], hsq[:], fsq[:], ALU.mult))
                            step("coef_s", nc.vector.tensor_scalar(hsq[:], hsq[:], lscale[:], None, ALU.mult))
                            step("scaled", tt(wo[:], wo[:], over_f(hsq[:]), ALU.mult))
                            wait_reuse(dve, s_p, c * len(PEQ))
                            step("y", tt(t1[:], wo[:], hn, ALU.add))
                        chunks(dve, one)

                        dve.wait_ge(s_a, NC * len(A))
                        nc.vector.tensor_reduce(total[:], G[:], AX, ALU.add).then_inc(s_bn, 1)
                        dve.wait_ge(s_bn, 1)
                        nc.vector.tensor_scalar(nmean[:], total[:], -1.0 / N, None, ALU.mult).then_inc(s_bn, 1)
                        nc.vector.memset(ssq[:], 0.0).then_inc(s_bn, 1)
                        dve.wait_ge(s_bn, 3)
                        for c in range(NC):
                            dve.wait_ge(s_a2, c + 1)
                            nc.vector.tensor_tensor(ssq[:], ssq[:], ssq2[:], ALU.add).then_inc(s_bn, 1)
                            dve.wait_ge(s_bn, 4 + c)
                        nc.vector.tensor_scalar(var[:], ssq[:], 1.0 / N, None, ALU.mult).then_inc(s_bn, 1)
                        dve.wait_ge(s_a2, NC + 1)
                        nc.vector.reciprocal(rstd[:], rstd[:]).then_inc(s_bn, 1)
                        dve.wait_ge(s_bn, NC + 5)
                        nc.vector.tensor_tensor(scale[:], rstd[:], gamma[:], ALU.mult).then_inc(s_bn, 1)
                        dve.wait_ge(s_bn, NC + 6)
                        nc.vector.scalar_tensor_tensor(out=shift[:], in0=nmean[:], scalar=scale[:], in1=beta[:],
                                                       op0=ALU.mult, op1=ALU.add).then_inc(s_bn, 1)

                        def last(c, it, par):
                            dve.wait_ge(s_p2, c + 1)
                            wait_reuse(dve, stored[par], 16 * it)
                            nc.vector.tensor_tensor(ot[par][:], pO[0:NP, 0:CH, :], over_n(b2r[:]), ALU.add).then_inc(s_d2, 1)
                            dve.wait_ge(s_d2, 2 * c + 1)
                            nc.vector.tensor_tensor(ot[par][:], ot[par][:], X[:, bass.ds(c * CH, CH), :], ALU.add).then_inc(s_d2, 1)
                        chunks(dve, last)

                    @block.scalar
                    def _(act):
                        act.wait_ge(s_w, 176)
                        act.wait_ge(s_set, 5)
                        nc.scalar.activation(w0[:], w0[:], ACT.Exp).then_inc(s_set, 1)
                        nc.scalar.activation(w1_[:], w1_[:], ACT.Exp).then_inc(s_set, 1)

                        def one(c, it, par):
                            wait_reuse(act, s_d, at(D, "fsq", c))
                            nc.scalar.activation(hsq[:], hsq[:], ACT.Sqrt).then_inc(s_a, 1)
                            nc.scalar.activation(fsq[:], fsq[:], ACT.Sqrt).then_inc(s_a, 1)
                            wait_reuse(act, s_p, at(PEQ, "turned", c))
                            nc.scalar.copy(hT[:], pA[:, 0:NPR, 0:NP]).then_inc(s_a, 1)
                            wait_reuse(act, s_p, at(PEQ, "lin1", c))
                            nc.scalar.activation(G[:, bass.ds(c * CH * NP, CH * NP)].rearrange("p (i n) -> p i n", i=CH),
                                                 pB[:, 0:CH, 0:NP], ACT.Identity, bias=b1[:]).then_inc(s_a, 1)
                        chunks(act, one)
                        act.wait_ge(s_bn, 3)
                        for c in range(NC):
                            act.wait_ge(s_bn, 3 + c)
                            nc.scalar.activation(dev[:], G[:, c * CH * NP:(c + 1) * CH * NP], ACT.Square, bias=nmean[:],
                                                 accum_out=ssq2[:]).then_inc(s_a2, 1)
                        act.wait_ge(s_bn, NC + 4)
                        nc.scalar.activation(rstd[:], var[:], ACT.Sqrt, bias=beps[:]).then_inc(s_a2, 1)
                        act.wait_ge(s_bn, NC + 7)

                        def last(c, it, par):
                            wait_reuse(act, s_p2, c)
                            nc.scalar.activation(act2[:].rearrange("p i n -> p (i n)"), G[:, bass.ds(c * CH * NP, CH * NP)], ACT.Relu,
                                                 bias=shift[:], scale=scale[:]).then_inc(s_a2, 1)
                        chunks(act, last)

                    @block.tensor
                    def _(pe):
                        pe.wait_ge(s_w, 176)

                        def one(c, it, par):
                            wait_reuse(pe, s_d, at(D, "y", c))
                            wait_reuse(pe, s_a, c * len(A))
                            turn_nodes(pA, t1).then_inc(s_p, 1)
                            wait_reuse(pe, s_a, at(A, "hT", c))
                            for t in range(CH):
                                mm = nc.tensor.matmul(pB[:, t, 0:NP], w1[:, t % 2, :], hT[:, t // 2, :], start=True, stop=True)
                            mm.then_inc(s_p, 1)
                        chunks(pe, one)

                        def last(c, it, par):
                            pe.wait_ge(s_a2, NC + 2 + c)
                            wait_reuse(pe, s_d2, 2 * c)
                            for t in range(CH):
                                mm = nc.tensor.matmul(pO[0:NP, t, :], act2[:, t, :], w2[:], start=True, stop=True)
                            mm.then_inc(s_p2, 1)
                        chunks(pe, last)
                ctx.clear()

        edge0()
        runs()
        node0()
        edge1()
        node12(1)
        edge2()
        node12(2)
        edge3()
        node3()


WEIGHTS = ["L0_gnn_W_edge", "L0_gnn_b_edge", "L0_gnn_W1", "L0_gnn_b1", "L0_gnn_W2", "L0_gnn_b2", "L0_gnn_bn_gamma",
           "L0_gnn_bn_beta", "L1_gnn_W1", "L1_gnn_b1", "L1_gnn_W2", "L1_gnn_b2", "L2_gnn_W", "L2_gnn_b", "L3_gnn_W1",
           "L3_gnn_b1", "L3_gnn_gamma", "L3_gnn_bn_beta", "L3_gnn_W2", "L3_gnn_b2", "L3_gnn_scale"]


def layout(inputs):
    import numpy as np
    a = {"in_" + k: np.ascontiguousarray(v) for k, v in inputs.items()}
    a["in_L2_gnn_W"] = np.ascontiguousarray(a["in_L2_gnn_W"].T)
    return a


def program(nc, a):
    gnn_kernel(nc, a["in_x"], a["in_src"], a["in_dst"], a["in_edge_attr_10"], a["in_edge_attr_64"],
               {k: a["in_" + k] for k in WEIGHTS}, a["out"])


def kernel(**inputs):
    import concourse.bacc as bacc
    from concourse.bass_utils import run_bass_kernel_spmd

    nc = bacc.Bacc("TRN2", target_bir_lowering=False, num_devices=1)
    arrays = layout(inputs)
    aps = {k: nc.dram_tensor(k, v.shape, mybir.dt.from_np(v.dtype), kind="ExternalInput").ap() for k, v in arrays.items()}
    aps["out"] = nc.dram_tensor("out", arrays["in_x"].shape, F32, kind="ExternalOutput").ap()
    program(nc, aps)
    r = run_bass_kernel_spmd(nc, [arrays], core_ids=[0])
    return r.results[0]["out"]
```

```python
from contextlib import ExitStack

import concourse.bass as bass
from concourse import mybir

ALU = mybir.AluOpType
ACT = mybir.ActivationFunctionType
F32 = mybir.dt.float32
BF16 = mybir.dt.bfloat16
I32 = mybir.dt.int32
AX = mybir.AxisListType.X

F = 64
P = 128
NP = 125
CH = 10
NPR = CH // 2
T = 8
BK = P * T
Q = T // 4
PIECES = 5
PIECE = CH * NP // PIECES
D10 = 10
BIG = 1e30
LN_EPS = 1e-5
BN_EPS = 1e-5
SM_EPS = 1e-7
NORM_EPS = 1e-12
IND = bass.IndirectOffsetOnAxis


def wait_reuse(eng, sem, value):
    if not (isinstance(value, int) and value <= 0):
        eng.wait_ge(sem, value)


def steps(*names):
    return {n: i + 1 for i, n in enumerate(names)}


def at(seq, name, rnd):
    return rnd * len(seq) + seq[name]


def gnn_kernel(nc, x, src, dst, ea10, ea64, w, out):
    N = x.shape[0]
    E = src.shape[0]
    NT = N // NP
    NC = NT // CH
    NB = -(-E // (2 * BK))
    NB += NB % 2
    NIT = NB // 2
    H = NB * BK
    BASE = E - H
    OVER = 2 * H - E
    HB = -(-N // P)
    assert N % (NP * CH) == 0 and E % P == 0 and HB <= P and 0 < BASE < E and OVER > 0 and OVER % P == 0
    OT = OVER // P

    def dram(name, shape, dt):
        return nc.dram_tensor(name, shape, dt, kind="Internal").ap()

    same_d = dram("same_d", (E,), BF16)
    reset_d = dram("reset_d", (E,), BF16)
    table0 = dram("table0", (N, F), F32)
    table1 = dram("table1", (N, F), F32)
    table2 = dram("table2", (N, F), F32)
    table3 = dram("table3", (N, F), F32)
    own_d = dram("own_d", (N, F), F32)
    own_at_start = dram("own_at_start", (2 * H, F), F32)
    stream = dram("stream", (2 * H, F), F32)
    stream3 = dram("stream3", (2 * H, 2 * F), F32)
    maxes = dram("maxes", (P, H), F32)
    count_d = dram("count_d", (2, HB * P), F32)

    def node_view(t):
        return t.rearrange("(p t) f -> p t f", p=NP)

    def edges_of(half, b):
        return b * BK + (BASE if half else 0)

    root = ExitStack()
    with root:
        class Stage(ExitStack):

            def __init__(self):
                super().__init__()
                self.sems = []

            def sem(self, name):
                self.sems.append(self.enter_context(nc.semaphore(name)))
                return self.sems[-1]

            def pair(self, name):
                return [self.sem(f"{name}{i}") for i in range(2)]

            def clear(self):
                with nc.Block() as block:
                    @block.gpsimd
                    def _(pool):
                        for s in self.sems:
                            pool.sem_clear(s)

        def sb(name, shape, dt=F32, ctx=root):
            return ctx.enter_context(nc.sbuf_tensor(name, shape, dt))

        def ps(name, shape, ctx):
            return ctx.enter_context(nc.psum_tensor(name, shape, F32))

        def dma_pair(name):
            return [root.enter_context(nc.semaphore(f"{name}{i}")) for i in range(2)]

        X = sb("X", [NP, NT, F])
        HN = sb("HN", [NP, NT, F])
        ident = sb("ident", [P, P])
        halves = sb("halves", [P, P])
        before = sb("before", [P, P])
        iota = sb("iota", [P, P])
        row_at = sb("row_at", [NP, NT + CH], I32)
        first_at = sb("first_at", [NP, NT + CH], I32)
        has = sb("has", [NP, NT])
        cut = sb("cut", [NP, NT])
        cut_last = sb("cut_last", [1, 1], I32)
        in_scale = sb("in_scale", [NP, NT])
        out_scale = sb("out_scale", [NP, NT])
        eps = sb("eps", [P, 1])

        with Stage() as ctx:
            W = E // P
            d_cur = sb("d_cur", [P, W + 1], I32, ctx)
            m_same = sb("m_same", [P, W], BF16, ctx)
            m_reset = sb("m_reset", [P, W], BF16, ctx)
            mean = sb("mean", [NP, NT], F32, ctx)
            var = sb("var", [NP, NT], F32, ctx)
            rstd = sb("rstd", [NP, NT], F32, ctx)
            sq = sb("sq", [NP, NT, F], F32, ctx)
            s_x, s_dst, s_first, s_dve, s_std, s_out, s_const = (
                ctx.sem(n) for n in ("setup_x", "setup_dst", "setup_first", "setup_dve", "setup_std", "setup_out", "setup_const"))
            SD = steps("eps", "same", "reset", "mean", "mean_s", "centred", "square", "var", "var_s", "rstd", "h")
            with nc.Block() as block:
                @block.sync
                def _(sp):
                    sp.dma_start(X[:], node_view(x)).then_inc(s_x, 16)
                    dv = dst.rearrange("(p i) -> p i", p=P)
                    sp.dma_start(d_cur[:, 1:W + 1], dv).then_inc(s_dst, 16)
                    sp.dma_start(d_cur[1:P, 0:1], dv[0:P - 1, W - 1:W], allow_slow_non_contiguous=True).then_inc(s_dst, 16)
                    sp.wait_ge(s_dve, SD["same"])
                    sp.dma_start(same_d.rearrange("(p i) -> p i", p=P), m_same[:]).then_inc(s_out, 16)
                    sp.wait_ge(s_dve, SD["reset"])
                    sp.dma_start(reset_d.rearrange("(p i) -> p i", p=P), m_reset[:]).then_inc(s_out, 16)
                    sp.wait_ge(s_dve, SD["h"])
                    sp.dma_start(node_view(table0), HN[:]).then_inc(s_out, 16)
                    sp.wait_ge(s_out, 48)

                @block.gpsimd
                def _(pool):
                    nc.gpsimd.memset(d_cur[0:1, 0:1], -1).then_inc(s_first, 1)
                    nc.gpsimd.memset(ident[:], 0.0).then_inc(s_const, 1)
                    nc.gpsimd.memset(halves[:], 0.0).then_inc(s_const, 1)
                    nc.gpsimd.memset(before[:], 1.0).then_inc(s_const, 1)
                    nc.gpsimd.iota(iota[:], pattern=[[1, P]], base=0, channel_multiplier=0,
                                   allow_small_or_imprecise_dtypes=True).then_inc(s_const, 1)
                    pool.wait_ge(s_const, 4)
                    nc.gpsimd.affine_select(out=ident[:], in_=ident[:], compare_op=ALU.not_equal, fill=1.0, base=0,
                                            pattern=[[-1, P]], channel_multiplier=1).then_inc(s_const, 1)
                    nc.gpsimd.affine_select(out=before[:], in_=before[:], compare_op=ALU.is_gt, fill=0.0, base=0,
                                            pattern=[[1, P]], channel_multiplier=-1).then_inc(s_const, 1)
                    for n, off in enumerate((0, F, -F)):
                        nc.gpsimd.affine_select(out=halves[:], in_=halves[:], compare_op=ALU.not_equal, fill=1.0,
                                                base=off, pattern=[[-1, P]], channel_multiplier=1).then_inc(s_const, 1)
                        pool.wait_ge(s_const, 7 + n)

                @block.vector
                def _(dve):
                    nc.vector.memset(eps[:], LN_EPS).then_inc(s_dve, 1)
                    dve.wait_ge(s_dst, 32)
                    dve.wait_ge(s_first, 1)
                    nc.vector.tensor_tensor(m_same[:], d_cur[:, 1:W + 1], d_cur[:, 0:W], ALU.is_equal).then_inc(s_dve, 1)
                    dve.wait_ge(s_dve, SD["same"])
                    nc.vector.tensor_scalar(m_reset[:], m_same[:], -1.0, BIG, ALU.add, ALU.mult).then_inc(s_dve, 1)
                    dve.wait_ge(s_x, 16)
                    nc.vector.tensor_reduce(mean[:], X[:], AX, ALU.add).then_inc(s_dve, 1)
                    dve.wait_ge(s_dve, SD["mean"])
                    nc.vector.tensor_scalar(mean[:], mean[:], 1.0 / F, None, ALU.mult).then_inc(s_dve, 1)
                    dve.wait_ge(s_dve, SD["mean_s"])
                    nc.vector.tensor_tensor(HN[:], X[:], mean[:].unsqueeze(2).to_broadcast([NP, NT, F]),
                                            ALU.subtract).then_inc(s_dve, 1)
                    dve.wait_ge(s_dve, SD["centred"])
                    nc.vector.tensor_tensor(sq[:], HN[:], HN[:], ALU.mult).then_inc(s_dve, 1)
                    dve.wait_ge(s_dve, SD["square"])
                    nc.vector.tensor_reduce(var[:], sq[:], AX, ALU.add).then_inc(s_dve, 1)
                    dve.wait_ge(s_dve, SD["var"])
                    nc.vector.tensor_scalar(var[:], var[:], 1.0 / F, None, ALU.mult).then_inc(s_dve, 1)
                    dve.wait_ge(s_std, 1)
                    nc.vector.reciprocal(rstd[:], rstd[:]).then_inc(s_dve, 1)
                    dve.wait_ge(s_dve, SD["rstd"])
                    nc.vector.scalar_tensor_tensor(out=HN[:], in0=HN[:], scalar=0.0,
                                                   in1=rstd[:].unsqueeze(2).to_broadcast([NP, NT, F]),
                                                   op0=ALU.max, op1=ALU.mult).then_inc(s_dve, 1)

                @block.scalar
                def _(act):
                    act.wait_ge(s_dve, SD["var_s"])
                    nc.scalar.activation(rstd[:], var[:], ACT.Sqrt, bias=eps[0:NP, :]).then_inc(s_std, 1)
            ctx.clear()

        def rounds(eng, body):
            body(0, 0)
            body(0, 1)
            with eng.Fori(1, NIT) as it:
                body(it, 0)
                body(it, 1)

        def staggered(eng, early, late, n=NIT):
            def one(it):
                early(it, 1)
                late(it, 0)
                early(it + 1, 0)
                late(it, 1)
            early(0, 0)
            if n > 1:
                one(0)
            if n > 2:
                with eng.Fori(1, n - 1) as it:
                    one(it)
            early(n - 1, 1)
            late(n - 1, 0)
            late(n - 1, 1)

        def turned(t, q):
            return t.rearrange("f (p j) -> f j p", j=T)[:, 4 * q:4 * q + 4, :]

        def block_rows(eng, b):
            return [eng.snap(edges_of(half, b)) if not isinstance(b, int) else edges_of(half, b) for half in range(2)]

        def load_rows(sp, buf, array, b, s, cols):
            for half in range(2):
                rows = array[bass.ds(b[half], BK)] if cols == 1 else array[bass.ds(b[half], BK), :]
                view = rows.rearrange("(p j) -> p j", p=P) if cols == 1 else rows.rearrange("(p j) f -> p (j f)", p=P)
                sp.dma_start(buf[:, half * T * cols:(half + 1) * T * cols], view).then_inc(s, 16)

        def load_mask(sp, buf, mask, b, s):
            for half in range(2):
                row = mask[bass.ds(b[half], BK)]
                sp.dma_start(buf[half * F:(half + 1) * F, :], row.partition_broadcast(F)).then_inc(s, 16)

        def gather(g, table, idx, s, top):
            for j in range(T):
                for half in range(2):
                    nc.gpsimd.indirect_dma_start(
                        g[:, j * P + half * F:j * P + (half + 1) * F], None, table,
                        IND(ap=idx[:, half * T + j:half * T + j + 1], axis=0),
                        bounds_check=top, oob_is_err=False).then_inc(s, 16)

        GOT = 2 * T * 16

        def store_rows(act, buf, to, b, s, cols):
            for half in range(2):
                rows = to[bass.ds(b * BK + half * H, BK), :].rearrange("(p j) f -> p (j f)", p=P)
                act.dma_start(rows, buf[:, half, :, :].rearrange("p j f -> p (j f)")).then_inc(s, 16)

        def edge0():
            with Stage() as ctx:
                sd = [sb(f"e0_sd{i}", [P, 4 * T], I32, ctx) for i in range(2)]
                same = [sb(f"e0_same{i}", [P, BK], BF16, ctx) for i in range(2)]
                ea = [sb(f"e0_ea{i}", [P, 2 * T * D10], F32, ctx) for i in range(2)]
                eaT = [sb(f"e0_eaT{i}", [T * D10, 2 * P], F32, ctx) for i in range(2)]
                g = [sb(f"e0_g{i}", [P, T * P], F32, ctx) for i in range(2)]
                msg = [sb(f"e0_msg{i}", [P, BK], F32, ctx) for i in range(2)]
                R = [sb(f"e0_R{i}", [P, BK], F32, ctx) for i in range(2)]
                o = [sb(f"e0_o{i}", [P, 2, T, F], F32, ctx) for i in range(2)]
                wpad = sb("e0_wpad", [T * D10, 2 * T, P], F32, ctx)
                bias = sb("e0_bias", [P, 1], F32, ctx)
                zero = sb("e0_zero", [P, 2 * BK * F // P], F32, ctx)
                low = sb("e0_low", [P, 4 * T], I32, ctx)
                high = sb("e0_high", [P, 4 * T], I32, ctx)
                hot_low = [sb(f"e0_hot_low{i}", [P, T, P], BF16, ctx) for i in range(2)]
                hot_high = [sb(f"e0_hot_high{i}", [P, T, HB], BF16, ctx) for i in range(2)]
                over = sb("e0_over", [P, 2 * OT], I32, ctx)
                over_low = sb("e0_over_low", [P, 2 * OT], I32, ctx)
                over_high = sb("e0_over_high", [P, 2 * OT], I32, ctx)
                o_low = sb("e0_o_low", [P, 2 * OT, P], BF16, ctx)
                o_high = sb("e0_o_high", [P, 2 * OT, HB], BF16, ctx)
                counts = sb("e0_counts", [HB, 2, P], F32, ctx)
                zT = [ps(f"e0_zT{i}", [P, 4, P], ctx) for i in range(Q)]
                oT = [ps(f"e0_oT{i}", [P, 4, 2, F], ctx) for i in range(Q)]
                eT = ps("e0_eT", [T * D10, 2 * P], ctx)
                cnt = [ps(f"e0_cnt{i}", [HB, P], ctx) for i in range(2)]
                s_w, s_wz, s_over, s_ov, s_ovm, s_zero, s_zf, s_init, s_cnt, s_cnto = (ctx.sem(f"e0_{n}") for n in (
                    "weights", "weights_zeroed", "over_loaded", "over_hot", "over_counted", "zero_set", "own_zeroed", "initial",
                    "counts_read", "counts_stored"))
                gathered = dma_pair("e0_gathered")
                idx_in, same_in, ea_in, ea_turned, ea_copied, scanned, stored = (ctx.pair(f"e0_{n}") for n in (
                    "idx_in", "same_in", "ea_in", "ea_turned", "ea_copied", "scanned", "stored"))
                z_ready, msg_ready, o_turned, o_copied = ([ctx.pair(f"e0_{n}{q}_") for q in range(Q)] for n in (
                    "z_ready", "msg_ready", "o_turned", "o_copied"))
                low_made, high_made = ctx.pair("e0_low_made"), ctx.pair("e0_high_made")
                hot = [ctx.sem(f"e0_hot{s}") for s in range(4)]
                begun, loading = ctx.sem("e0_gathers_begun"), ctx.sem("e0_loads_begun")
                s_cntp = ctx.sem("e0_counts_read0")
                counted = [ctx.sem(f"e0_counted{s}") for s in range(4)]
                with nc.Block() as block:
                    @block.sync
                    def _(sp):
                        sp.wait_ge(s_wz, 1)
                        for j in range(T):
                            for half in range(2):
                                sp.dma_start(wpad[j * D10:(j + 1) * D10, half * T + j, half * F:(half + 1) * F],
                                             w["L0_gnn_W_edge"]).then_inc(s_w, 16)
                        for half in range(2):
                            sp.dma_start(bias[half * F:(half + 1) * F, :],
                                         w["L0_gnn_b_edge"].rearrange("(f o) -> f o", o=1)).then_inc(s_w, 16)
                        sp.dma_start(over[:, 0:OT], src[BASE:H].rearrange("(p j) -> p j", p=P)).then_inc(s_over, 16)
                        sp.dma_start(over[:, OT:2 * OT], dst[BASE:H].rearrange("(p j) -> p j", p=P)).then_inc(s_over, 16)
                        sp.wait_ge(s_zero, 1)

                        def load(it, par):
                            b = 2 * it + par
                            rows = block_rows(sp, b)
                            zeros_at = b * 2 * BK if isinstance(b, int) else sp.snap(b * 2 * BK)
                            wait_reuse(sp, gathered[par], it * GOT)
                            wait_reuse(sp, high_made[par], it)
                            sp.sem_inc(loading, 1)
                            load_rows(sp, sd[par][:, 0:2 * T], src, rows, idx_in[par], 1)
                            load_rows(sp, sd[par][:, 2 * T:4 * T], dst, rows, idx_in[par], 1)
                            wait_reuse(sp, ea_turned[par], it)
                            sp.sem_inc(loading, 1)
                            load_rows(sp, ea[par], ea10, rows, ea_in[par], D10)
                            wait_reuse(sp, scanned[par], it)
                            sp.sem_inc(loading, 1)
                            load_mask(sp, same[par], same_d, rows, same_in[par])
                            sp.dma_start(own_at_start[bass.ds(zeros_at, 2 * BK), :].rearrange("(p j) f -> p (j f)", p=P),
                                         zero[:]).then_inc(s_zf, 16)
                        rounds(sp, load)
                        sp.wait_ge(s_zf, 16 * NB)
                        sp.wait_ge(s_cnt, 1)
                        sp.dma_start(count_d.rearrange("a (h l) -> h a l", l=P), counts[:]).then_inc(s_cnto, 16)
                        sp.wait_ge(s_cnto, 16)

                    @block.gpsimd
                    def _(pool):
                        def g_block(it, par):
                            pool.wait_ge(idx_in[par], 64 * (it + 1))
                            wait_reuse(pool, z_ready[Q - 1][par], it)
                            pool.sem_inc(begun, 1)
                            gather(g[par], table0, sd[par], gathered[par], top)
                        top = pool.to_reg(N - 1)
                        rounds(pool, g_block)

                    @block.tensor
                    def _(pe):
                        pe.wait_ge(s_w, 16 * (2 * T + 2))
                        pe.wait_ge(s_ov, 5)
                        for a in range(2):
                            for j in range(OT):
                                mm = nc.tensor.matmul(cnt[a][:], o_high[:, a * OT + j, :], o_low[:, a * OT + j, :],
                                                      start=(j == 0), stop=False, skip_group_check=True)
                            mm.then_inc(s_ovm, 1)

                        def turn_in(it, par):
                            b = 2 * it + par
                            for s in range(4):
                                pe.wait_ge(hot[s], b + 1)
                                for j in range(T):
                                    mm = nc.tensor.matmul(cnt[s // 2][:], hot_high[s % 2][:, j, :], hot_low[s % 2][:, j, :],
                                                          start=False, stop=False, skip_group_check=True)
                                mm.then_inc(counted[s], 1)
                            pe.wait_ge(ea_in[par], 32 * (it + 1))
                            wait_reuse(pe, ea_copied[1 - par], it + par)
                            for half in range(2):
                                mm = nc.tensor.transpose(eT[:, half * P:(half + 1) * P],
                                                         ea[par][:, half * T * D10:(half + 1) * T * D10], ident[:])
                            mm.then_inc(ea_turned[par], 1)
                            pe.wait_ge(ea_copied[par], it + 1)
                            pe.wait_ge(gathered[par], GOT * (it + 1))
                            for q in range(Q):
                                wait_reuse(pe, msg_ready[q][1 - par], it + par)
                                for jj in range(4):
                                    j = 4 * q + jj
                                    nc.tensor.matmul(zT[q][:, jj, :], g[par][:, j * P:(j + 1) * P], ident[:],
                                                     start=True, stop=False)
                                    for half in range(2):
                                        mm = nc.tensor.matmul(zT[q][:, jj, :], wpad[:, half * T + j, :],
                                                              eaT[par][:, half * P:(half + 1) * P],
                                                              start=False, stop=(half == 1))
                                mm.then_inc(z_ready[q][par], 1)

                        def turn_out(it, par):
                            pe.wait_ge(scanned[par], it + 1)
                            v = R[par][:, :].rearrange("f (p j) -> f j p", j=T)
                            for q in range(Q):
                                wait_reuse(pe, o_copied[q][1 - par], it + par)
                                for jj in range(4):
                                    mm = nc.tensor.transpose(oT[q][:, jj, :, :].rearrange("p h f -> p (h f)"),
                                                             v[:, 4 * q + jj, :], ident[:])
                                mm.then_inc(o_turned[q][par], 1)
                        staggered(pe, turn_in, turn_out)

                    @block.scalar
                    def _(act):
                        act.wait_ge(s_w, 16 * (2 * T + 2))

                        def relu(it, par):
                            act.wait_ge(ea_turned[par], it + 1)
                            wait_reuse(act, z_ready[Q - 1][par], it)
                            nc.scalar.copy(eaT[par][:], eT[:]).then_inc(ea_copied[par], 1)
                            wait_reuse(act, scanned[par], it)
                            for q in range(Q):
                                act.wait_ge(z_ready[q][par], it + 1)
                                nc.scalar.activation(turned(msg[par][:, :], q), zT[q][:], ACT.Relu,
                                                     bias=bias[:]).then_inc(msg_ready[q][par], 1)

                        def give(it, par):
                            wait_reuse(act, stored[par], 32 * it)
                            for q in range(Q):
                                act.wait_ge(o_turned[q][par], it + 1)
                                nc.scalar.copy(o[par][:, :, 4 * q:4 * q + 4, :], oT[q][:].rearrange("p j h f -> p h j f")
                                               ).then_inc(o_copied[q][par], 1)
                            act.wait_ge(o_copied[0][par], it + 1)
                            act.wait_ge(o_copied[Q - 1][par], it + 1)
                            store_rows(act, o[par], stream, 2 * it + par, stored[par], F)
                        staggered(act, relu, give)
                        act.wait_ge(stored[0], 32 * NIT)
                        act.wait_ge(stored[1], 32 * NIT)

                    @block.vector
                    def _(dve):
                        nc.vector.memset(wpad[:], 0.0).then_inc(s_wz, 1)
                        nc.vector.memset(zero[:], 0.0).then_inc(s_zero, 1)
                        nc.vector.memset(R[1][:, BK - 1:BK], 0.0).then_inc(s_init, 1)
                        dve.wait_ge(s_over, 32)
                        nc.vector.tensor_scalar(over_low[:], over[:], P - 1, None, ALU.bitwise_and).then_inc(s_ov, 1)
                        nc.vector.tensor_scalar(over_high[:], over[:], 7, None, ALU.logical_shift_right).then_inc(s_ov, 1)
                        dve.wait_ge(s_ov, 2)
                        nc.vector.tensor_tensor(o_low[:], iota[:, 0:P].unsqueeze(1).to_broadcast([P, 2 * OT, P]),
                                                over_low[:].unsqueeze(2).to_broadcast([P, 2 * OT, P]),
                                                ALU.is_equal).then_inc(s_ov, 1)
                        nc.vector.tensor_tensor(o_high[:], iota[:, 0:HB].unsqueeze(1).to_broadcast([P, 2 * OT, HB]),
                                                over_high[:].unsqueeze(2).to_broadcast([P, 2 * OT, HB]),
                                                ALU.is_equal).then_inc(s_ov, 1)
                        dve.wait_ge(s_ov, 4)
                        nc.vector.tensor_scalar(o_high[:], o_high[:], -1.0, None, ALU.mult).then_inc(s_ov, 1)
                        dve.wait_ge(s_init, 1)

                        def histogram(it, par):
                            b = 2 * it + par
                            dve.wait_ge(idx_in[par], 64 * (it + 1))
                            wait_reuse(dve, hot[3], b)
                            nc.vector.tensor_scalar(low[:], sd[par][:], P - 1, None, ALU.bitwise_and
                                                    ).then_inc(low_made[par], 1)
                            nc.vector.tensor_scalar(high[:], sd[par][:], 7, None, ALU.logical_shift_right
                                                    ).then_inc(high_made[par], 1)
                            dve.wait_ge(low_made[par], it + 1)
                            dve.wait_ge(high_made[par], it + 1)
                            for s in range(4):
                                if s < 2:
                                    wait_reuse(dve, counted[s + 2], b)
                                else:
                                    dve.wait_ge(counted[s - 2], b + 1)
                                lv = low[:, s * T:(s + 1) * T].unsqueeze(2)
                                hv = high[:, s * T:(s + 1) * T].unsqueeze(2)
                                nc.vector.tensor_tensor(hot_low[s % 2][:], iota[:, 0:P].unsqueeze(1).to_broadcast([P, T, P]),
                                                        lv.to_broadcast([P, T, P]), ALU.is_equal)
                                nc.vector.tensor_tensor(hot_high[s % 2][:], iota[:, 0:HB].unsqueeze(1).to_broadcast([P, T, HB]),
                                                        hv.to_broadcast([P, T, HB]), ALU.is_equal).then_inc(hot[s], 1)

                        def scan(it, par):
                            dve.wait_ge(same_in[par], 32 * (it + 1))
                            for q in range(Q):
                                dve.wait_ge(msg_ready[q][par], it + 1)
                            wait_reuse(dve, o_turned[Q - 1][par], it)
                            wait_reuse(dve, scanned[1 - par], it + par)
                            nc.vector.tensor_tensor_scan(R[par][:, :], same[par][:, :], msg[par][:, :],
                                                         R[1 - par][:, BK - 1:BK], ALU.mult, ALU.add
                                                         ).then_inc(scanned[par], 1)
                        staggered(dve, histogram, scan)
                        for s in range(4):
                            dve.wait_ge(counted[s], NB)
                        nc.vector.tensor_copy(counts[:, 0, :], cnt[0][:]).then_inc(s_cntp, 1)
                        dve.wait_ge(s_cntp, 1)
                        nc.vector.tensor_copy(counts[:, 1, :], cnt[1][:]).then_inc(s_cnt, 1)
                ctx.clear()

                        
        def edge1():
            with Stage() as ctx:
                idx = [sb(f"e1_idx{i}", [P, 2 * T], I32, ctx) for i in range(2)]
                same = [sb(f"e1_same{i}", [P, BK], BF16, ctx) for i in range(2)]
                reset = [sb(f"e1_reset{i}", [P, BK], BF16, ctx) for i in range(2)]
                g = [sb(f"e1_g{i}", [P, T * P], F32, ctx) for i in range(2)]
                own = [sb(f"e1_own{i}", [P, T, 2, F], F32, ctx) for i in range(2)]
                ownT = [sb(f"e1_ownT{i}", [P, BK], F32, ctx) for i in range(2)]
                filled = [sb(f"e1_filled{i}", [P, BK], F32, ctx) for i in range(2)]
                z = [sb(f"e1_z{i}", [P, BK], F32, ctx) for i in range(2)]
                R = [sb(f"e1_R{i}", [P, BK], F32, ctx) for i in range(2)]
                o = [sb(f"e1_o{i}", [P, 2, T, F], F32, ctx) for i in range(2)]
                w2 = sb("e1_w2", [P, P], F32, ctx)
                base_dst = sb("e1_base_dst", [1, 1], I32, ctx)
                owT = [ps(f"e1_owT{i}", [P, 4, P], ctx) for i in range(Q)]
                gT = [ps(f"e1_gT{i}", [P, 4, P], ctx) for i in range(Q)]
                zW = [ps(f"e1_zW{i}", [P, 4 * P], ctx) for i in range(Q)]
                oT = [ps(f"e1_oT{i}", [P, 4, 2, F], ctx) for i in range(Q)]
                s_w, s_wz, s_b, s_init, s_first, begun, loading = (ctx.sem(f"e1_{n}") for n in (
                    "weights", "weights_zeroed", "base_dst", "initial", "first_own", "gathers_begun", "loads_begun"))
                gathered = dma_pair("e1_gathered")
                idx_in, same_in, reset_in, own_in, fill_done, relued, scanned, stored = (ctx.pair(f"e1_{n}") for n in (
                    "idx_in", "same_in", "reset_in", "own_in", "fill_done", "relued", "scanned", "stored"))
                own_turned, own_copied, g_turned, z_made, w_ready, o_turned, o_copied = (
                    [ctx.pair(f"e1_{n}{q}_") for q in range(Q)] for n in (
                        "own_turned", "own_copied", "g_turned", "z_made", "w_ready", "o_turned", "o_copied"))
                with nc.Block() as block:
                    @block.sync
                    def _(sp):
                        sp.dma_start(base_dst[:], dst[BASE:BASE + 1].rearrange("(o f) -> o f", o=1)).then_inc(s_b, 16)
                        sp.wait_ge(s_wz, 1)
                        for half in range(2):
                            sp.dma_start(w2[half * F:(half + 1) * F, half * F:(half + 1) * F], w["L1_gnn_W2"]).then_inc(s_w, 16)
                        sp.wait_ge(s_b, 16)
                        node = sp.value_load(base_dst[0:1, 0:1], min_val=0, max_val=N - 1)
                        sp.wait_ge(s_init, 2)
                        sp.dma_start(filled[1][F:P, BK - 1:BK], own_d[bass.ds(node, 1), :].rearrange("o f -> f o")
                                     ).then_inc(s_first, 16)

                        def load(it, par):
                            rows = block_rows(sp, 2 * it + par)
                            wait_reuse(sp, gathered[par], it * GOT)
                            sp.sem_inc(loading, 1)
                            load_rows(sp, idx[par], src, rows, idx_in[par], 1)
                            wait_reuse(sp, own_turned[Q - 1][par], it)
                            sp.sem_inc(loading, 1)
                            load_pairs(sp, own[par], own_at_start, rows, own_in[par])
                            wait_reuse(sp, fill_done[par], it)
                            sp.sem_inc(loading, 1)
                            load_mask(sp, same[par], same_d, rows, same_in[par])
                            wait_reuse(sp, scanned[par], it)
                            sp.sem_inc(loading, 1)
                            load_mask(sp, reset[par], reset_d, rows, reset_in[par])
                        rounds(sp, load)

                    @block.gpsimd
                    def _(pool):
                        top = pool.to_reg(N - 1)

                        def g_block(it, par):
                            pool.wait_ge(idx_in[par], 32 * (it + 1))
                            wait_reuse(pool, g_turned[Q - 1][par], it)
                            pool.sem_inc(begun, 1)
                            gather(g[par], table1, idx[par], gathered[par], top)
                        rounds(pool, g_block)

                    @block.tensor
                    def _(pe):
                        pe.wait_ge(s_w, 32)

                        def turn_in(it, par):
                            pe.wait_ge(own_in[par], 32 * (it + 1))
                            for q in range(Q):
                                wait_reuse(pe, own_copied[q][1 - par], it + par)
                                for jj in range(4):
                                    mm = nc.tensor.transpose(owT[q][:, jj, :],
                                                             own[par][:, 4 * q + jj, :, :].rearrange("p h f -> p (h f)"), ident[:])
                                mm.then_inc(own_turned[q][par], 1)
                            pe.wait_ge(gathered[par], GOT * (it + 1))
                            for q in range(Q):
                                wait_reuse(pe, z_made[q][1 - par], it + par)
                                for jj in range(4):
                                    j = 4 * q + jj
                                    mm = nc.tensor.transpose(gT[q][:, jj, :], g[par][:, j * P:(j + 1) * P], ident[:])
                                mm.then_inc(g_turned[q][par], 1)

                        def turn_out(it, par):
                            pe.wait_ge(relued[par], it + 1)
                            wait_reuse(pe, scanned[1 - par], it + par)
                            for q in range(Q):
                                nc.tensor.matmul(zW[q][:], w2[:], z[par][:, q * 4 * P:(q + 1) * 4 * P], start=True, stop=True
                                                 ).then_inc(w_ready[q][par], 1)
                            turn_back(pe, it, par, R[par], scanned, oT, o_copied, o_turned)
                        staggered(pe, turn_in, turn_out)

                    @block.scalar
                    def _(act):
                        def copy_own(it, par):
                            wait_reuse(act, fill_done[par], it)
                            for q in range(Q):
                                act.wait_ge(own_turned[q][par], it + 1)
                                nc.scalar.copy(turned(ownT[par][:, :], q), owT[q][:]).then_inc(own_copied[q][par], 1)

                        def give(it, par):
                            for q in range(Q):
                                act.wait_ge(z_made[q][par], it + 1)
                            nc.scalar.activation(z[par][:], z[par][:], ACT.Relu).then_inc(relued[par], 1)
                            give_back(act, it, par, o[par], stream, oT, o_turned, o_copied, stored)
                        staggered(act, copy_own, give)
                        act.wait_ge(stored[0], 32 * NIT)
                        act.wait_ge(stored[1], 32 * NIT)

                    @block.vector
                    def _(dve):
                        nc.vector.memset(w2[:], 0.0).then_inc(s_wz, 1)
                        nc.vector.memset(filled[1][:, BK - 1:BK], 0.0).then_inc(s_init, 1)
                        nc.vector.memset(R[1][:, BK - 1:BK], -BIG).then_inc(s_init, 1)
                        dve.wait_ge(s_first, 16)

                        def fill(it, par):
                            dve.wait_ge(same_in[par], 32 * (it + 1))
                            for q in range(Q):
                                dve.wait_ge(own_copied[q][par], it + 1)
                            wait_reuse(dve, fill_done[1 - par], it + par)
                            nc.vector.tensor_tensor_scan(filled[par][:], same[par][:], ownT[par][:],
                                                         filled[1 - par][:, BK - 1:BK], ALU.mult, ALU.add
                                                         ).then_inc(fill_done[par], 1)
                            dve.wait_ge(fill_done[par], it + 1)
                            wait_reuse(dve, w_ready[Q - 1][par], it)
                            for q in range(Q):
                                dve.wait_ge(g_turned[q][par], it + 1)
                                nc.vector.tensor_tensor(turned(z[par][:, :], q), gT[q][:], turned(filled[par][:, :], q),
                                                        ALU.add).then_inc(z_made[q][par], 1)

                        def scan(it, par):
                            dve.wait_ge(reset_in[par], 32 * (it + 1))
                            wait_reuse(dve, o_turned[Q - 1][par], it)
                            wait_reuse(dve, scanned[1 - par], it + par)
                            for q in range(Q):
                                dve.wait_ge(w_ready[q][par], it + 1)
                                before_ = R[1 - par][:, BK - 1:BK] if q == 0 else R[par][:, q * 512 - 1:q * 512]
                                if q:
                                    dve.wait_ge(half_scanned[par], it * (Q - 1) + q)
                                sc = nc.vector.tensor_tensor_scan(
                                    R[par][:, q * 512:(q + 1) * 512], reset[par][:, q * 512:(q + 1) * 512], zW[q][:],
                                    before_, ALU.add, ALU.max)
                                sc.then_inc(scanned[par] if q == Q - 1 else half_scanned[par], 1)
                        half_scanned = ctx.pair("e1_half_scanned")

                        def both(it, par):
                            fill(it, par)
                            scan(it, par)
                        rounds(dve, both)
                ctx.clear()

        def edge2():
            with Stage() as ctx:
                idx = [sb(f"e2_idx{i}", [P, 2 * T], I32, ctx) for i in range(2)]
                same = [sb(f"e2_same{i}", [P, BK], BF16, ctx) for i in range(2)]
                g = [sb(f"e2_g{i}", [P, T * P], F32, ctx) for i in range(2)]
                msg = [sb(f"e2_msg{i}", [P, BK], F32, ctx) for i in range(2)]
                R = [sb(f"e2_R{i}", [P, BK], F32, ctx) for i in range(2)]
                o = [sb(f"e2_o{i}", [P, 2, T, F], F32, ctx) for i in range(2)]
                gT = [ps(f"e2_gT{i}", [P, 4, P], ctx) for i in range(Q)]
                oT = [ps(f"e2_oT{i}", [P, 4, 2, F], ctx) for i in range(Q)]
                s_init, begun, loading = (ctx.sem(f"e2_{n}") for n in ("initial", "gathers_begun", "loads_begun"))
                gathered = dma_pair("e2_gathered")
                idx_in, same_in, scanned, stored = (ctx.pair(f"e2_{n}") for n in (
                    "idx_in", "same_in", "scanned", "stored"))
                g_turned, msg_ready, o_turned, o_copied = ([ctx.pair(f"e2_{n}{q}_") for q in range(Q)] for n in (
                    "g_turned", "msg_ready", "o_turned", "o_copied"))
                with nc.Block() as block:
                    @block.sync
                    def _(sp):
                        def load(it, par):
                            rows = block_rows(sp, 2 * it + par)
                            wait_reuse(sp, gathered[par], it * GOT)
                            sp.sem_inc(loading, 1)
                            load_rows(sp, idx[par], src, rows, idx_in[par], 1)
                            wait_reuse(sp, scanned[par], it)
                            sp.sem_inc(loading, 1)
                            load_mask(sp, same[par], same_d, rows, same_in[par])
                        rounds(sp, load)

                    @block.gpsimd
                    def _(pool):
                        top = pool.to_reg(N - 1)

                        def g_block(it, par):
                            pool.wait_ge(idx_in[par], 32 * (it + 1))
                            wait_reuse(pool, g_turned[Q - 1][par], it)
                            pool.sem_inc(begun, 1)
                            gather(g[par], table2, idx[par], gathered[par], top)
                        rounds(pool, g_block)

                    @block.tensor
                    def _(pe):
                        def turn_in(it, par):
                            pe.wait_ge(gathered[par], GOT * (it + 1))
                            for q in range(Q):
                                wait_reuse(pe, msg_ready[q][1 - par], it + par)
                                for jj in range(4):
                                    j = 4 * q + jj
                                    mm = nc.tensor.transpose(gT[q][:, jj, :], g[par][:, j * P:(j + 1) * P], ident[:])
                                mm.then_inc(g_turned[q][par], 1)

                        def turn_out(it, par):
                            turn_back(pe, it, par, R[par], scanned, oT, o_copied, o_turned)
                        staggered(pe, turn_in, turn_out)

                    @block.scalar
                    def _(act):
                        def copy_in(it, par):
                            wait_reuse(act, scanned[par], it)
                            for q in range(Q):
                                act.wait_ge(g_turned[q][par], it + 1)
                                nc.scalar.copy(turned(msg[par][:, :], q), gT[q][:]).then_inc(msg_ready[q][par], 1)

                        def give(it, par):
                            give_back(act, it, par, o[par], stream, oT, o_turned, o_copied, stored)
                        staggered(act, copy_in, give)
                        act.wait_ge(stored[0], 32 * NIT)
                        act.wait_ge(stored[1], 32 * NIT)

                    @block.vector
                    def _(dve):
                        nc.vector.memset(R[1][:, BK - 1:BK], 0.0).then_inc(s_init, 1)
                        dve.wait_ge(s_init, 1)

                        def scan(it, par):
                            dve.wait_ge(same_in[par], 32 * (it + 1))
                            for q in range(Q):
                                dve.wait_ge(msg_ready[q][par], it + 1)
                            wait_reuse(dve, o_turned[Q - 1][par], it)
                            wait_reuse(dve, scanned[1 - par], it + par)
                            nc.vector.tensor_tensor_scan(R[par][:, :], same[par][:, :], msg[par][:, :],
                                                         R[1 - par][:, BK - 1:BK], ALU.mult, ALU.add
                                                         ).then_inc(scanned[par], 1)
                        rounds(dve, scan)
                ctx.clear()

        def edge3():
            with Stage() as ctx:
                C = 4 * P
                idx = [sb(f"e3_idx{i}", [P, 2 * T], I32, ctx) for i in range(2)]
                same = [sb(f"e3_same{i}", [P, BK], BF16, ctx) for i in range(2)]
                g = [sb(f"e3_g{i}", [P, T * P], F32, ctx) for i in range(2)]
                eh = [sb(f"e3_eh{i}", [P, T, 2, F], F32, ctx) for i in range(2)]
                m = [sb(f"e3_m{i}", [P, BK], F32, ctx) for i in range(2)]
                top_ = [sb(f"e3_max{i}", [P, BK + 1], F32, ctx) for i in range(2)]
                lift = [sb(f"e3_lift{q}", [P, 2, C], F32, ctx) for q in range(Q)]
                part = [sb(f"e3_part{q}", [P, 2, C], F32, ctx) for q in range(Q)]
                den = [sb(f"e3_den{i}", [P, BK], F32, ctx) for i in range(2)]
                num = [sb(f"e3_num{i}", [P, BK], F32, ctx) for i in range(2)]
                o = [sb(f"e3_o{i}", [P, 2, T, 2 * F], F32, ctx) for i in range(2)]
                zT = [ps(f"e3_zT{i}", [P, 4, P], ctx) for i in range(Q)]
                oT = [[ps(f"e3_oT{k}_{i}", [P, 4, 2, F], ctx) for i in range(Q)] for k in range(2)]
                s_init, begun, loading = (ctx.sem(f"e3_{n}") for n in ("initial", "gathers_begun", "loads_begun"))
                gathered = dma_pair("e3_gathered")
                idx_in, same_in, eh_in, stored, carried = (ctx.pair(f"e3_{n}") for n in (
                    "idx_in", "same_in", "eh_in", "stored", "carried"))
                z_ready, m_ready, maxed, lifted, under, expd, decay, parted, den_done, num_done = (
                    [ctx.pair(f"e3_{n}{q}_") for q in range(Q)] for n in (
                        "z_ready", "m_ready", "maxed", "lifted", "under", "expd", "decay", "parted", "den_done", "num_done"))
                o_turned = [ctx.pair(f"e3_o_turned{q}_") for q in range(Q)]
                o_copied = [ctx.pair(f"e3_o_copied{q}_") for q in range(Q)]
                with nc.Block() as block:
                    @block.sync
                    def _(sp):
                        def load(it, par):
                            rows = block_rows(sp, 2 * it + par)
                            wait_reuse(sp, gathered[par], it * GOT)
                            sp.sem_inc(loading, 1)
                            load_rows(sp, idx[par], src, rows, idx_in[par], 1)
                            wait_reuse(sp, z_ready[Q - 1][par], it)
                            sp.sem_inc(loading, 1)
                            load_pairs(sp, eh[par], ea64, rows, eh_in[par])
                            wait_reuse(sp, num_done[Q - 1][par], it)
                            sp.sem_inc(loading, 1)
                            load_mask(sp, same[par], same_d, rows, same_in[par])
                        rounds(sp, load)

                    @block.gpsimd
                    def _(pool):
                        top = pool.to_reg(N - 1)

                        def g_block(it, par):
                            pool.wait_ge(idx_in[par], 32 * (it + 1))
                            wait_reuse(pool, z_ready[Q - 1][par], it)
                            pool.sem_inc(begun, 1)
                            gather(g[par], table3, idx[par], gathered[par], top)
                        rounds(pool, g_block)

                    @block.tensor
                    def _(pe):
                        def turn_in(it, par):
                            pe.wait_ge(eh_in[par], 32 * (it + 1))
                            pe.wait_ge(gathered[par], GOT * (it + 1))
                            for q in range(Q):
                                wait_reuse(pe, m_ready[q][1 - par], it + par)
                                for jj in range(4):
                                    j = 4 * q + jj
                                    nc.tensor.matmul(zT[q][:, jj, :], g[par][:, j * P:(j + 1) * P], ident[:],
                                                     start=True, stop=False)
                                    mm = nc.tensor.matmul(zT[q][:, jj, :], eh[par][:, j, :, :].rearrange("p h f -> p (h f)"),
                                                          ident[:], start=False, stop=True)
                                mm.then_inc(z_ready[q][par], 1)

                        def turn_out(it, par):
                            for q in range(Q):
                                pe.wait_ge(num_done[q][par], it + 1)
                            pe.wait_ge(den_done[Q - 1][par], it + 1)
                            for q in range(Q):
                                wait_reuse(pe, o_copied[q][1 - par], it + par)
                                for k, t in enumerate((num[par][:, :], den[par][:, :])):
                                    v = t.rearrange("f (p j) -> f j p", j=T)
                                    for jj in range(4):
                                        mm = nc.tensor.transpose(oT[k][q][:, jj, :, :].rearrange("p h f -> p (h f)"),
                                                                 v[:, 4 * q + jj, :], ident[:])
                                mm.then_inc(o_turned[q][par], 1)
                        staggered(pe, turn_in, turn_out)

                    @block.scalar
                    def _(act):
                        def exps(it, par):
                            for q in range(Q):
                                act.wait_ge(lifted[q][par], it + 1)
                                act.wait_ge(under[q][par], it + 1)
                                nc.scalar.activation(lift[q][:], lift[q][:], ACT.Exp).then_inc(expd[q][par], 1)

                        def relu(it, par):
                            wait_reuse(act, num_done[Q - 1][par], it)
                            for q in range(Q):
                                act.wait_ge(z_ready[q][par], it + 1)
                                nc.scalar.activation(turned(m[par][:, :], q), zT[q][:], ACT.Relu).then_inc(m_ready[q][par], 1)
                            exps(it, par)

                        def give(it, par):
                            wait_reuse(act, stored[par], 48 * it)
                            for q in range(Q):
                                act.wait_ge(o_turned[q][par], it + 1)
                                for k in range(2):
                                    cp = nc.scalar.copy(o[par][:, :, 4 * q:4 * q + 4, k * F:(k + 1) * F],
                                                        oT[k][q][:].rearrange("p j h f -> p h j f"))
                                cp.then_inc(o_copied[q][par], 1)
                            for q in range(Q):
                                act.wait_ge(o_copied[q][par], it + 1)
                            store_rows(act, o[par], stream3, 2 * it + par, stored[par], 2 * F)
                            act.dma_start(maxes[:, bass.ds((2 * it + par) * BK, BK)], top_[par][:, 1:BK + 1]
                                          ).then_inc(stored[par], 16)
                        staggered(act, relu, give)
                        act.wait_ge(stored[0], 48 * NIT)
                        act.wait_ge(stored[1], 48 * NIT)

                    @block.vector
                    def _(dve):
                        nc.vector.memset(top_[1][:, BK:BK + 1], 0.0).then_inc(s_init, 1)
                        nc.vector.memset(den[1][:, BK - 1:BK], 0.0).then_inc(s_init, 1)
                        nc.vector.memset(num[1][:, BK - 1:BK], 0.0).then_inc(s_init, 1)
                        dve.wait_ge(s_init, 3)

                        def logits(it, par, q):
                            c = slice(q * C, (q + 1) * C)
                            dve.wait_ge(maxed[q - 1][par] if q else carried[par], it + 1)
                            nc.vector.tensor_tensor_scan(top_[par][:, q * C + 1:(q + 1) * C + 1], same[par][:, c], m[par][:, c],
                                                         top_[par][:, q * C:q * C + 1], ALU.mult, ALU.max
                                                         ).then_inc(maxed[q][par], 1)
                            dve.wait_ge(maxed[q][par], it + 1)
                            wait_reuse(dve, den_done[q][1 - par], it + par)
                            nc.vector.tensor_tensor(lift[q][:, 0, :], top_[par][:, c], top_[par][:, q * C + 1:(q + 1) * C + 1],
                                                    ALU.subtract).then_inc(lifted[q][par], 1)
                            nc.vector.tensor_tensor(lift[q][:, 1, :], m[par][:, c], top_[par][:, q * C + 1:(q + 1) * C + 1],
                                                    ALU.subtract).then_inc(under[q][par], 1)

                        def sums(it, par, q):
                            c = slice(q * C, (q + 1) * C)
                            last = slice(BK - 1, BK) if q == 0 else slice(q * C - 1, q * C)
                            of = 1 - par if q == 0 else par
                            dve.wait_ge(expd[q][par], it + 1)
                            nc.vector.tensor_tensor(part[q][:, 0, :], lift[q][:, 0, :], same[par][:, c], ALU.mult
                                                    ).then_inc(decay[q][par], 1)
                            nc.vector.tensor_tensor(part[q][:, 1, :], lift[q][:, 1, :], m[par][:, c], ALU.mult
                                                    ).then_inc(parted[q][par], 1)
                            dve.wait_ge(decay[q][par], it + 1)
                            dve.wait_ge(parted[q][par], it + 1)
                            n_before = it + par if q == 0 else it + 1
                            wait_reuse(dve, den_done[(q - 1) % Q][of], n_before)
                            wait_reuse(dve, num_done[(q - 1) % Q][of], n_before)
                            nc.vector.tensor_tensor_scan(den[par][:, c], part[q][:, 0, :], lift[q][:, 1, :], den[of][:, last],
                                                         ALU.mult, ALU.add).then_inc(den_done[q][par], 1)
                            nc.vector.tensor_tensor_scan(num[par][:, c], part[q][:, 0, :], part[q][:, 1, :], num[of][:, last],
                                                         ALU.mult, ALU.add).then_inc(num_done[q][par], 1)

                        def both(it, par):
                            dve.wait_ge(same_in[par], 32 * (it + 1))
                            wait_reuse(dve, o_turned[Q - 1][par], it)
                            wait_reuse(dve, stored[par], 48 * it)
                            for q in range(Q):
                                dve.wait_ge(m_ready[q][par], it + 1)
                            wait_reuse(dve, maxed[Q - 1][1 - par], it + par)
                            nc.vector.tensor_copy(top_[par][:, 0:1], top_[1 - par][:, BK:BK + 1]).then_inc(carried[par], 1)
                            for q in range(Q):
                                logits(it, par, q)
                            for q in range(Q):
                                sums(it, par, q)
                        rounds(dve, both)
                ctx.clear()

        def load_pairs(sp, buf, array, b, s):
            for half in range(2):
                sp.dma_start(buf[:, :, half, :], array[bass.ds(b[half], BK), :].rearrange("(p j) f -> p j f", p=P)
                             ).then_inc(s, 16)

        def turn_back(pe, it, par, R, scanned, oT, o_copied, o_turned):
            pe.wait_ge(scanned[par], it + 1)
            v = R[:, :].rearrange("f (p j) -> f j p", j=T)
            for q in range(Q):
                wait_reuse(pe, o_copied[q][1 - par], it + par)
                for jj in range(4):
                    mm = nc.tensor.transpose(oT[q][:, jj, :, :].rearrange("p h f -> p (h f)"), v[:, 4 * q + jj, :], ident[:])
                mm.then_inc(o_turned[q][par], 1)

        def give_back(act, it, par, o, to, oT, o_turned, o_copied, stored):
            wait_reuse(act, stored[par], 32 * it)
            for q in range(Q):
                act.wait_ge(o_turned[q][par], it + 1)
                nc.scalar.copy(o[:, :, 4 * q:4 * q + 4, :], oT[q][:].rearrange("p j h f -> p h j f")
                               ).then_inc(o_copied[q][par], 1)
            for q in range(Q):
                act.wait_ge(o_copied[q][par], it + 1)
            store_rows(act, o, to, 2 * it + par, stored[par], F)

        def chunk(t, c):
            return t[:, bass.ds(c * CH, CH)]

        def same_values(to, of):
            return nc.vector.tensor_scalar(to, of, 1.0, None, ALU.mult)

        def over_f(v):
            return v.unsqueeze(2).to_broadcast([NP, CH, F])

        def over_n(row):
            return row.unsqueeze(1).to_broadcast([NP, CH, F])

        def chunks(eng, body):
            body(0, 0, 0)
            body(1, 0, 1)
            if NC > 2:
                with eng.Fori(1, NC // 2) as it:
                    body(2 * it, it, 0)
                    body(2 * it + 1, it, 1)

        def fetch(pool, ag, ix, table, got, ix_ready, used, begun, top):
            def one(c, it, par):
                pool.wait_ge(ix_ready[par], it + 1)
                wait_reuse(pool, used[par], it)
                pool.sem_inc(begun, 1)
                for t in range(CH):
                    nc.gpsimd.indirect_dma_start(ag[par][:, t, :], None, table, IND(ap=ix[par][:, t:t + 1], axis=0),
                                                 bounds_check=top, oob_is_err=False).then_inc(got[par], 16)
            chunks(pool, one)

        def next_index(dve, c, it, par, ix, got, ix_ready):
            wait_reuse(dve, got[1 - par], 16 * CH * (it + par))
            same_values(ix[1 - par][:], row_at[:, bass.ds(c * CH + CH, CH)]).then_inc(ix_ready[1 - par], 1)

        class Normed:
            names = ("mean", "mean_s", "centred", "square", "var", "var_s", "rstd", "h")

            def __init__(self, ctx, tag):
                self.small = [sb(f"{tag}_{n}", [NP, CH], F32, ctx) for n in ("lmean", "lvar", "lrstd")]
                self.sq = sb(f"{tag}_lsq", [NP, CH, F], F32, ctx)

            def vector(self, dve, xs, hn, s, seq, std, c, ready):
                mean, var, rstd = self.small
                nc.vector.tensor_reduce(mean[:], xs, AX, ALU.add).then_inc(s, 1)
                wait_reuse(dve, s, at(seq, "mean", c))
                nc.vector.tensor_scalar(mean[:], mean[:], 1.0 / F, None, ALU.mult).then_inc(s, 1)
                wait_reuse(dve, s, at(seq, "mean_s", c))
                ready()
                nc.vector.tensor_tensor(hn, xs, over_f(mean[:]), ALU.subtract).then_inc(s, 1)
                wait_reuse(dve, s, at(seq, "centred", c))
                nc.vector.tensor_tensor(self.sq[:], hn, hn, ALU.mult).then_inc(s, 1)
                wait_reuse(dve, s, at(seq, "square", c))
                nc.vector.tensor_reduce(var[:], self.sq[:], AX, ALU.add).then_inc(s, 1)
                wait_reuse(dve, s, at(seq, "var", c))
                nc.vector.tensor_scalar(var[:], var[:], 1.0 / F, None, ALU.mult).then_inc(s, 1)
                dve.wait_ge(std, c + 1)
                nc.vector.reciprocal(rstd[:], rstd[:]).then_inc(s, 1)
                wait_reuse(dve, s, at(seq, "rstd", c))
                nc.vector.scalar_tensor_tensor(out=hn, in0=hn, scalar=0.0, in1=over_f(rstd[:]), op0=ALU.max,
                                               op1=ALU.mult).then_inc(s, 1)

            def scalar(self, act, s, seq, std, c):
                mean, var, rstd = self.small
                wait_reuse(act, s, at(seq, "var_s", c))
                nc.scalar.activation(rstd[:], var[:], ACT.Sqrt, bias=eps[0:NP, :]).then_inc(std, 1)

        def turn_nodes(pT, rows):
            for i in range(NPR):
                mm = nc.tensor.transpose(pT[:, i, 0:NP], rows[:, 2 * i:2 * i + 2, :].rearrange("p a f -> p (a f)"),
                                         ident[0:NP, 0:NP])
            return mm

        def blocks_of(sp, big, small, s):
            for half in range(2):
                sp.dma_start(big[half * F:(half + 1) * F, half * F:(half + 1) * F], small).then_inc(s, 16)

        def column(sp, col, vec, s):
            for half in range(2):
                sp.dma_start(col[half * F:(half + 1) * F, :], vec.rearrange("(f o) -> f o", o=1)).then_inc(s, 16)

        def runs():
            with Stage() as ctx:
                c2 = sb("r_counts", [NP, 2, NT], F32, ctx)
                ones = sb("r_ones", [NP, NT], F32, ctx)
                cum = sb("r_cum", [NP, NT], F32, ctx)
                off = sb("r_off", [NP, 1], F32, ctx)
                first = sb("r_first", [NP, NT], F32, ctx)
                lastf = sb("r_last", [NP, NT], F32, ctx)
                late = sb("r_late", [NP, NT], F32, ctx)
                tmp = sb("r_tmp", [NP, NT], F32, ctx)
                none = sb("r_none", [NP, NT], F32, ctx)
                p = ps("r_p", [P, 512], ctx)
                at_cut = sb("r_at_cut", [NP, 1], F32, ctx)
                s_c, s_d, s_p, s_a = (ctx.sem(f"r_{n}") for n in ("counts_in", "dve", "rows_before", "roots"))
                with nc.Block() as block:
                    @block.sync
                    def _(sp):
                        for a in range(2):
                            sp.dma_start(c2[:, a, :], count_d[a, 0:N].rearrange("(p t) -> p t", p=NP)).then_inc(s_c, 16)

                    @block.tensor
                    def _(pe):
                        pe.wait_ge(s_d, 2)
                        nc.tensor.matmul(p[0:NP, 0:1], before[0:NP, 0:NP], cum[:, NT - 1:NT], start=True, stop=True
                                         ).then_inc(s_p, 1)

                        pe.wait_ge(s_d, 18)
                        nc.tensor.matmul(p[0:1, 0:1], at_cut[:], ones[:, 0:1], start=True, stop=True).then_inc(s_p, 1)

                    @block.scalar
                    def _(act):
                        act.wait_ge(s_d, 4)
                        nc.scalar.activation(in_scale[:], in_scale[:], ACT.Sqrt).then_inc(s_a, 1)
                        nc.scalar.activation(out_scale[:], out_scale[:], ACT.Sqrt).then_inc(s_a, 1)

                    @block.vector
                    def _(dve):
                        done = [0]

                        def then(i):
                            i.then_inc(s_d, 1)
                            done[0] += 1
                            dve.wait_ge(s_d, done[0])
                        then(nc.vector.memset(ones[:], 1.0))
                        dve.wait_ge(s_c, 32)
                        then(nc.vector.tensor_tensor_scan(cum[:], ones[:], c2[:, 1, :], 0.0, ALU.mult, ALU.add))
                        then(nc.vector.tensor_scalar(out_scale[:], c2[:, 0, :], 1.0, None, ALU.max))
                        then(nc.vector.tensor_scalar(in_scale[:], c2[:, 1, :], 1.0, None, ALU.max))
                        then(nc.vector.tensor_scalar(has[:], c2[:, 1, :], 1.0, None, ALU.is_ge))
                        dve.wait_ge(s_p, 1)
                        then(nc.vector.tensor_copy(off[:], p[0:NP, 0:1]))
                        then(nc.vector.tensor_scalar(cum[:], cum[:], off[:], None, ALU.add))
                        then(nc.vector.tensor_tensor(first[:], cum[:], c2[:, 1, :], ALU.subtract))
                        then(nc.vector.tensor_scalar(lastf[:], cum[:], -1.0, 0.0, ALU.add, ALU.max))
                        then(nc.vector.tensor_scalar(late[:], lastf[:], float(H), None, ALU.is_ge))
                        then(nc.vector.scalar_tensor_tensor(out=lastf[:], in0=late[:], scalar=float(H - BASE), in1=lastf[:],
                                                            op0=ALU.mult, op1=ALU.add))
                        then(nc.vector.memset(row_at[:], 0))
                        then(nc.vector.memset(first_at[:], 0))
                        then(nc.vector.tensor_copy(row_at[:, 0:NT], lastf[:]))
                        then(nc.vector.tensor_scalar(tmp[:], first[:], float(BASE), None, ALU.is_lt))
                        then(nc.vector.tensor_tensor(cut[:], tmp[:], late[:], ALU.mult))
                        then(nc.vector.scalar_tensor_tensor(out=tmp[:], in0=lastf[:], scalar=-float(H), in1=cut[:],
                                                            op0=ALU.add, op1=ALU.mult))
                        then(nc.vector.tensor_reduce(at_cut[:], tmp[:], AX, ALU.add))
                        dve.wait_ge(s_p, 2)
                        then(nc.vector.tensor_copy(cut_last[:], p[0:1, 0:1]))
                        then(nc.vector.tensor_scalar(none[:], has[:], -1.0, -float(1 << 22), ALU.add, ALU.mult))
                        then(nc.vector.tensor_tensor(none[:], none[:], first[:], ALU.add))
                        then(nc.vector.tensor_copy(first_at[:, 0:NT], none[:]))
                        dve.wait_ge(s_a, 2)
                        then(nc.vector.reciprocal(out_scale[:], out_scale[:]))
                        then(nc.vector.reciprocal(in_scale[:], in_scale[:]))
                        then(nc.vector.tensor_tensor(in_scale[:], in_scale[:], has[:], ALU.mult))
                ctx.clear()

        def node0():
            with Stage() as ctx:
                G = sb("n0_G", [P, NC * NPR * NP], F32, ctx)
                dev = sb("n0_dev", [P, NC * NPR * NP], F32, ctx)
                ag = [sb(f"n0_ag{i}", [NP, CH, F], F32, ctx) for i in range(2)]
                ix = [sb(f"n0_ix{i}", [NP, CH], I32, ctx) for i in range(2)]
                carry = sb("n0_carry", [NP, F], F32, ctx)
                hs = sb("n0_hs", [NP, CH, F], F32, ctx)
                cr = sb("n0_cr", [NP, CH, F], F32, ctx)
                hT = sb("n0_hT", [P, NPR, NP], F32, ctx)
                a1 = sb("n0_a1", [P, NPR, NP], F32, ctx)
                w1, w2, wa, wb = (sb(f"n0_w{i}", [P, P], F32, ctx) for i in "12ab")
                ownb = sb("n0_ownb", [NP, F], F32, ctx)
                b1, b2, gamma, beta = (sb(f"n0_{n}", [P, 1], F32, ctx) for n in ("b1", "b2", "gamma", "beta"))
                total, nmean, ssq, var, rstd, scale, shift, beps = (sb(f"n0_{n}", [P, 1], F32, ctx) for n in (
                    "total", "nmean", "ssq", "var", "rstd", "scale", "shift", "beps"))
                pA, pB, pC, pD = (ps(f"n0_p{n}", [P, 8, P], ctx) for n in "ABCD")
                s_w, s_wz, s_d, s_p, s_a, begun, s_ix0, s_bn, s_w2 = (ctx.sem(f"n0_{n}") for n in (
                    "weights", "weights_zeroed", "dve", "pe", "act", "gathers_begun", "index0", "bn", "weights2"))
                got = dma_pair("n0_got")
                ix_ready, used = (ctx.pair(f"n0_{n}") for n in ("ix_ready", "used"))
                D = steps("masked", "plus_h", "carry", "sum")
                PEQ = steps("turned", "lin1", "lin2")
                A = steps("hT", "a1", "g")
                with nc.Block() as block:
                    @block.sync
                    def _(sp):
                        sp.wait_ge(s_wz, 4)
                        blocks_of(sp, w1, w["L0_gnn_W1"], s_w)
                        blocks_of(sp, w2, w["L0_gnn_W2"], s_w)
                        column(sp, b1, w["L0_gnn_b1"], s_w)
                        column(sp, b2, w["L0_gnn_b2"], s_w)
                        column(sp, gamma, w["L0_gnn_bn_gamma"], s_w)
                        column(sp, beta, w["L0_gnn_bn_beta"], s_w)
                        sp.dma_start(carry[:], stream[BASE - 1, :].partition_broadcast(NP)).then_inc(s_w, 16)
                        blocks_of(sp, wa, w["L1_gnn_W1"][0:F, :], s_w2)
                        blocks_of(sp, wb, w["L1_gnn_W1"][F:2 * F, :], s_w2)
                        sp.dma_start(ownb[:], w["L1_gnn_b1"].partition_broadcast(NP)).then_inc(s_w2, 16)

                    @block.gpsimd
                    def _(pool):
                        fetch(pool, ag, ix, stream, got, ix_ready, used, begun, pool.to_reg(2 * H - 1))

                    @block.vector
                    def _(dve):
                        for m in (w1, w2, wa, wb):
                            nc.vector.memset(m[:], 0.0).then_inc(s_wz, 1)
                        nc.vector.memset(beps[:], BN_EPS).then_inc(s_ix0, 1)
                        nc.vector.tensor_copy(ix[0][:], row_at[:, 0:CH]).then_inc(ix_ready[0], 1)
                        dve.wait_ge(s_w, 208)

                        def one(c, it, par):
                            next_index(dve, c, it, par, ix, got, ix_ready)
                            dve.wait_ge(got[par], 16 * CH * (it + 1))
                            wait_reuse(dve, s_p, c * len(PEQ))
                            nc.vector.tensor_tensor(hs[:], ag[par][:], over_f(chunk(has, c)), ALU.mult).then_inc(s_d, 1)
                            wait_reuse(dve, s_d, at(D, "masked", c))
                            nc.vector.tensor_tensor(hs[:], hs[:], HN[:, bass.ds(c * CH, CH), :], ALU.add).then_inc(s_d, 1)
                            nc.vector.tensor_tensor(cr[:], over_n(carry[:]), over_f(chunk(cut, c)), ALU.mult).then_inc(s_d, 1)
                            wait_reuse(dve, s_d, at(D, "carry", c))
                            nc.vector.tensor_tensor(hs[:], hs[:], cr[:], ALU.add).then_inc(s_d, 1)
                            wait_reuse(dve, s_d, at(D, "sum", c))
                            dve.sem_inc(used[par], 1)
                        chunks(dve, one)
                        dve.wait_ge(s_w2, 80)
                        nc.vector.tensor_tensor(wa[:], wa[:], wb[:], ALU.subtract)

                        dve.wait_ge(s_a, NC * len(A))
                        nc.vector.tensor_reduce(total[:], G[:], AX, ALU.add).then_inc(s_bn, 1)
                        dve.wait_ge(s_bn, 2)
                        nc.vector.tensor_scalar(nmean[:], pA[:, 0, 0:1], -1.0 / N, None, ALU.mult).then_inc(s_bn, 1)
                        dve.wait_ge(s_bn, 5)
                        nc.vector.tensor_scalar(var[:], pA[:, 4, 0:1], 1.0 / N, None, ALU.mult).then_inc(s_bn, 1)
                        dve.wait_ge(s_bn, 7)
                        nc.vector.reciprocal(rstd[:], rstd[:]).then_inc(s_bn, 1)
                        dve.wait_ge(s_bn, 8)
                        nc.vector.tensor_tensor(scale[:], rstd[:], gamma[:], ALU.mult).then_inc(s_bn, 1)
                        dve.wait_ge(s_bn, 9)
                        nc.vector.scalar_tensor_tensor(out=shift[:], in0=nmean[:], scalar=scale[:], in1=beta[:],
                                                       op0=ALU.mult, op1=ALU.add).then_inc(s_bn, 1)

                    @block.tensor
                    def _(pe):
                        pe.wait_ge(s_w, 208)

                        def one(c, it, par):
                            wait_reuse(pe, s_d, at(D, "sum", c))
                            wait_reuse(pe, s_a, c * len(A))
                            turn_nodes(pA, hs).then_inc(s_p, 1)
                            wait_reuse(pe, s_a, at(A, "hT", c))
                            for i in range(NPR):
                                mm = nc.tensor.matmul(pB[:, i, 0:NP], w1[:], hT[:, i, :], start=True, stop=True)
                            mm.then_inc(s_p, 1)
                            wait_reuse(pe, s_a, at(A, "a1", c))
                            for i in range(NPR):
                                mm = nc.tensor.matmul(pA[:, i, 0:NP], w2[:], a1[:, i, :], start=True, stop=True)
                            mm.then_inc(s_p, 1)
                        chunks(pe, one)
                        pe.wait_ge(s_a, NC * len(A))
                        pe.wait_ge(s_bn, 1)
                        nc.tensor.matmul(pA[:, 0, 0:1], halves[:], total[:], start=True, stop=True).then_inc(s_bn, 1)
                        pe.wait_ge(s_bn, 4)
                        nc.tensor.matmul(pA[:, 4, 0:1], halves[:], ssq[:], start=True, stop=True).then_inc(s_bn, 1)

                    @block.scalar
                    def _(act):
                        act.wait_ge(s_w, 208)
                        act.wait_ge(s_ix0, 1)

                        def one(c, it, par):
                            wait_reuse(act, s_p, at(PEQ, "turned", c))
                            nc.scalar.copy(hT[:], pA[:, 0:NPR, 0:NP]).then_inc(s_a, 1)
                            wait_reuse(act, s_p, at(PEQ, "lin1", c))
                            nc.scalar.activation(a1[:], pB[:, 0:NPR, 0:NP], ACT.Relu, bias=b1[:]).then_inc(s_a, 1)
                            wait_reuse(act, s_p, at(PEQ, "lin2", c))
                            nc.scalar.activation(G[:, bass.ds(c * NPR * NP, NPR * NP)].rearrange("p (i n) -> p i n", i=NPR),
                                                 pA[:, 0:NPR, 0:NP], ACT.Relu, bias=b2[:]).then_inc(s_a, 1)
                        chunks(act, one)
                        act.wait_ge(s_bn, 3)
                        nc.scalar.activation(dev[:], G[:], ACT.Square, bias=nmean[:], accum_out=ssq[:]).then_inc(s_bn, 1)
                        act.wait_ge(s_bn, 6)
                        nc.scalar.activation(rstd[:], var[:], ACT.Sqrt, bias=beps[:]).then_inc(s_bn, 1)

                gT = [sb(f"n0_gT{i}", [P, NPR, NP], F32, ctx) for i in range(2)]
                ln = Normed(ctx, "n0")
                own = [sb(f"n0_own{i}", [NP, CH, F], F32, ctx) for i in range(2)]
                tab = [sb(f"n0_tab{i}", [NP, CH, F], F32, ctx) for i in range(2)]
                fx = [sb(f"n0_fx{i}", [NP, CH], I32, ctx) for i in range(2)]
                s_d, s_a, begun, std, back, storing, turned_in, lin, tabbed = (ctx.sem(f"n0b_{n}") for n in (
                    "dve", "act", "scatters_begun", "roots", "back", "stores_begun", "turned", "lin", "tabbed"))
                normalised, owned, summed = ctx.pair("n0b_normed"), ctx.sem("n0b_owned"), ctx.sem("n0b_summed")
                stored, scattered = ctx.pair("n0b_stored"), dma_pair("n0b_scattered")
                DB = steps("x", *Normed.names)
                with nc.Block() as block:
                    @block.sync
                    def _(sp):
                        def one(c, it, par):
                            t_at = c * CH if isinstance(c, int) else sp.snap(c * CH)
                            sp.wait_ge(owned, c + 1)
                            sp.wait_ge(tabbed, c + 1)
                            sp.sem_inc(storing, 1)
                            sp.dma_start(node_view(own_d)[:, bass.ds(t_at, CH), :], own[par][:]).then_inc(stored[par], 16)
                            sp.dma_start(node_view(table1)[:, bass.ds(t_at, CH), :], tab[par][:]).then_inc(stored[par], 16)
                        chunks(sp, one)
                        sp.wait_ge(stored[0], 32 * (NC // 2))
                        sp.wait_ge(stored[1], 32 * (NC // 2))

                    @block.gpsimd
                    def _(pool):
                        top = pool.to_reg(E - 1)

                        def one(c, it, par):
                            pool.wait_ge(owned, c + 1)
                            pool.sem_inc(begun, 1)
                            for t in range(CH):
                                nc.gpsimd.indirect_dma_start(own_at_start, IND(ap=fx[par][:, t:t + 1], axis=0), own[par][:, t, :],
                                                             None, bounds_check=top, oob_is_err=False
                                                             ).then_inc(scattered[par], 16)
                        chunks(pool, one)
                        pool.wait_ge(scattered[0], 16 * CH * (NC // 2))
                        pool.wait_ge(scattered[1], 16 * CH * (NC // 2))

                    @block.vector
                    def _(dve):
                        def residual(c, it, par):
                            xs = X[:, bass.ds(c * CH, CH), :]
                            dve.wait_ge(back, c + 1)
                            nc.vector.tensor_tensor(xs, xs, pC[0:NP, 0:NPR, :].rearrange("p i (a f) -> p (i a) f", a=2), ALU.add
                                                    ).then_inc(s_d, 1)
                            wait_reuse(dve, s_d, at(DB, "x", c))
                            dve.sem_inc(summed, 1)
                            ln.vector(dve, xs, hs[:], s_d, DB, std, c, lambda: wait_reuse(dve, turned_in, c))

                        def own_part(it, par):
                            wait_reuse(dve, scattered[par], 16 * CH * it)
                            wait_reuse(dve, stored[par], 32 * it)
                            c = 2 * it + par
                            same_values(fx[par][:], chunk(first_at, c))
                            dve.wait_ge(lin, c + 1)
                            nc.vector.tensor_tensor(own[par][:], pA[0:NP, 0:NPR, :].rearrange("p i (a f) -> p (i a) f", a=2),
                                                    over_n(ownb[:]), ALU.add).then_inc(owned, 1)
                        staggered(dve, lambda it, par: residual(2 * it + par, it, par), own_part, NC // 2)

                    @block.tensor
                    def _(pe):
                        def turn_back_to_nodes(it, par):
                            c = 2 * it + par
                            pe.wait_ge(normalised[par], it + 1)
                            wait_reuse(pe, s_d, (c - 1) * len(DB) + DB["x"] if not isinstance(c, int) or c else 0)
                            for i in range(NPR):
                                mm = nc.tensor.transpose(pC[0:NP, i, :], gT[par][:, i, :], ident[:])
                            mm.then_inc(back, 1)

                        def parts(it, par):
                            c = 2 * it + par
                            wait_reuse(pe, s_d, at(DB, "h", c))
                            turn_nodes(pB, hs).then_inc(turned_in, 1)
                            pe.wait_ge(s_a, c + 1)
                            wait_reuse(pe, owned, c)
                            wait_reuse(pe, tabbed, c)
                            for i in range(NPR):
                                nc.tensor.matmul(pA[0:NP, i, :], a1[:, i, :], wa[:], start=True, stop=True)
                            for i in range(NPR):
                                mm = nc.tensor.matmul(pD[0:NP, i, :], a1[:, i, :], wb[:], start=True, stop=True)
                            mm.then_inc(lin, 1)
                        staggered(pe, turn_back_to_nodes, parts, NC // 2)

                    @block.scalar
                    def _(act):
                        def batch_norm(it, par):
                            wait_reuse(act, back, 2 * it + par - 1)
                            c = 2 * it + par
                            nc.scalar.activation(gT[par][:].rearrange("p i n -> p (i n)"), G[:, bass.ds(c * NPR * NP, NPR * NP)],
                                                 ACT.Identity, bias=shift[:], scale=scale[:]).then_inc(normalised[par], 1)

                        def rest(it, par):
                            c = 2 * it + par
                            ln.scalar(act, s_d, DB, std, c)
                            act.wait_ge(turned_in, c + 1)
                            wait_reuse(act, lin, c)
                            nc.scalar.copy(a1[:], pB[:, 0:NPR, 0:NP]).then_inc(s_a, 1)
                            act.wait_ge(lin, c + 1)
                            wait_reuse(act, stored[par], 32 * it)
                            nc.scalar.copy(tab[par][:], pD[0:NP, 0:NPR, :].rearrange("p i (a f) -> p (i a) f", a=2)
                                           ).then_inc(tabbed, 1)
                        staggered(act, batch_norm, rest, NC // 2)
                ctx.clear()

        def node12(layer):
            tag = f"n{layer}"
            with Stage() as ctx:
                ag = [sb(f"{tag}_ag{i}", [NP, CH, F], F32, ctx) for i in range(2)]
                ix = [sb(f"{tag}_ix{i}", [NP, CH], I32, ctx) for i in range(2)]
                carry = sb(f"{tag}_carry", [NP, F], F32, ctx)
                cr = sb(f"{tag}_cr", [NP, CH, F], F32, ctx)
                pen = sb(f"{tag}_pen", [NP, NT], F32, ctx)
                hs = sb(f"{tag}_hs", [NP, CH, F], F32, ctx)
                hT = sb(f"{tag}_hT", [P, NPR, NP], F32, ctx)
                tab = [sb(f"{tag}_tab{i}", [NP, CH, F], F32, ctx) for i in range(2)]
                wt = sb(f"{tag}_wt", [P, P], F32, ctx)
                br, b2r = (sb(f"{tag}_{n}", [NP, F], F32, ctx) for n in ("br", "b2r"))
                ln = Normed(ctx, tag)
                pA, pB = (ps(f"{tag}_p{n}", [P, 8, P], ctx) for n in "AB")
                s_w, s_wz, s_pen, s_d, s_p, s_a, begun, std, storing, biased, made = (ctx.sem(f"{tag}_{n}") for n in (
                    "weights", "weights_zeroed", "penalty", "dve", "pe", "act", "gathers_begun", "roots", "stores_begun",
                    "biased", "table_made"))
                got = dma_pair(f"{tag}_got")
                ix_ready, used, stored = (ctx.pair(f"{tag}_{n}") for n in ("ix_ready", "used", "stored"))
                if layer == 1:
                    D = steps("carry", "less", "max", "bias", "masked", "x", *Normed.names)
                else:
                    D = steps("carry", "sum", "scaled", "x", *Normed.names)
                PEQ = steps("turned", "lin")
                A = steps("hT")
                with nc.Block() as block:
                    @block.sync
                    def _(sp):
                        sp.dma_start(carry[:], stream[BASE - 1, :].partition_broadcast(NP)).then_inc(s_w, 16)
                        sp.dma_start(br[:], w["L2_gnn_b"].partition_broadcast(NP)).then_inc(s_w, 16)
                        sp.dma_start(b2r[:], w["L1_gnn_b2"].partition_broadcast(NP)).then_inc(s_w, 16)
                        sp.wait_ge(s_wz, 1)
                        blocks_of(sp, wt, w["L2_gnn_W"], s_w)

                        def one(c, it, par):
                            t_at = c * CH if isinstance(c, int) else sp.snap(c * CH)
                            sp.wait_ge(made, c + 1)
                            sp.sem_inc(storing, 1)
                            sp.dma_start(node_view(table2 if layer == 1 else table3)[:, bass.ds(t_at, CH), :], tab[par][:]
                                         ).then_inc(stored[par], 16)
                        chunks(sp, one)
                        sp.wait_ge(stored[0], 16 * (NC // 2))
                        sp.wait_ge(stored[1], 16 * (NC // 2))

                    @block.gpsimd
                    def _(pool):
                        fetch(pool, ag, ix, stream, got, ix_ready, used, begun, pool.to_reg(2 * H - 1))

                    @block.vector
                    def _(dve):
                        nc.vector.memset(wt[:], 0.0).then_inc(s_wz, 1)
                        nc.vector.tensor_scalar(pen[:], cut[:], -1.0, BIG, ALU.add, ALU.mult).then_inc(s_pen, 1)
                        nc.vector.tensor_copy(ix[0][:], row_at[:, 0:CH]).then_inc(ix_ready[0], 1)
                        dve.wait_ge(s_w, 80)
                        dve.wait_ge(s_pen, 1)

                        def normed(it, par):
                            c = 2 * it + par
                            next_index(dve, c, it, par, ix, got, ix_ready)
                            dve.wait_ge(got[par], 16 * CH * (it + 1))

                            def step(name, i):
                                i.then_inc(s_d, 1)
                                wait_reuse(dve, s_d, at(D, name, c))
                            step("carry", nc.vector.tensor_tensor(cr[:], over_n(carry[:]), over_f(chunk(cut, c)), ALU.mult))
                            if layer == 1:
                                step("less", nc.vector.tensor_tensor(cr[:], cr[:], over_f(chunk(pen, c)), ALU.add))
                                step("max", nc.vector.tensor_tensor(cr[:], cr[:], ag[par][:], ALU.max))
                                step("bias", nc.vector.tensor_tensor(cr[:], cr[:], over_n(b2r[:]), ALU.add))
                                step("masked", nc.vector.tensor_tensor(cr[:], cr[:], over_f(chunk(has, c)), ALU.mult))
                            else:
                                step("sum", nc.vector.tensor_tensor(cr[:], cr[:], ag[par][:], ALU.add))
                                step("scaled", nc.vector.tensor_tensor(cr[:], cr[:], over_f(chunk(in_scale, c)), ALU.mult))
                            xs = X[:, bass.ds(c * CH, CH), :]
                            step("x", nc.vector.tensor_tensor(xs, xs, cr[:], ALU.add))
                            dve.sem_inc(used[par], 1)
                            free_rows = lambda: wait_reuse(dve, s_p, (c - 1) * len(PEQ) + PEQ["turned"]) if layer == 1 else None
                            ln.vector(dve, xs, hs[:], s_d, D, std, c, free_rows)

                        def table(it, par):
                            c = 2 * it + par
                            wait_reuse(dve, stored[par], 16 * it)
                            if layer == 1:
                                wait_reuse(dve, s_p, at(PEQ, "lin", c))
                                nc.vector.tensor_tensor(tab[par][:], pB[0:NP, 0:NPR, :].rearrange("p i (a f) -> p (i a) f", a=2),
                                                        over_n(br[:]), ALU.add).then_inc(biased, 1)
                                dve.wait_ge(biased, c + 1)
                                nc.vector.tensor_tensor(tab[par][:], tab[par][:], over_f(chunk(out_scale, c)), ALU.mult
                                                        ).then_inc(made, 1)
                            else:
                                wait_reuse(dve, s_d, at(D, "h", c))
                                same_values(HN[:, bass.ds(c * CH, CH), :], hs[:])
                                nc.vector.tensor_copy(tab[par][:], hs[:]).then_inc(made, 1)
                        if layer == 1:
                            staggered(dve, normed, table, NC // 2)
                        else:
                            chunks(dve, lambda c, it, par: (normed(it, par), table(it, par)))

                    @block.scalar
                    def _(act):
                        def one(c, it, par):
                            ln.scalar(act, s_d, D, std, c)
                            if layer == 1:
                                wait_reuse(act, s_p, at(PEQ, "turned", c))
                                nc.scalar.copy(hT[:], pA[:, 0:NPR, 0:NP]).then_inc(s_a, 1)
                        chunks(act, one)

                    if layer == 1:
                        @block.tensor
                        def _(pe):
                            pe.wait_ge(s_w, 80)

                            def one(c, it, par):
                                wait_reuse(pe, s_d, at(D, "h", c))
                                wait_reuse(pe, s_a, c * len(A))
                                turn_nodes(pA, hs).then_inc(s_p, 1)
                                wait_reuse(pe, s_a, at(A, "hT", c))
                                wait_reuse(pe, biased, c)
                                for i in range(NPR):
                                    mm = nc.tensor.matmul(pB[0:NP, i, :], hT[:, i, :], wt[:], start=True, stop=True)
                                mm.then_inc(s_p, 1)
                            chunks(pe, one)
                ctx.clear()

        def node3():
            with Stage() as ctx:
                G = sb("n3_G", [P, NC * CH * NP], F32, ctx)
                ag = [sb(f"n3_ag{i}", [NP, CH, 2 * F], F32, ctx) for i in range(2)]
                ix = [sb(f"n3_ix{i}", [NP, CH], I32, ctx) for i in range(2)]
                part0, part1 = (sb(f"n3_{n}", [1, 2 * F], F32, ctx) for n in ("part0", "part1"))
                top0, top1, top01 = (sb(f"n3_{n}", [1, F], F32, ctx) for n in ("top0", "top1", "top01"))
                mx = sb("n3_mx", [NP, CH, F], F32, ctx)
                msg = [sb(f"n3_msg{i}", [NP, CH, F], F32, ctx) for i in range(2)]
                sq = [sb(f"n3_sq{i}", [NP, 2, CH, F], F32, ctx) for i in range(2)]
                norms = sb("n3_norms", [NP, 2, CH], F32, ctx)
                y = sb("n3_y", [NP, CH, F], F32, ctx)
                hT = sb("n3_hT", [P, NPR, NP], F32, ctx)
                w1 = sb("n3_w1", [P, 2, P], F32, ctx)
                w2 = sb("n3_w2", [P, F], F32, ctx)
                b1, gamma, beta, nmean, rstd, scale, shift, beps = (sb(f"n3_{n}", [P, 1], F32, ctx) for n in (
                    "b1", "gamma", "beta", "nmean", "rstd", "scale", "shift", "beps"))
                stats = sb("n3_stats", [P, NC * PIECES, 6], F32, ctx)
                mv = sb("n3_mv", [P, 2], F32, ctx)
                b2r = sb("n3_b2r", [NP, F], F32, ctx)
                lscale = sb("n3_lscale", [NP, 1], F32, ctx)
                act2 = [sb(f"n3_act2{i}", [P, CH, NP], F32, ctx) for i in range(2)]
                ot = [sb(f"n3_ot{i}", [NP, CH, F], F32, ctx) for i in range(2)]
                pA = ps("n3_pA", [P, 8, P], ctx)
                pB = ps("n3_pB", [P, 12, P], ctx)
                pO = [ps("n3_pO", [P, 16, F], ctx), pA.rearrange("p i (a f) -> p (i a) f", a=2)]
                s_w, s_wz, s_set, s_parts, s_mended, s_patch, s_h, s_d, s_sq, s_root, s_p, s_a, begun, s_bn, s_std, s_d2, storing = (
                    ctx.sem(f"n3_{n}") for n in (
                        "weights", "weights_zeroed", "set", "parts_in", "mended", "patched", "messages", "dve", "squares",
                        "roots", "pe", "act", "gathers_begun", "bn", "bn_root", "dve2", "stores_begun"))
                got = dma_pair(f"n3_got")
                ix_ready, used, activated, projected, added, stored = (ctx.pair(f"n3_{n}") for n in (
                    "ix_ready", "used", "activated", "projected", "added", "stored"))
                DH = steps("rden", "h", "h_masked")
                D = steps("sums", "hmax", "hrec", "coef", "scaled", "y")
                SQ = steps("input", "message")
                PEQ = steps("turned", "lin1")
                A = steps("hT", "g")
                with nc.Block() as block:
                    @block.sync
                    def _(sp):
                        sp.dma_start(part0[:], stream3[BASE - 1:BASE, :]).then_inc(s_parts, 16)
                        sp.dma_start(top0[:], maxes[0:F, BASE - 1:BASE].rearrange("f o -> o f"), allow_slow_non_contiguous=True
                                     ).then_inc(s_parts, 16)
                        edge = sp.value_load(cut_last[0:1, 0:1], min_val=0, max_val=H - 1)
                        sp.dma_start(part1[:], stream3[bass.ds(edge + H, 1), :]).then_inc(s_parts, 16)
                        sp.dma_start(top1[:], maxes[F:P, bass.ds(edge, 1)].rearrange("f o -> o f"),
                                     allow_slow_non_contiguous=True).then_inc(s_parts, 16)
                        row = sp.snap(edge + H)
                        sp.wait_ge(s_wz, 1)
                        for k in range(2):
                            sp.dma_start(w1[k * F:(k + 1) * F, k, :], w["L3_gnn_W1"]).then_inc(s_w, 16)
                        sp.dma_start(w2[:], w["L3_gnn_W2"]).then_inc(s_w, 16)
                        for col, v in ((b1, "L3_gnn_b1"), (gamma, "L3_gnn_gamma"), (beta, "L3_gnn_bn_beta")):
                            sp.dma_start(col[:], w[v].rearrange("(f o) -> f o", o=1)).then_inc(s_w, 16)
                        sp.dma_start(b2r[:], w["L3_gnn_b2"].partition_broadcast(NP)).then_inc(s_w, 16)
                        sp.dma_start(lscale[:], w["L3_gnn_scale"].partition_broadcast(NP)).then_inc(s_w, 16)
                        sp.wait_ge(s_mended, 8)
                        sp.dma_start(stream3[bass.ds(row, 1), :], part1[:]).then_inc(s_patch, 16)

                        def one(c, it, par):
                            t_at = c * CH if isinstance(c, int) else sp.snap(c * CH)
                            sp.wait_ge(added[par], it + 1)
                            sp.sem_inc(storing, 1)
                            sp.dma_start(node_view(out)[:, bass.ds(t_at, CH), :], ot[par][:]).then_inc(stored[par], 16)
                        chunks(sp, one)
                        sp.wait_ge(stored[0], 16 * (NC // 2))
                        sp.wait_ge(stored[1], 16 * (NC // 2))

                    @block.gpsimd
                    def _(pool):
                        pool.wait_ge(s_patch, 16)
                        fetch(pool, ag, ix, stream3, got, ix_ready, used, begun, pool.to_reg(2 * H - 1))

                    @block.vector
                    def _(dve):
                        tt = nc.vector.tensor_tensor
                        nc.vector.memset(w1[:], 0.0).then_inc(s_wz, 1)
                        nc.vector.memset(beps[:], BN_EPS).then_inc(s_set, 1)
                        nc.vector.tensor_copy(ix[0][:], row_at[:, 0:CH]).then_inc(ix_ready[0], 1)
                        dve.wait_ge(s_parts, 64)
                        tt(top01[:], top0[:], top1[:], ALU.max).then_inc(s_mended, 1)
                        dve.wait_ge(s_mended, 1)
                        tt(top0[:], top0[:], top01[:], ALU.subtract).then_inc(s_mended, 1)
                        tt(top1[:], top1[:], top01[:], ALU.subtract).then_inc(s_mended, 1)
                        dve.wait_ge(s_mended, 5)
                        for k in range(2):
                            cols = slice(k * F, (k + 1) * F)
                            tt(part0[:, cols], part0[:, cols], top0[:], ALU.mult)
                            tt(part1[:, cols], part1[:, cols], top1[:], ALU.mult).then_inc(s_mended, 1)
                        dve.wait_ge(s_mended, 7)
                        tt(part1[:], part1[:], part0[:], ALU.add).then_inc(s_mended, 1)
                        dve.wait_ge(s_w, 128)

                        def messages(it, par):
                            c = 2 * it + par
                            next_index(dve, c, it, par, ix, got, ix_ready)
                            dve.wait_ge(got[par], 16 * CH * (it + 1))
                            num, den = (ag[par][:, :, k * F:(k + 1) * F] for k in range(2))
                            nc.vector.reciprocal(mx[:], den).then_inc(s_h, 1)
                            wait_reuse(dve, s_h, at(DH, "rden", c))
                            wait_reuse(dve, s_sq, (c - 1) * len(SQ))
                            tt(msg[par][:], num, mx[:], ALU.mult).then_inc(s_h, 1)
                            wait_reuse(dve, s_h, at(DH, "h", c))
                            dve.sem_inc(used[par], 1)
                            nc.vector.scalar_tensor_tensor(out=msg[par][:], in0=msg[par][:], scalar=SM_EPS,
                                                           in1=over_f(chunk(has, c)), op0=ALU.add, op1=ALU.mult
                                                           ).then_inc(s_h, 1)

                        def statistics(c):
                            dve.wait_ge(s_a, at(A, "g", c))
                            for k in range(PIECES):
                                i = nc.vector.bn_stats(stats[:, bass.ds(c * PIECES + k, 1), :].rearrange("p o s -> p (o s)"),
                                                       G[:, bass.ds(c * CH * NP + k * PIECE, PIECE)])
                            i.then_inc(s_bn, 1)

                        def combine(it, par):
                            c = 2 * it + par

                            def step(name, i):
                                i.then_inc(s_d, 1)
                                wait_reuse(dve, s_d, at(D, name, c))
                            if not (isinstance(c, int) and c < 2):
                                statistics(c - 2)
                            dve.wait_ge(s_sq, at(SQ, "message", c))
                            step("sums", nc.vector.tensor_reduce(norms[:], sq[par][:], AX, ALU.add))
                            dve.wait_ge(s_root, c + 1)
                            step("hmax", nc.vector.tensor_scalar(norms[:, 0, :], norms[:, 0, :], NORM_EPS, None, ALU.max))
                            step("hrec", nc.vector.reciprocal(norms[:, 0, :], norms[:, 0, :]))
                            step("coef", nc.vector.scalar_tensor_tensor(out=norms[:, 0, :], in0=norms[:, 0, :], scalar=lscale[:],
                                                                        in1=norms[:, 1, :], op0=ALU.mult, op1=ALU.mult))
                            step("scaled", tt(msg[par][:], msg[par][:], over_f(norms[:, 0, :]), ALU.mult))
                            wait_reuse(dve, s_p, c * len(PEQ))
                            tt(y[:], msg[par][:], HN[:, bass.ds(c * CH, CH), :], ALU.add).then_inc(s_d, 1)
                        staggered(dve, messages, combine, NC // 2)

                        statistics(NC - 2)
                        statistics(NC - 1)
                        dve.wait_ge(s_bn, NC)
                        nc.vector.bn_aggr(mv[:], stats[:]).then_inc(s_bn, 1)
                        dve.wait_ge(s_bn, NC + 1)
                        nc.vector.tensor_scalar(nmean[:], mv[:, 0:1], -1.0, None, ALU.mult).then_inc(s_bn, 1)
                        dve.wait_ge(s_std, 1)
                        nc.vector.reciprocal(rstd[:], rstd[:]).then_inc(s_bn, 1)
                        dve.wait_ge(s_bn, NC + 3)
                        nc.vector.tensor_tensor(scale[:], rstd[:], gamma[:], ALU.mult).then_inc(s_bn, 1)
                        dve.wait_ge(s_bn, NC + 4)
                        nc.vector.scalar_tensor_tensor(out=shift[:], in0=nmean[:], scalar=scale[:], in1=beta[:],
                                                       op0=ALU.mult, op1=ALU.add).then_inc(s_bn, 1)

                        def last(c, it, par):
                            dve.wait_ge(projected[par], it + 1)
                            wait_reuse(dve, stored[par], 16 * it)
                            tt(ot[par][:], pO[par][0:NP, 0:CH, :], over_n(b2r[:]), ALU.add).then_inc(s_d2, 1)
                            dve.wait_ge(s_d2, c + 1)
                            tt(ot[par][:], ot[par][:], X[:, bass.ds(c * CH, CH), :], ALU.add).then_inc(added[par], 1)
                        chunks(dve, last)

                    @block.scalar
                    def _(act):
                        act.wait_ge(s_mended, 3)
                        nc.scalar.activation(top0[:], top0[:], ACT.Exp).then_inc(s_mended, 1)
                        nc.scalar.activation(top1[:], top1[:], ACT.Exp).then_inc(s_mended, 1)
                        act.wait_ge(s_w, 128)
                        act.wait_ge(s_set, 1)

                        def squares(it, par):
                            c = 2 * it + par
                            wait_reuse(act, s_d, (c - 1) * len(D))
                            nc.scalar.activation(sq[par][:, 1, :, :], HN[:, bass.ds(c * CH, CH), :], ACT.Square).then_inc(s_sq, 1)
                            wait_reuse(act, s_h, at(DH, "h_masked", c))
                            nc.scalar.activation(sq[par][:, 0, :, :], msg[par][:], ACT.Square).then_inc(s_sq, 1)

                        def hidden(it, par):
                            c = 2 * it + par
                            wait_reuse(act, s_d, at(D, "sums", c))
                            nc.scalar.activation(norms[:], norms[:], ACT.Sqrt).then_inc(s_root, 1)
                            wait_reuse(act, s_p, at(PEQ, "turned", c))
                            nc.scalar.copy(hT[:], pA[:, 0:NPR, 0:NP]).then_inc(s_a, 1)
                            wait_reuse(act, s_p, at(PEQ, "lin1", c))
                            nc.scalar.activation(G[:, bass.ds(c * CH * NP, CH * NP)].rearrange("p (i n) -> p i n", i=CH),
                                                 pB[:, 0:CH, 0:NP], ACT.Identity, bias=b1[:]).then_inc(s_a, 1)
                        staggered(act, squares, hidden, NC // 2)
                        act.wait_ge(s_bn, NC + 1)
                        nc.scalar.activation(rstd[:], mv[:, 1:2], ACT.Sqrt, bias=beps[:]).then_inc(s_std, 1)
                        act.wait_ge(s_bn, NC + 5)

                        def last(c, it, par):
                            wait_reuse(act, projected[par], it)
                            nc.scalar.activation(act2[par][:].rearrange("p i n -> p (i n)"), G[:, bass.ds(c * CH * NP, CH * NP)],
                                                 ACT.Relu, bias=shift[:], scale=scale[:]).then_inc(activated[par], 1)
                        chunks(act, last)

                    @block.tensor
                    def _(pe):
                        pe.wait_ge(s_w, 128)

                        def one(c, it, par):
                            wait_reuse(pe, s_d, at(D, "y", c))
                            wait_reuse(pe, s_a, c * len(A))
                            turn_nodes(pA, y).then_inc(s_p, 1)
                            wait_reuse(pe, s_a, at(A, "hT", c))
                            for t in range(CH):
                                mm = nc.tensor.matmul(pB[:, t, 0:NP], w1[:, t % 2, :], hT[:, t // 2, :], start=True, stop=True)
                            mm.then_inc(s_p, 1)
                        chunks(pe, one)

                        def last(c, it, par):
                            pe.wait_ge(activated[par], it + 1)
                            wait_reuse(pe, added[par], it)
                            for t in range(CH):
                                mm = nc.tensor.matmul(pO[par][0:NP, t, :], act2[par][:, t, :], w2[:], start=True, stop=True)
                            mm.then_inc(projected[par], 1)
                        chunks(pe, last)
                ctx.clear()

        edge0()
        runs()
        node0()
        edge1()
        node12(1)
        edge2()
        node12(2)
        edge3()
        node3()


WEIGHTS = ["L0_gnn_W_edge", "L0_gnn_b_edge", "L0_gnn_W1", "L0_gnn_b1", "L0_gnn_W2", "L0_gnn_b2", "L0_gnn_bn_gamma",
           "L0_gnn_bn_beta", "L1_gnn_W1", "L1_gnn_b1", "L1_gnn_W2", "L1_gnn_b2", "L2_gnn_W", "L2_gnn_b", "L3_gnn_W1",
           "L3_gnn_b1", "L3_gnn_gamma", "L3_gnn_bn_beta", "L3_gnn_W2", "L3_gnn_b2", "L3_gnn_scale"]


def layout(inputs):
    import numpy as np
    a = {"in_" + k: np.ascontiguousarray(v) for k, v in inputs.items()}
    a["in_L2_gnn_W"] = np.ascontiguousarray(a["in_L2_gnn_W"].T)
    return a


def program(nc, a):
    gnn_kernel(nc, a["in_x"], a["in_src"], a["in_dst"], a["in_edge_attr_10"], a["in_edge_attr_64"],
               {k: a["in_" + k] for k in WEIGHTS}, a["out"])


def kernel(**inputs):
    import concourse.bacc as bacc
    from concourse.bass_utils import run_bass_kernel_spmd

    nc = bacc.Bacc("TRN2", target_bir_lowering=False, num_devices=1)
    arrays = layout(inputs)
    aps = {k: nc.dram_tensor(k, v.shape, mybir.dt.from_np(v.dtype), kind="ExternalInput").ap() for k, v in arrays.items()}
    aps["out"] = nc.dram_tensor("out", arrays["in_x"].shape, F32, kind="ExternalOutput").ap()
    program(nc, aps)
    r = run_bass_kernel_spmd(nc, [arrays], core_ids=[0])
    return r.results[0]["out"]
```
